# Optimizing a Trainium2 kernel written in Bass

```python
import numpy as np
import jax
import jax.numpy as jnp

def _softmax(x, axis=-1):
    return jax.nn.softmax(x, axis=axis)

def _gelu(x):
    return jax.nn.gelu(x, approximate=True)

def _silu(x):
    return jax.nn.silu(x)

def _sigmoid(x):
    return jax.nn.sigmoid(x)

def _layernorm(x, axis=-1, eps=1e-05):
    m = jnp.mean(x, axis=axis, keepdims=True)
    v = jnp.var(x, axis=axis, keepdims=True)
    return (x - m) / jnp.sqrt(v + eps)

def _scatter_add(tgt, idx, src, axis=0):
    return tgt.at[idx].add(src)

def _segment_sum(src, seg, n):
    return jax.ops.segment_sum(src, seg, n)
kernel_name = 'mk_decoder_postln_d2_seqx_r8_c77fea'

def setup_inputs(seed: int=0):
    np.random.seed(seed)
    _w = jnp.asarray

    def _rec_inputs():
        import jax
        import jax.numpy as jnp
        _rk = jax.random.key(seed)
        x = 7.22e-05 + 1 * jax.random.normal(jax.random.fold_in(_rk, 1), (16, 256, 128), jnp.float32)
        _lenS = 256 - jax.random.randint(jax.random.fold_in(_rk, 7), (16,), 0, max(1, 256 // 4) + 1, jnp.int32)
        _lenS2 = 64 - jax.random.randint(jax.random.fold_in(_rk, 8), (16,), 0, max(1, 64 // 4) + 1, jnp.int32)
        _ctx_768P = jax.random.normal(jax.random.fold_in(_rk, 11), (16, 16, 96), jnp.float32)
        _ctx_768c = jax.random.dirichlet(jax.random.fold_in(_rk, 511), 0.3 * jnp.ones((16,), jnp.float32), (16, 64))
        _ctx_768t = jnp.einsum('bsk,bkd->bsd', _ctx_768c, _ctx_768P)
        _ctx_768t = _ctx_768t * jax.lax.rsqrt(jnp.mean(jnp.square(_ctx_768t)) + 1e-12) * 0.953939
        ctx_768 = -0.00055796 + 0.999787 * (_ctx_768t + 0.3 * jax.random.normal(jax.random.fold_in(_rk, 611), (16, 64, 96), jnp.float32))
        return (x, ctx_768)
    x, ctx_768 = _rec_inputs()

    def _L0_attn_setup():
        import jax, jax.numpy as jnp
        import numpy as np
        B, T, D, H = (2, 256, 128, 16)
        key = jax.random.key(seed)
        k0, k1, k2, k3 = jax.random.split(key, 4)
        s = 0.02
        return {'x': jax.random.normal(k0, (B, T, D), dtype=jnp.float32), 'Wqkv': jax.random.normal(k1, (3 * D, D), dtype=jnp.float32) * s, 'Wout': jax.random.normal(k2, (D, D), dtype=jnp.float32) * s, 'bout': jax.random.normal(k3, (D,), dtype=jnp.float32) * s}
    _L0_attn_all = _L0_attn_setup()
    _L0_attn_in = {k: v for k, v in _L0_attn_all.items() if k in ('Wqkv', 'Wout', 'bout')}
    del _L0_attn_all

    def _L0_xattn_setup():
        import jax, jax.numpy as jnp
        import numpy as np
        H = 8
        key = jax.random.key(seed)
        ks = jax.random.split(key, 7)
        B, Lq, Lkv = (4, 256, 64)
        dim_q, dim_kv = (128, 96)
        q = jax.random.normal(ks[0], (B, Lq, dim_q), dtype=jnp.float32)
        kv = jax.random.normal(ks[1], (B, Lkv, dim_kv), dtype=jnp.float32)
        Wq = jax.random.normal(ks[2], (dim_q, dim_q), dtype=jnp.float32) / np.sqrt(dim_q)
        Wk = jax.random.normal(ks[3], (dim_kv, dim_q), dtype=jnp.float32) / np.sqrt(dim_kv)
        Wv = jax.random.normal(ks[4], (dim_kv, dim_q), dtype=jnp.float32) / np.sqrt(dim_kv)
        Wo = jax.random.normal(ks[5], (dim_q, dim_q), dtype=jnp.float32) / np.sqrt(dim_q)
        bo = jax.random.normal(ks[6], (dim_q,), dtype=jnp.float32) * 0.01
        return {'q': q, 'kv': kv, 'Wq': Wq, 'Wk': Wk, 'Wv': Wv, 'Wo': Wo, 'bo': bo}
    _L0_xattn_all = _L0_xattn_setup()
    _L0_xattn_in = {k: v for k, v in _L0_xattn_all.items() if k in ('Wq', 'Wk', 'Wv', 'Wo', 'bo')}
    del _L0_xattn_all

    def _L0_ffn_setup():
        import jax, jax.numpy as jnp
        import numpy as np
        E = 64
        K = 6
        CAP = 64
        ROUTE_SCALE = 1.0
        key = jax.random.key(seed)
        ks = jax.random.split(key, 9)
        B, S, D, I = (2, 128, 128, 88)
        SI = 2 * I
        s = 0.02
        return {'x': jax.random.normal(ks[0], (B, S, D), jnp.float32), 'gate_w': jax.random.normal(ks[1], (E, D), jnp.float32) * s, 'gate_b': jnp.zeros((E,), jnp.float32), 'w1': jax.random.normal(ks[2], (E, I, D), jnp.float32) * s, 'w2': jax.random.normal(ks[3], (E, D, I), jnp.float32) * s, 'w3': jax.random.normal(ks[4], (E, I, D), jnp.float32) * s, 'ws1': jax.random.normal(ks[5], (SI, D), jnp.float32) * s, 'ws2': jax.random.normal(ks[6], (D, SI), jnp.float32) * s, 'ws3': jax.random.normal(ks[7], (SI, D), jnp.float32) * s}
    _L0_ffn_all = _L0_ffn_setup()
    _L0_ffn_in = {k: v for k, v in _L0_ffn_all.items() if k in ('gate_w', 'gate_b', 'w1', 'w2', 'w3', 'ws1', 'ws2', 'ws3')}
    del _L0_ffn_all

    def _L1_attn_setup():
        import jax, jax.numpy as jnp
        import numpy as np
        HIDDEN = 128
        NUM_HEADS = 16
        HEAD_SIZE = 64
        key = jax.random.key(seed)
        ks = jax.random.split(key, 5)
        B, S = (2, 256)
        scale = 1.0 / np.sqrt(HIDDEN)
        x = jax.random.normal(ks[0], (B, S, HIDDEN), dtype=jnp.float32)
        W_qkv = jax.random.normal(ks[1], (HIDDEN, 3 * NUM_HEADS * HEAD_SIZE), dtype=jnp.float32) * scale
        b_qkv = jnp.zeros((3 * NUM_HEADS * HEAD_SIZE,), dtype=jnp.float32)
        W_out = jax.random.normal(ks[2], (NUM_HEADS * HEAD_SIZE, HIDDEN), dtype=jnp.float32) * scale
        b_out = jnp.zeros((HIDDEN,), dtype=jnp.float32)
        return {'x': x, 'W_qkv': W_qkv, 'b_qkv': b_qkv, 'W_out': W_out, 'b_out': b_out}
    _L1_attn_all = _L1_attn_setup()
    _L1_attn_in = {k: v for k, v in _L1_attn_all.items() if k in ('W_qkv', 'b_qkv', 'W_out', 'b_out')}
    del _L1_attn_all

    def _L1_xattn_setup():
        import jax, jax.numpy as jnp
        import numpy as np
        HEADS = 16
        DIM_HEAD = 64
        key = jax.random.key(seed)
        ks = jax.random.split(key, 7)
        b, n, m = (2, 256, 128)
        query_dim, context_dim = (128, 96)
        inner = HEADS * DIM_HEAD
        s_q = 1.0 / np.sqrt(query_dim)
        s_c = 1.0 / np.sqrt(context_dim)
        s_i = 1.0 / np.sqrt(inner)
        return {'x': jax.random.normal(ks[0], (b, n, query_dim), jnp.float32), 'context': jax.random.normal(ks[1], (b, m, context_dim), jnp.float32), 'Wq': jax.random.normal(ks[2], (query_dim, inner), jnp.float32) * s_q, 'Wk': jax.random.normal(ks[3], (context_dim, inner), jnp.float32) * s_c, 'Wv': jax.random.normal(ks[4], (context_dim, inner), jnp.float32) * s_c, 'Wo': jax.random.normal(ks[5], (inner, query_dim), jnp.float32) * s_i, 'bo': jax.random.normal(ks[6], (query_dim,), jnp.float32) * 0.01}
    _L1_xattn_all = _L1_xattn_setup()
    _L1_xattn_in = {k: v for k, v in _L1_xattn_all.items() if k in ('Wq', 'Wk', 'Wv', 'Wo', 'bo')}
    del _L1_xattn_all

    def _L1_ffn_setup():
        import jax, jax.numpy as jnp
        import numpy as np
        B, T, D, E, H = (4, 256, 128, 4, 8)
        EPS = 1e-05

        def _uniform(k, shape, bound):
            return jax.random.uniform(k, shape, jnp.float32, -bound, bound)

        def _layernorm(x, w, b):
            mu = jnp.mean(x, axis=-1, keepdims=True)
            var = jnp.mean(jnp.square(x - mu), axis=-1, keepdims=True)
            return (x - mu) * jax.lax.rsqrt(var + EPS) * w + b
        key = jax.random.key(seed)
        ks = jax.random.split(key, 12)
        wb = np.sqrt(6.0 / D) / np.sqrt(6.0)
        wb = 1.0 / np.sqrt(D)
        return {'x': jax.random.normal(ks[0], (B, T, D), jnp.float32), 'router_prob': jax.random.uniform(ks[1], (B, T, E), jnp.float32), 'norm_w': jnp.ones((D,), jnp.float32), 'norm_b': jnp.zeros((D,), jnp.float32), 'q_w': _uniform(ks[2], (D, D), wb), 'q_b': _uniform(ks[3], (D,), wb), 'k_w': _uniform(ks[4], (D, D), wb), 'k_b': _uniform(ks[5], (D,), wb), 'v_w': _uniform(ks[6], (D, D), wb), 'v_b': _uniform(ks[7], (D,), wb), 'o_w': _uniform(ks[8], (D, D), wb), 'o_b': _uniform(ks[9], (D,), wb)}
    _L1_ffn_all = _L1_ffn_setup()
    _L1_ffn_in = {k: v for k, v in _L1_ffn_all.items() if k in ('router_prob', 'norm_w', 'norm_b', 'q_w', 'q_b', 'k_w', 'k_b', 'v_w', 'v_b', 'o_w', 'o_b')}
    del _L1_ffn_all
    return {'x': x, 'ctx_768': ctx_768, 'L0_attn_Wqkv': _L0_attn_in['Wqkv'], 'L0_attn_Wout': _L0_attn_in['Wout'], 'L0_attn_bout': _L0_attn_in['bout'], 'L0_xattn_Wq': _L0_xattn_in['Wq'], 'L0_xattn_Wk': _L0_xattn_in['Wk'], 'L0_xattn_Wv': _L0_xattn_in['Wv'], 'L0_xattn_Wo': _L0_xattn_in['Wo'], 'L0_xattn_bo': _L0_xattn_in['bo'], 'L0_ffn_gate_w': _L0_ffn_in['gate_w'], 'L0_ffn_gate_b': _L0_ffn_in['gate_b'], 'L0_ffn_w1': _L0_ffn_in['w1'], 'L0_ffn_w2': _L0_ffn_in['w2'], 'L0_ffn_w3': _L0_ffn_in['w3'], 'L0_ffn_ws1': _L0_ffn_in['ws1'], 'L0_ffn_ws2': _L0_ffn_in['ws2'], 'L0_ffn_ws3': _L0_ffn_in['ws3'], 'L1_attn_W_qkv': _L1_attn_in['W_qkv'], 'L1_attn_b_qkv': _L1_attn_in['b_qkv'], 'L1_attn_W_out': _L1_attn_in['W_out'], 'L1_attn_b_out': _L1_attn_in['b_out'], 'L1_xattn_Wq': _L1_xattn_in['Wq'], 'L1_xattn_Wk': _L1_xattn_in['Wk'], 'L1_xattn_Wv': _L1_xattn_in['Wv'], 'L1_xattn_Wo': _L1_xattn_in['Wo'], 'L1_xattn_bo': _L1_xattn_in['bo'], 'L1_ffn_router_prob': _L1_ffn_in['router_prob'], 'L1_ffn_norm_w': _L1_ffn_in['norm_w'], 'L1_ffn_norm_b': _L1_ffn_in['norm_b'], 'L1_ffn_q_w': _L1_ffn_in['q_w'], 'L1_ffn_q_b': _L1_ffn_in['q_b'], 'L1_ffn_k_w': _L1_ffn_in['k_w'], 'L1_ffn_k_b': _L1_ffn_in['k_b'], 'L1_ffn_v_w': _L1_ffn_in['v_w'], 'L1_ffn_v_b': _L1_ffn_in['v_b'], 'L1_ffn_o_w': _L1_ffn_in['o_w'], 'L1_ffn_o_b': _L1_ffn_in['o_b']}

def reference(x, ctx_768, L0_attn_Wqkv, L0_attn_Wout, L0_attn_bout, L0_xattn_Wq, L0_xattn_Wk, L0_xattn_Wv, L0_xattn_Wo, L0_xattn_bo, L0_ffn_gate_w, L0_ffn_gate_b, L0_ffn_w1, L0_ffn_w2, L0_ffn_w3, L0_ffn_ws1, L0_ffn_ws2, L0_ffn_ws3, L1_attn_W_qkv, L1_attn_b_qkv, L1_attn_W_out, L1_attn_b_out, L1_xattn_Wq, L1_xattn_Wk, L1_xattn_Wv, L1_xattn_Wo, L1_xattn_bo, L1_ffn_router_prob, L1_ffn_norm_w, L1_ffn_norm_b, L1_ffn_q_w, L1_ffn_q_b, L1_ffn_k_w, L1_ffn_k_b, L1_ffn_v_w, L1_ffn_v_b, L1_ffn_o_w, L1_ffn_o_b):
    import jax
    import jax.numpy as jnp

    def _L0_attn_ref(x, Wqkv, Wout, bout):
        import jax, jax.numpy as jnp
        import numpy as np
        B, T, D, H = (2, 256, 128, 16)
        b, t, d = x.shape
        h = H
        dh = d // h
        qkv = x @ Wqkv.T
        q, k, v = jnp.split(qkv, 3, axis=-1)

        def merge_heads(z):
            return z.reshape(b, t, h, dh).transpose(0, 2, 1, 3)
        q, k, v = map(merge_heads, (q, k, v))
        scale = dh ** (-0.5)
        dots = jnp.einsum('bhid,bhjd->bhij', q, k) * scale
        causal_mask = jnp.triu(jnp.ones((t, t), dtype=bool), 1)
        dots = jnp.where(causal_mask, -jnp.inf, dots)
        attn = jax.nn.softmax(dots, axis=-1)
        out = jnp.einsum('bhij,bhjd->bhid', attn, v)
        out = out.transpose(0, 2, 1, 3).reshape(b, t, d)
        return out @ Wout.T + bout

    def _L0_xattn_ref(q, kv, Wq, Wk, Wv, Wo, bo):
        import jax, jax.numpy as jnp
        import numpy as np
        H = 8
        B, Lq, dim_q = q.shape
        hd = dim_q // H
        scale = jnp.asarray(hd, q.dtype) ** (-0.5)
        qp = q @ Wq
        kp = kv @ Wk
        vp = kv @ Wv
        qh = qp.reshape(B, Lq, H, hd)
        kh = kp.reshape(B, kv.shape[1], H, hd)
        vh = vp.reshape(B, kv.shape[1], H, hd)
        scores = jnp.einsum('bqhd,bkhd->bhqk', qh, kh) * scale
        attn = jax.nn.softmax(scores, axis=-1)
        out = jnp.einsum('bhqk,bkhd->bqhd', attn, vh).reshape(B, Lq, dim_q)
        return out @ Wo + bo

    def _L0_ffn_ref(x, gate_w, gate_b, w1, w2, w3, ws1, ws2, ws3):
        import jax, jax.numpy as jnp
        import numpy as np
        E = 64
        K = 6
        CAP = 64
        ROUTE_SCALE = 1.0
        shape = x.shape
        D = shape[-1]
        xf = x.reshape(-1, D)
        T = xf.shape[0]
        scores = jax.nn.softmax(xf @ gate_w.T, axis=-1)
        _, idx = jax.lax.top_k(scores + gate_b, K)
        weights = jnp.take_along_axis(scores, idx, axis=1) * ROUTE_SCALE
        flat_e = idx.reshape(-1)
        order = jnp.argsort(flat_e)
        se = flat_e[order]
        counts = jnp.bincount(flat_e, length=E)
        starts = jnp.cumsum(counts) - counts
        pos = jnp.arange(T * K) - starts[se]
        tok = order // K
        xb = jnp.zeros((E, CAP, D), xf.dtype).at[se, pos].set(xf[tok], mode='drop')
        h = jax.nn.silu(jnp.einsum('ecd,eid->eci', xb, w1)) * jnp.einsum('ecd,eid->eci', xb, w3)
        yb = jnp.einsum('eci,edi->ecd', h, w2)
        valid = (pos < CAP).astype(xf.dtype)
        contrib = yb[se, jnp.minimum(pos, CAP - 1)]
        wf = weights.reshape(-1)[order] * valid
        y = jnp.zeros_like(xf).at[tok].add(contrib * wf[:, None])
        z = jax.nn.silu(xf @ ws1.T) * (xf @ ws3.T) @ ws2.T
        return (y + z).reshape(shape)

    def _L1_attn_ref(x, W_qkv, b_qkv, W_out, b_out):
        import jax, jax.numpy as jnp
        import numpy as np
        HIDDEN = 128
        NUM_HEADS = 16
        HEAD_SIZE = 64
        B, S, _ = x.shape
        qkv = x @ W_qkv + b_qkv
        qkv = qkv.reshape(B, S, 3 * NUM_HEADS, HEAD_SIZE)
        Q = qkv[:, :, :NUM_HEADS, :]
        K = qkv[:, :, NUM_HEADS:2 * NUM_HEADS, :]
        V = qkv[:, :, 2 * NUM_HEADS:, :]
        scores = jnp.einsum('bqhi,bkhi->bhqk', Q, K) / jnp.sqrt(jnp.float32(HEAD_SIZE))
        mask = jnp.triu(jnp.full((S, S), -10000.0, dtype=scores.dtype), k=1)
        scores = scores + mask
        probs = jax.nn.softmax(scores, axis=-1)
        vals = jnp.einsum('bkhi,bhqk->bqhi', V, probs)
        vals = vals.reshape(B, S, NUM_HEADS * HEAD_SIZE)
        return vals @ W_out + b_out

    def _L1_xattn_ref(x, context, Wq, Wk, Wv, Wo, bo):
        import jax, jax.numpy as jnp
        import numpy as np
        HEADS = 16
        DIM_HEAD = 64
        b, n, _ = x.shape
        h, d = (HEADS, DIM_HEAD)
        scale = d ** (-0.5)
        q = (x @ Wq).reshape(b, n, h, d).transpose(0, 2, 1, 3)
        k = (context @ Wk).reshape(b, -1, h, d).transpose(0, 2, 1, 3)
        v = (context @ Wv).reshape(b, -1, h, d).transpose(0, 2, 1, 3)
        sim = jnp.einsum('bhid,bhjd->bhij', q, k) * scale
        attn = jax.nn.softmax(sim, axis=-1)
        out = jnp.einsum('bhij,bhjd->bhid', attn, v)
        out = out.transpose(0, 2, 1, 3).reshape(b, n, h * d)
        return out @ Wo + bo

    def _L1_ffn_ref(x, router_prob, norm_w, norm_b, q_w, q_b, k_w, k_b, v_w, v_b, o_w, o_b):
        import jax, jax.numpy as jnp
        import numpy as np
        B, T, D, E, H = (4, 256, 128, 4, 8)
        EPS = 1e-05

        def _uniform(k, shape, bound):
            return jax.random.uniform(k, shape, jnp.float32, -bound, bound)

        def _layernorm(x, w, b):
            mu = jnp.mean(x, axis=-1, keepdims=True)
            var = jnp.mean(jnp.square(x - mu), axis=-1, keepdims=True)
            return (x - mu) * jax.lax.rsqrt(var + EPS) * w + b
        e_cnt = router_prob.shape[2]
        b, t, d = x.shape
        n = t // e_cnt
        h = H
        scale = d ** (-0.5)
        qs, ks_, vs = ([], [], [])
        for e in range(e_cnt):
            xe = x[:, e * n:(e + 1) * n, :]
            xn = _layernorm(xe, norm_w, norm_b)
            m = d // 2 ** e
            xm = xn[..., :m]
            qs.append(jnp.einsum('bnm,dm->bnd', xm, q_w[:, :m]) + q_b)
            ks_.append(jnp.einsum('bnm,dm->bnd', xm, k_w[:, :m]) + k_b)
            vs.append(jnp.einsum('bnm,dm->bnd', xm, v_w[:, :m]) + v_b)
        q = jnp.concatenate(qs, axis=1)
        k = jnp.concatenate(ks_, axis=1)
        v = jnp.concatenate(vs, axis=1)
        dh = d // h
        q = q.reshape(b, t, h, dh).transpose(0, 2, 1, 3)
        k = k.reshape(b, t, h, dh).transpose(0, 2, 1, 3)
        v = v.reshape(b, t, h, dh).transpose(0, 2, 1, 3)
        attn = jnp.einsum('bhqd,bhkd->bhqk', q, k) * scale
        attn = jax.nn.softmax(attn, axis=-1)
        attn_out = jnp.einsum('bhqk,bhkd->bhqd', attn, v)
        attn_out = attn_out.transpose(0, 2, 1, 3).reshape(b, t, d)
        outs = []
        for e in range(e_cnt):
            sl = slice(e * n, (e + 1) * n)
            m = d // 2 ** e
            xm = attn_out[:, sl, :m]
            out = jnp.einsum('bnm,om->bno', xm, o_w[:m, :m]) + o_b[:m]
            pad = d - m
            if pad:
                out = jnp.pad(out, ((0, 0), (0, 0), (0, pad)))
            outs.append(out + x[:, sl, :])
        return jnp.concatenate(outs, axis=1)
    x = _layernorm(x + _L0_attn_ref(x, L0_attn_Wqkv, L0_attn_Wout, L0_attn_bout), axis=-1)
    x = _layernorm(x + _L0_xattn_ref(x, ctx_768, L0_xattn_Wq, L0_xattn_Wk, L0_xattn_Wv, L0_xattn_Wo, L0_xattn_bo), axis=-1)
    x = _layernorm(x + _L0_ffn_ref(x, L0_ffn_gate_w, L0_ffn_gate_b, L0_ffn_w1, L0_ffn_w2, L0_ffn_w3, L0_ffn_ws1, L0_ffn_ws2, L0_ffn_ws3), axis=-1)
    x = _layernorm(x + _L1_attn_ref(x, L1_attn_W_qkv, L1_attn_b_qkv, L1_attn_W_out, L1_attn_b_out), axis=-1)
    x = _layernorm(x + _L1_xattn_ref(x, ctx_768, L1_xattn_Wq, L1_xattn_Wk, L1_xattn_Wv, L1_xattn_Wo, L1_xattn_bo), axis=-1)
    x = _layernorm(x + _L1_ffn_ref(x, L1_ffn_router_prob, L1_ffn_norm_w, L1_ffn_norm_b, L1_ffn_q_w, L1_ffn_q_b, L1_ffn_k_w, L1_ffn_k_b, L1_ffn_v_w, L1_ffn_v_b, L1_ffn_o_w, L1_ffn_o_b), axis=-1)
    return x

_drawn_inputs = setup_inputs


def setup_inputs(seed=0):
    import zlib

    import numpy as np

    out = dict(_drawn_inputs(seed))
    spreads = {'L0_ffn_gate_b': (0.0, 0.8),
     'L1_attn_b_qkv': (0.0, 0.1),
     'L1_attn_b_out': (0.0, 0.1),
     'L1_ffn_norm_w': (1.0, 0.6),
     'L1_ffn_norm_b': (0.0, 0.8)}
    factors = {'L0_attn_Wqkv': 4.469,
     'L0_attn_Wout': 4.354,
     'L0_xattn_bo': 3.833,
     'L0_ffn_gate_w': 8.0,
     'L0_ffn_w1': 8.0,
     'L0_ffn_w2': 8.0,
     'L0_ffn_w3': 8.0,
     'L0_ffn_ws1': 8.0,
     'L0_ffn_ws2': 8.0,
     'L0_ffn_ws3': 8.0,
     'L1_xattn_bo': 6.137,
     'L1_ffn_q_w': 8.0,
     'L1_ffn_q_b': 35.01,
     'L1_ffn_k_w': 8.0,
     'L1_ffn_k_b': 64.0,
     'L1_ffn_v_b': 6.916,
     'L1_ffn_o_b': 3.027}
    for name, (base, spread) in spreads.items():
        noise = np.random.default_rng([zlib.crc32(name.encode()), seed]).standard_normal(out[name].shape)
        drawn = base * np.exp(spread * noise) if base else spread * noise
        out[name] = jnp.asarray(drawn.astype(out[name].dtype))
    for name, factor in factors.items():
        out[name] = (out[name] * factor).astype(out[name].dtype)
    return out
```

```python
import numpy as np
import concourse.bass as bass
from concourse import mybir
from contextlib import ExitStack

FP32 = mybir.dt.float32
BF16 = mybir.dt.bfloat16
I32 = mybir.dt.int32
U32 = mybir.dt.uint32
ALU = mybir.AluOpType
ACT = mybir.ActivationFunctionType
AX = mybir.AxisListType

SEQS, T, D = 16, 256, 128
TOK = SEQS * T
CTX, DC = 64, 96
E, TOPK, CAP = 64, 6, 64
FI = 88
EPS = 1e-5
XW = D + E
BIG = 3.0e38
AB = (0, 1)
ITERS = SEQS // 2


class Attn:

    def __init__(self, name, heads, dh, ctx=False, causal=None, scale=None):
        self.name, self.heads, self.dh, self.ctx, self.causal = name, heads, dh, ctx, causal
        self.scale = scale
        self.big = dh == 64
        self.groups = heads // 4
        self.units = heads // 2 if self.big else heads // 4
        self.keys = CTX if ctx else T

    def s_chunks(self):
        out = []
        for qt in range(2):
            keys = self.keys
            if self.causal == "inf" and qt == 0:
                keys = 128
            n = 512 // keys
            out += [(qt, h, n, keys) for h in range(0, self.heads, n)]
        return out

    def t_chunks(self):
        if self.ctx:
            return [(0, (0, 1, 2, 3), 256)]
        if self.causal == "inf":
            return [(0, (0, 1), 256), (0, (2, 3), 256), (1, (0, 1, 2, 3), 128)]
        halves = ((0, 2), (1, 3)) if self.big else ((0, 1), (2, 3))
        return [(k, heads, 256) for k in range(2) for heads in halves]

    def place(self, ktile, j):
        if self.ctx:
            return 0, (j // 2) * 256, 0
        for i, (k, heads, queries) in enumerate(self.t_chunks()):
            if k == ktile and j in heads:
                return i, heads.index(j) * queries, T - queries


L0 = Attn("L0", 16, 8, causal="inf", scale=8.0 ** -0.5)
L0X = Attn("L0X", 8, 16, ctx=True, scale=0.25)
L1 = Attn("L1", 16, 64, causal="add", scale=0.125)
L1X = Attn("L1X", 16, 64, ctx=True, scale=0.125)
L1F = Attn("L1F", 8, 16, scale=float(D) ** -0.5)
NESTED = [(e, D >> e) for e in range(4)]


def project_steps(a, s):
    out = [("Q", a, s, i) for i in range(4 if a.big else 1)]
    if a is L1:
        out += [("K", a, s, i) for i in range(4)]
    elif a is L1X:
        out += [("K", a, s, 0)]
    out += [("C", a, s, 0)]
    nv = {L1: 4, L1X: 2}.get(a, 1)
    out += [("V", a, s, i) for i in range(nv)]
    out += [("S", a, s, i) for i in range(len(a.s_chunks()))]
    return out + [("N", a, s, 0)]


def head_steps(a, s):
    out = []
    for g in range(a.groups):
        out += [("T", a, s, g, i) for i in range(len(a.t_chunks()))]
        if g:
            out.append(("P", a, s, g - 1))
    return out + [("P", a, s, a.groups - 1)]


def tail_steps(a, s):
    out = [] if a.big else [("X", a, s, 0)]
    out += [("D", a, s, 0)] + [("B", a, s, i) for i in range(a.units // 2)]
    return out + [("W", a, s, 0), ("L", a, s, 0)]


def merged(main, side):
    out, k = [], 0
    for i, step in enumerate(main):
        out.append(step)
        while k < len(side) and k < (i + 1) * len(side) / len(main):
            out.append(side[k])
            k += 1
    return out + side[k:]


def phase1_steps():
    A, B = AB
    pre = lambda s: project_steps(L0, s)
    mid = lambda s: tail_steps(L0, s) + [("XT", L0X, s, 0)] + project_steps(L0X, s)
    end = lambda s: tail_steps(L0X, s) + [("XT", "R", s, 0)] + [(k, "R", s, 0) for k in ("R1", "R2", "R3")]
    return (pre(A) + merged(head_steps(L0, A), pre(B)) + merged(head_steps(L0, B), mid(A))
            + merged(head_steps(L0X, A), mid(B)) + merged(head_steps(L0X, B), end(A)) + end(B))


def phase3_steps():
    A, B = AB
    pre = lambda s: ([("XT", "F", s, 0), ("F1", "F", s, 0), ("F2", "F", s, 0), ("L", "F", s, 0),
                      ("XT", L1, s, 0)] + project_steps(L1, s))
    mid = lambda s: tail_steps(L1, s) + [("XT", L1X, s, 0)] + project_steps(L1X, s)
    last = lambda s: tail_steps(L1X, s) + [("LN", L1F, s, 0), ("XT", L1F, s, 0)] + project_steps(L1F, s)
    end = lambda s: tail_steps(L1F, s)
    return (pre(A) + merged(head_steps(L1, A), pre(B)) + merged(head_steps(L1, B), mid(A))
            + merged(head_steps(L1X, A), mid(B)) + merged(head_steps(L1X, B), last(A))
            + merged(head_steps(L1F, A), last(B)) + merged(head_steps(L1F, B), end(A)) + end(B))


BANKS = {"S": (0, 1), "T": (2, 3), "O": (4,), "D": (5,), "M": (6, 7)}


def fills(step):
    kind, a = step[0], step[1]
    if kind == "P":
        g = step[3]
        if g == 0 and a.big:
            return ["D", "O"]
        if a.big or g % 2 == 0:
            return ["O"]
        return []
    if kind == "F1":
        return ["M", "M"]
    if kind == "D" or kind == "L" or kind == "C" or kind == "LN":
        return []
    return [{"S": "S", "T": "T", "X": "D"}.get(kind, "M")]


class Ledger:

    def __init__(self, steps):
        self.use, self.per = {}, [0] * 8
        turn = {k: 0 for k in BANKS}
        for step in steps:
            for i, kind in enumerate(fills(step)):
                ring = BANKS[kind]
                b = ring[turn[kind] % len(ring)]
                turn[kind] += 1
                self.use[step, i] = (b, self.per[b])
                self.per[b] += 1


def decoder_program(nc, inp, out):
    ctx = ExitStack()
    with ctx:
        def sb(name, shape, dt=FP32):
            return ctx.enter_context(nc.sbuf_tensor(name, shape, dt))

        def sem(name):
            return ctx.enter_context(nc.semaphore(name))

        def pair(name, shape, dt=FP32):
            return [sb(f"{name}{s}", shape, dt) for s in AB]

        xg = nc.dram_tensor("xg", [TOK, XW], FP32, kind="Internal").ap()
        keyd = nc.dram_tensor("keyd", [E, TOK], FP32, kind="Internal").ap()
        zd = nc.dram_tensor("zd", [TOK * TOPK, D], FP32, kind="Internal").ap()

        ident = sb("ident", [128, 128])
        ident_b = sb("ident_b", [128, 128], BF16)
        neg_ident = sb("neg_ident", [128, 128], BF16)
        ident_inf = sb("ident_inf", [128, 128], BF16)
        ident_add = sb("ident_add", [128, 128], BF16)
        mask_s = sb("mask_s", [128, 384], BF16)
        mask_t = sb("mask_t", [128, 384], BF16)
        sel_h = sb("sel_h", [16, 16, 128], BF16)
        sel_flat = sel_h[:, :, :].rearrange("i h k -> i (h k)")
        head_mask = sb("head_mask", [128, 24])
        ones_g = sb("ones_g", [128, 4, 32])
        ones_u = sb("ones_u", [128, 2, 4, 32])
        pick_sum = sb("pick_sum", [128, 32])
        spread_s = sb("spread_s", [128, 4, 128])
        spread_b = sb("spread_b", [128, 8, 128])
        upper = sb("upper", [64, 64])
        upper_b = sb("upper_b", [64, 64], BF16)

        w0_qkv = sb("w0_qkv", [128, 384])
        w0_o = sb("w0_o", [128, 4, 128])
        b0_o = sb("b0_o", [128, 128])
        wx_q = sb("wx_q", [128, 128])
        wx_kv = sb("wx_kv", [DC, 256])
        wx_o = sb("wx_o", [128, 2, 128])
        bx_o = sb("bx_o", [128, 128])
        gate_w = sb("gate_w", [128, E])
        gate_b = sb("gate_b", [128, E])
        ws13 = sb("ws13", [128, 4, FI])
        ws2 = sb("ws2", [FI, 2, 128])
        w1_qkv = sb("w1_qkv", [128, 3072])
        b1_qk = sb("b1_qk", [128, 16])
        b1_v = sb("b1_v", [128, 1024])
        w1_o = sb("w1_o", [128, 8, 128])
        b1_o = sb("b1_o", [128, 128])
        w1x_q = sb("w1x_q", [128, 1024])
        w1x_k = sb("w1x_k", [DC, 1024])
        w1x_v = sb("w1x_v", [DC, 1024])
        w1x_o = sb("w1x_o", [128, 8, 128])
        b1x_o = sb("b1x_o", [128, 128])
        wf_qkv = sb("wf_qkv", [128, 384])
        bf_cols = sb("bf_cols", [128, 4])
        bf_v = sb("bf_v", [128, 128])
        wf_o = sb("wf_o", [128, 5, 128])
        bf_o = sb("bf_o", [128, 2, 128])

        union = pair("union", [128, 1536])
        x_in = [u[:, 0:256].rearrange("p (t d) -> p t d", t=2) for u in union]
        xt_in = [u[:, 256:512] for u in union]
        xs = [u[:, 512:512 + 2 * XW].rearrange("p (t d) -> p t d", t=2) for u in union]
        va_x = [u[:, 1024:1280].rearrange("p (h d) -> p h d", h=8) for u in union]
        routed = [u[:, :].rearrange("p (t k d) -> p t k d", t=2, k=TOPK) for u in union]
        x3_in = pair("x3_in", [128, 2, D])
        tri = x3_in[0][:, :, :].rearrange("p t d -> p (t d)")
        x_tok = pair("x_tok", [128, 2, D])
        x_res = pair("x_res", [128, 2, D])
        xt = pair("xt", [128, T])
        summed = pair("summed", [128, 2, D])
        x_out = pair("x_out", [128, 2, D])
        ctx_t = pair("ctx_t", [DC, 2, CTX])
        qt = pair("qt", [128, 8, T])
        kt = pair("kt", [128, 8, T])
        v_big = pair("v_big", [128, 2, 1024])
        kx = pair("kx", [128, 16, CTX])
        vx = pair("vx", [128, 8, 128])
        va = pair("va", [128, 2, 16, 32])
        qb = sb("qb", [128, 8, T], BF16)
        kb = sb("kb", [128, 16, T], BF16)
        kbf = sb("kbf", [128, 8, T], BF16)
        zeros = kbf[:, :, :].rearrange("p a b -> p (a b)").bitcast(FP32)
        kxb = sb("kxb", [128, 16, CTX], BF16)
        prob = sb("prob", [128, 8, 512])
        peak = pair("peak", [128, 2, 16], BF16)
        shift = pair("shift", [16, T], BF16)
        rsum = pair("rsum", [128, T])
        stats = pair("stats", [128, 2, 6])
        moments = pair("moments", [128, 2, 2])
        powers = sb("powers", [128, 4])
        rstd = pair("rstd", [128, 2])
        hid = [t[0:FI, 0, 0:512].rearrange("p (c t) -> p c t", c=2) for t in v_big]
        hid_e = [t[0:FI, 1, 0:512].rearrange("p (c t) -> p c t", c=2) for t in v_big]
        r_exp = pair("r_exp", [128, 2, E])
        r_sel = pair("r_sel", [128, 2, E + 2])
        r_top = pair("r_top", [128, 2, 8])
        r_rep = pair("r_rep", [128, 2, E + 2])
        r_mask = pair("r_mask", [128, 2, E], BF16)
        r_maskt = pair("r_maskt", [E, T], BF16)
        r_col = pair("r_col", [128, 6])
        r_key = [t[0:E, :, :].rearrange("p t d -> p (t d)") for t in x_out]
        token_key = x3_in[1][0:E, :, :].rearrange("p t d -> p (t d)")

        kv = [v_big[s][:, :, :].rearrange("p a (b t) -> p (a b) t", t=T) for s in AB]

        def k_of(a, s, h):
            if a is L0:
                return (kt[s] if h < 8 else kv[s])[:, h % 8, :]
            if a is L1F:
                return kv[s][:, h, :]
            return kx[s][:, h, :]

        psum = [ctx.enter_context(nc.psum_tensor(f"bank{b}", [128, 512], FP32)) for b in range(8)]

        weights_in = sem("weights_in")
        consts_ready = sem("consts_ready")
        zeroed = sem("zeroed")
        passed = sem("passed")
        chain = sem("chain")

        class Sync:

            def __init__(self, tag):
                n = lambda name: [sem(f"{tag}_{name}{s}") for s in AB]
                self.full = [sem(f"{tag}_full{b}") for b in range(8)]
                self.free = [sem(f"{tag}_free{b}") for b in range(8)]
                self.x_in = n("x_in")
                self.x_used = n("x_used")
                self.x_ready = n("x_ready")
                self.res_ready = n("res_ready")
                self.moments_ready = n("moments_ready")
                self.stats_ready = n("stats_ready")
                self.rstd_ready = n("rstd_ready")
                self.eps_added = n("eps_added")
                self.q16 = n("q16")
                self.k_masked = n("k_masked")
                self.k16 = n("k16")
                self.out_done = n("out_done")
                if tag == "p1":
                    self.r_neg = n("r_neg")
                    self.r_link = n("r_link")
                    self.r_masked = n("r_masked")
                    self.r_keyed = n("r_keyed")
                    self.key_done = n("key_done")
                    self.tk_link = sem(f"{tag}_tk_link")
                else:
                    self.twice = n("twice")
                    self.h_exp = n("h_exp")
                    self.h_link = n("h_link")
                    self.z_sum = n("z_sum")
                    self.ctx_in = n("ctx_in")

        p1, p3 = Sync("p1"), Sync("p3")

        LNS = {("p1", L0): 0, ("p1", L0X): 1,
               ("p3", "F"): 0, ("p3", L1): 1, ("p3", L1X): 2, ("p3", "LN"): 3, ("p3", L1F): 4}
        LN_PER = {"p1": 2, "p3": 5}
        ATTN = {("p1", L0): 0, ("p1", L0X): 1, ("p3", L1): 0, ("p3", L1X): 1, ("p3", L1F): 2}
        ATTN_PER = {"p1": 2, "p3": 3}

        plan = {"p1": phase1_steps(), "p3": phase3_steps()}

        def carry_wait(eng):
            eng.sem_inc(passed, 1)

        ledger = {tag: Ledger(steps) for tag, steps in plan.items()}
        sync = {"p1": p1, "p3": p3}

        class View:

            def __init__(self, tag, it):
                self.tag, self.it, self.y = tag, it, sync[tag]

            def may_fill(self, step, i=0):
                b, n = ledger[self.tag].use[step, i]
                return self.y.free[b], self.it * ledger[self.tag].per[b] + (n + 1)

            def filled(self, step, i=0):
                b, n = ledger[self.tag].use[step, i]
                return self.y.full[b], self.it * ledger[self.tag].per[b] + (n + 1)

            def drained(self, step, i=0):
                b, n = ledger[self.tag].use[step, i]
                return self.y.free[b], self.it * ledger[self.tag].per[b] + (n + 2)

            def bank(self, step, i=0):
                return psum[ledger[self.tag].use[step, i][0]]

            def full(self, step, i=0):
                return self.y.full[ledger[self.tag].use[step, i][0]]

            def free(self, step, i=0):
                return self.y.free[ledger[self.tag].use[step, i][0]]

            def ln(self, which):
                return self.it * LN_PER[self.tag] + (LNS[self.tag, which] + 1)

            def attn(self, a):
                return self.it * ATTN_PER[self.tag] + (ATTN[self.tag, a] + 1)

            def once(self):
                return self.it * 1 + 1

        def previous_x(a):
            return {L0X: L0, "R": L0X, L1: "F", L1X: L1, L1F: "LN"}[a]

        def x_source(tag, a, s):
            if a is L0:
                return x_in[s][:, :, :]
            if a == "F":
                return x3_in[s][:, :, :]
            if a == "R":
                return xs[s][:, :, 0:D]
            if a is L1F:
                return summed[s][:, :, :]
            return x_tok[s][:, :, :]

        def o_unit(a, s, u, n=1):
            base = {L0: 2, L0X: 2, L1F: 2}.get(a, 0)
            return qt[s][:, base + u:base + u + n, :]

        def tensor_step(pe, v, step):
            kind, a, s = step[0], step[1], step[2]
            y, mm = v.y, nc.tensor.matmul
            if kind == "XT":
                if a == "F":
                    pe.wait_ge(y.x_in[s], v.it * 32 + 32)
                else:
                    pe.wait_ge(y.x_ready[s], v.ln(previous_x(a)))
                pe.wait_ge(*v.may_fill(step))
                src, bank = x_source(v.tag, a, s), v.bank(step)
                for t in range(2):
                    last = mm(bank[:, t * 128:(t + 1) * 128], src[:, t, :], ident[:, :], start=True, stop=True)
                last.then_inc(v.full(step), 1)
            elif kind == "Q":
                i, bank = step[3], v.bank(step)
                x = xt_in[s] if a is L0 else xt[s][:, :]
                if a is L0:
                    pe.wait_ge(y.x_in[s], v.it * 48 + 48)
                elif i == 0:
                    pe.wait_ge(*v.drained(("XT", a, s, 0)))
                    if a is L0X:
                        pe.wait_ge(y.x_in[s], v.it * 48 + 48)
                pe.wait_ge(*v.may_fill(step))
                if a.big:
                    w = w1_qkv if a is L1 else w1x_q
                    for j in range(2):
                        c = 2 * i + j
                        last = mm(bank[:, j * 256:(j + 1) * 256], w[:, c * 128:(c + 1) * 128], x,
                                  start=True, stop=True)
                elif a is L0:
                    for j in range(2):
                        last = mm(bank[:, j * 256:(j + 1) * 256], w0_qkv[:, j * 128:(j + 1) * 128], x,
                                  start=True, stop=True)
                elif a is L0X:
                    mm(bank[:, 0:256], wx_q[:, :], x, start=True, stop=True)
                    last = mm(bank[:, 256:256 + CTX], wx_kv[:, 0:128], ctx_t[s][:, 0, :], start=True, stop=True)
                else:
                    for j in range(2):
                        for e, m in NESTED:
                            last = mm(bank[:, j * 256 + 64 * e:j * 256 + 64 * e + 64],
                                      wf_qkv[0:m, j * 128:(j + 1) * 128], xt[s][0:m, 64 * e:64 * e + 64],
                                      start=True, stop=True)
                last.then_inc(v.full(step), 1)
            elif kind == "K":
                i, bank = step[3], v.bank(step)
                if a is L1X:
                    pe.wait_ge(y.ctx_in[s], v.it * 16 + 16)
                pe.wait_ge(*v.may_fill(step))
                if a is L1:
                    for j in range(2):
                        c = 8 + 2 * i + j
                        last = mm(bank[:, j * 256:(j + 1) * 256], w1_qkv[:, c * 128:(c + 1) * 128], xt[s][:, :],
                                  start=True, stop=True)
                else:
                    for c in range(8):
                        last = mm(bank[:, c * CTX:(c + 1) * CTX], w1x_k[:, c * 128:(c + 1) * 128],
                                  ctx_t[s][:, 0, :], start=True, stop=True)
                last.then_inc(v.full(step), 1)
            elif kind == "V":
                i, bank = step[3], v.bank(step)
                pe.wait_ge(*v.may_fill(step))
                if a is L1:
                    t, half = i // 2, i % 2
                    last = mm(bank[:, :], xt[s][:, t * 128:(t + 1) * 128],
                              w1_qkv[:, 2048 + 512 * half:2560 + 512 * half], start=True, stop=True)
                elif a is L1X:
                    last = mm(bank[:, :], ctx_t[s][:, :, :], w1x_v[:, 512 * i:512 * i + 512], start=True, stop=True)
                elif a is L0:
                    for t in range(2):
                        last = mm(bank[:, t * 128:(t + 1) * 128], xt_in[s][:, t * 128:(t + 1) * 128],
                                  w0_qkv[:, 256:384], start=True, stop=True)
                elif a is L0X:
                    last = mm(bank[:, 0:128], ctx_t[s][:, :, :], wx_kv[:, 128:256], start=True, stop=True)
                else:
                    for e, m in NESTED:
                        p = 64 * (e % 2)
                        last = mm(bank[p:p + 64, (e // 2) * 128:(e // 2) * 128 + 128],
                                  xt[s][0:m, 64 * e:64 * e + 64], wf_qkv[0:m, 256:384], start=True, stop=True)
                last.then_inc(v.full(step), 1)
            elif kind == "S":
                qtile, h0, n, keys = a.s_chunks()[step[3]]
                bank = v.bank(step)
                if step[3] == 0:
                    pe.wait_ge(y.q16[s], v.attn(a))
                    pe.wait_ge(y.k16[s], v.attn(a))
                pe.wait_ge(*v.may_fill(step))
                q0 = qtile * 128
                if a.causal:
                    neg = ident_inf if a.causal == "inf" else ident_add
                    lo = 128 if qtile == 0 else 0
                    mask = mask_s[:, lo:lo + keys].unsqueeze(1).to_broadcast([128, n, keys])
                    mm(bank[:, :].rearrange("p (h k) -> p h k", h=n), neg[:, :], mask, start=True, stop=False)
                if a.ctx and a.big:
                    for j in range(n // 2):
                        c = h0 // 2 + j
                        last = mm(bank[:, j * 128:(j + 1) * 128], qb[:, c, q0:q0 + 128],
                                  kxb[:, 2 * c:2 * c + 2, :], start=True, stop=True)
                else:
                    k16 = (kxb if a.ctx else kbf if a is L1F else kb)[:, h0:h0 + n, 0:keys]
                    c = h0 // 2 if a.big else 0
                    last = mm(bank[:, 0:n * keys].rearrange("p (h k) -> p h k", h=n), qb[:, c, q0:q0 + 128], k16,
                              start=not a.causal, stop=True)
                last.then_inc(v.full(step), 1)
            elif kind == "N":
                bank = v.bank(step)
                pe.wait_ge(*v.drained(("S", a, s, len(a.s_chunks()) - 1)))
                pe.wait_ge(*v.may_fill(step))
                for t in range(2):
                    last = mm(bank[0:a.heads, t * 128:(t + 1) * 128], peak[s][:, t, 0:a.heads], neg_ident[:, :],
                              start=True, stop=True)
                last.then_inc(v.full(step), 1)
            elif kind == "T":
                g, i = step[3], step[4]
                ktile, heads, queries = a.t_chunks()[i]
                n = len(heads)
                bank = v.bank(step)
                if g == 0 and i == 0:
                    pe.wait_ge(*v.drained(("N", a, s, 0)))
                pe.wait_ge(*v.may_fill(step))
                q0 = 256 - queries
                if a.ctx:
                    for j in range(2):
                        c = 2 * g + j
                        cols = bank[:, j * 256:(j + 1) * 256]
                        pair_sel = sel_flat[0:a.heads, 256 * c + CTX:256 * c + 3 * CTX]
                        mm(cols, pair_sel, shift[s][0:a.heads, :],
                           start=True, stop=False)
                        q = qt[s][:, c, :] if a.big else qt[s][:, 0, :]
                        last = mm(cols, kx[s][:, 2 * c:2 * c + 2, :], q, start=False, stop=True)
                else:
                    if a.causal:
                        neg = ident_inf if a.causal == "inf" else ident_add
                        lo = 128 if (ktile == 0 or queries == 128) else 0
                        mask = mask_t[:, lo:lo + queries].unsqueeze(1).to_broadcast([128, n, queries])
                        mm(bank[:, :].rearrange("p (h q) -> p h q", h=n), neg[:, :], mask, start=True, stop=False)
                    for j in range(n):
                        h = 4 * g + heads[j]
                        cols = bank[:, j * queries:(j + 1) * queries]
                        mm(cols, sel_h[0:a.heads, h, :], shift[s][0:a.heads, q0:256], start=not a.causal, stop=False)
                        if a.big:
                            r = 64 * (h % 2)
                            lhs = kt[s][r:r + 64, h // 2, ktile * 128:(ktile + 1) * 128]
                            rhs = qt[s][r:r + 64, h // 2, :]
                        else:
                            lhs = k_of(a, s, h)[:, ktile * 128:(ktile + 1) * 128]
                            rhs = qt[s][:, 0, q0:256]
                        last = mm(cols, lhs, rhs, start=False, stop=not a.causal or j == n - 1)
                last.then_inc(v.full(step), 1)
            elif kind == "P":
                g = step[3]
                nt = len(a.t_chunks())
                for i in range(max(0, nt - 2), nt):
                    pe.wait_ge(*v.drained(("T", a, s, g, i)))
                if g == 0:
                    if a is L1:
                        pe.wait_ge(*v.drained(("V", a, s, 3)))
                    elif a is L1X:
                        pe.wait_ge(*v.drained(("V", a, s, 1)))
                    else:
                        pe.wait_ge(*v.drained(("V", a, s, 0)))
                slot = 4 * (g % 2)

                def p_of(ktile, j):
                    i, col, q0 = a.place(ktile, j)
                    return prob[:, slot + i, col:col + T - q0], q0

                kts = 1 if a.ctx else 2
                if a.big:
                    o_fill = step, 1 if g == 0 else 0
                    pe.wait_ge(*v.may_fill(*o_fill))
                    bank = v.bank(*o_fill)
                    for j in range(2):
                        cols = bank[:, j * 256:(j + 1) * 256]
                        if a.ctx:
                            last = mm(cols, vx[s][:, 2 * g + j, :], p_of(0, 2 * j)[0], start=True, stop=True)
                        else:
                            for k in range(2):
                                for u in range(2):
                                    h = 4 * g + 2 * j + u
                                    last = mm(cols[64 * u:64 * u + 64, :], v_big[s][:, k, h * 64:(h + 1) * 64],
                                              p_of(k, 2 * j + u)[0], start=(k == 0), stop=(k == 1))
                    last.then_inc(v.full(*o_fill), 1)
                    d_fill = ("P", a, s, 0), 0
                    if g == 0:
                        pe.wait_ge(*v.may_fill(*d_fill))
                    sums = v.bank(*d_fill)
                    for k in range(kts):
                        for j in range(4):
                            lhs = ones_u[:, j % 2, g, :] if a.ctx else ones_g[:, g, :]
                            last = mm(sums[32 * j:32 * j + 32, 0:256], lhs, p_of(k, j)[0],
                                      start=(g == 0 and k == 0), stop=(g == a.groups - 1 and k == kts - 1))
                    if g == a.groups - 1:
                        last.then_inc(v.full(*d_fill), 1)
                else:
                    fill = ("P", a, s, g - g % 2), 0
                    if g % 2 == 0:
                        pe.wait_ge(*v.may_fill(*fill))
                    bank = v.bank(*fill)
                    for k in range(kts):
                        for j in range(4):
                            p, q0 = p_of(k, j)
                            h = 4 * g + j
                            lhs = va_x[s][:, h, :] if a.ctx else va[s][:, k, h, :]
                            last = mm(bank[32 * j:32 * j + 32, (g % 2) * 256 + q0:(g % 2) * 256 + 256], lhs, p,
                                      start=(k == 0), stop=(k == kts - 1))
                    if g % 2 == 1:
                        last.then_inc(v.full(*fill), 1)
            elif kind == "X":
                bank = v.bank(step)
                for u in range(0, a.units, 2):
                    pe.wait_ge(*v.drained(("P", a, s, u)))
                pe.wait_ge(*v.may_fill(step))
                for u in range(a.units):
                    last = mm(bank[32 * u:32 * u + 32, 0:256], pick_sum[:, :], o_unit(a, s, u)[:, 0, :],
                              start=True, stop=True)
                last.then_inc(v.full(step), 1)
            elif kind == "B":
                i, bank = step[3], v.bank(step)
                if i == 0:
                    pe.wait_ge(*v.drained(("P", a, s, 0) if a.big else ("X", a, s, 0)))
                pe.wait_ge(*v.may_fill(step))
                rows = 128 if a.big else 32 * a.units
                for j in range(2):
                    u = 2 * i + j
                    lhs = (spread_b if a.big else spread_s)[0:rows, u, :]
                    last = mm(bank[:, j * 256:(j + 1) * 256], lhs, rsum[s][0:rows, :], start=True, stop=True)
                last.then_inc(v.full(step), 1)
            elif kind == "W":
                bank = v.bank(step)
                pe.wait_ge(*v.drained(("B", a, s, a.units // 2 - 1)))
                pe.wait_ge(*v.may_fill(step))
                if a is L1F:
                    for e, m in NESTED:
                        p = 64 * (e % 2)
                        rows = [(u, 128) for u in range(2)] if e == 0 else [(0, {1: 128, 2: 64, 3: 32}[e])]
                        for n, (u, r) in enumerate(rows):
                            last = mm(bank[p:p + 64, (e // 2) * 128:(e // 2) * 128 + 128],
                                      o_unit(a, s, u)[0:r, 0, 64 * e:64 * e + 64], wf_o[0:r, e + (e > 0) + u, :],
                                      start=(n == 0), stop=(n == len(rows) - 1))
                else:
                    w = {L0: w0_o, L0X: wx_o, L1: w1_o, L1X: w1x_o}[a]
                    for t in range(2):
                        for u in range(a.units):
                            last = mm(bank[:, t * 128:(t + 1) * 128], o_unit(a, s, u)[:, 0, t * 128:(t + 1) * 128],
                                      w[:, u, :], start=(u == 0), stop=(u == a.units - 1))
                last.then_inc(v.full(step), 1)
            elif kind == "R1":
                pe.wait_ge(*v.drained(("XT", "R", s, 0)))
                pe.wait_ge(*v.may_fill(step))
                bank = v.bank(step)
                for t in range(2):
                    last = mm(bank[:, t * E:(t + 1) * E], xt[s][:, t * 128:(t + 1) * 128], gate_w[:, :],
                              start=True, stop=True)
                last.then_inc(v.full(step), 1)
            elif kind == "R2":
                pe.wait_ge(y.r_masked[s], v.once())
                pe.wait_ge(*v.may_fill(step))
                bank = v.bank(step)
                for t in range(2):
                    last = mm(bank[0:E, t * 128:(t + 1) * 128], r_mask[s][:, t, :], ident_b[:, :],
                              start=True, stop=True)
                last.then_inc(v.full(step), 1)
            elif kind == "R3":
                pe.wait_ge(*v.drained(("R2", "R", s, 0)))
                pe.wait_ge(*v.may_fill(step))
                carry_wait(pe)
                mm(v.bank(step)[0:E, 0:256], upper_b[:, :], r_maskt[s][:, :],
                   start=True, stop=True).then_inc(v.full(step), 1)
            elif kind == "F1":
                pe.wait_ge(*v.drained(("XT", "F", s, 0)))
                for i in range(2):
                    pe.wait_ge(*v.may_fill(step, i))
                    for c in range(2):
                        last = mm(v.bank(step, i)[0:FI, c * 256:(c + 1) * 256], ws13[:, 2 * i + c, :], xt[s][:, :],
                                  start=True, stop=True)
                    last.then_inc(v.full(step, i), 1)
            elif kind == "F2":
                pe.wait_ge(*v.drained(("F1", "F", s, 0), 1))
                pe.wait_ge(*v.may_fill(step))
                for t in range(2):
                    for c in range(2):
                        last = mm(v.bank(step)[:, t * 128:(t + 1) * 128], hid[s][:, c, t * 128:(t + 1) * 128],
                                  ws2[:, c, :], start=(c == 0), stop=(c == 1))
                last.then_inc(v.full(step), 1)

        def scalar_step(act, v, step):
            kind, a, s = step[0], step[1], step[2]
            y, copy = v.y, nc.scalar.copy
            if kind == "XT":
                act.wait_ge(*v.filled(step))
                if a is L1F:
                    nc.scalar.activation(xt[s][:, :], v.bank(step)[:, 0:256], ACT.Identity, bias=bf_cols[:, 1:2],
                                         scale=bf_cols[:, 0:1]).then_inc(v.free(step), 1)
                else:
                    copy(xt[s][:, :], v.bank(step)[:, 0:256]).then_inc(v.free(step), 1)
            elif kind == "Q":
                i, bank = step[3], v.bank(step)
                act.wait_ge(*v.filled(step))
                if a is L1:
                    for j in range(2):
                        c = 2 * i + j
                        last = nc.scalar.activation(qt[s][:, c, :], bank[:, j * 256:(j + 1) * 256], ACT.Identity,
                                                    bias=b1_qk[:, c:c + 1])
                elif a is L1X:
                    last = copy(qt[s][:, 2 * i:2 * i + 2, :], bank[:, :].rearrange("p (c t) -> p c t", c=2))
                elif a is L1F:
                    for j in range(2):
                        last = nc.scalar.activation(qt[s][:, j, :], bank[:, j * 256:(j + 1) * 256], ACT.Identity,
                                                    bias=bf_cols[:, 2 + j:3 + j])
                elif a is L0:
                    last = copy(qt[s][:, 0:2, :], bank[:, :].rearrange("p (c t) -> p c t", c=2))
                else:
                    flat = qt[s][:, :, :].rearrange("p c t -> p (c t)")
                    last = copy(flat[:, 0:256 + CTX], bank[:, 0:256 + CTX])
                last.then_inc(v.free(step), 1)
            elif kind == "C":
                last_q = ("Q", a, s, 3 if a.big else 0)
                act.wait_ge(*v.drained(last_q))
                n = 8 if a.big else 1
                copy(qb[:, 0:n, :], qt[s][:, 0:n, :]).then_inc(y.q16[s], 1)
            elif kind == "V" and a not in (L1, L1F):
                i, bank = step[3], v.bank(step)
                act.wait_ge(*v.filled(step))
                if a is L0:
                    last = copy(va[s][:, :, :, 0:8], bank[:, 0:256].rearrange("p (t h d) -> p t h d", t=2, h=16))
                elif a is L0X:
                    for u in range(2):
                        src = bank[64 * u:64 * u + 64, 0:128].rearrange("p (c u d) -> p c u d", u=2, d=16)
                        dst = va_x[s][64 * u:64 * u + 64, :, 0:16].rearrange("p (c u) d -> p c u d", u=2)
                        last = copy(dst[:, :, u, :], src[:, :, u, :])
                else:
                    for u in range(2):
                        src = bank[64 * u:64 * u + 64, :].rearrange("p (c u d) -> p c u d", u=2, d=64)
                        last = copy(vx[s][64 * u:64 * u + 64, 4 * i:4 * i + 4, 64 * u:64 * u + 64], src[:, :, u, :])
                last.then_inc(v.free(step), 1)
            elif kind == "N":
                act.wait_ge(*v.filled(step))
                copy(shift[s][0:a.heads, :], v.bank(step)[0:a.heads, 0:256]).then_inc(v.free(step), 1)
            elif kind == "T":
                g, i = step[3], step[4]
                act.wait_ge(*v.filled(step))
                nc.scalar.activation(prob[:, 4 * (g % 2) + i, :], v.bank(step)[:, :], ACT.Exp,
                                     scale=a.scale).then_inc(v.free(step), 1)
            elif kind == "P":
                g = step[3]
                if a.big:
                    fill = step, 1 if g == 0 else 0
                elif g % 2 == 1:
                    fill = ("P", a, s, g - 1), 0
                else:
                    return
                act.wait_ge(*v.filled(*fill))
                u0 = 2 * g if a.big else g - 1
                copy(o_unit(a, s, u0, 2), v.bank(*fill)[:, :].rearrange("p (c t) -> p c t", c=2)).then_inc(
                    v.free(*fill), 1)
            elif kind == "R1":
                act.wait_ge(y.r_neg[s], v.once())
                for t in range(2):
                    last = nc.scalar.activation(r_exp[s][:, t, :], v.bank(step)[:, t * E:(t + 1) * E], ACT.Exp,
                                                bias=r_col[s][:, t:t + 1], accum_out=r_col[s][:, 2 + t:3 + t])
                last.then_inc(v.free(step), 1)
            elif kind == "R2":
                act.wait_ge(*v.filled(step))
                copy(r_maskt[s][:, :], v.bank(step)[0:E, 0:256]).then_inc(v.free(step), 1)
            elif kind == "F1":
                act.wait_ge(*v.filled(step, 0))
                nc.scalar.activation(hid_e[s], v.bank(step, 0)[0:FI, :].rearrange("p (c t) -> p c t", c=2),
                                     ACT.Exp, scale=-1.0).then_inc(y.h_exp[s], 1)

        def layer_norm_sums(dve, v, s, which, src):
            y = v.y
            for t in range(2):
                last = nc.vector.bn_stats(stats[s][:, t, :], src[:, t, :])
            last.then_inc(y.stats_ready[s], 1)
            dve.wait_ge(y.stats_ready[s], v.ln(which))
            carry_wait(dve)
            for t in range(2):
                last = nc.vector.bn_aggr(moments[s][:, t, :], stats[s][:, t, :])
            last.then_inc(y.moments_ready[s], 1)

        def layer_norm_apply(dve, v, s, which, src, dst):
            y = v.y
            dve.wait_ge(y.rstd_ready[s], v.ln(which))
            for t in range(2):
                last = nc.vector.tensor_scalar(dst[:, t, :], src[:, t, :], moments[s][:, t, 0:1],
                                               rstd[s][:, t:t + 1], ALU.subtract, ALU.mult)
            last.then_inc(y.x_ready[s], 1)

        def vector_step(dve, v, step):
            kind, a, s = step[0], step[1], step[2]
            y, tt = v.y, nc.vector.tensor_tensor
            if kind == "K":
                i, bank = step[3], v.bank(step)
                dve.wait_ge(*v.filled(step))
                if a is L1:
                    bias = b1_qk[:, 8 + 2 * i:10 + 2 * i].unsqueeze(2).to_broadcast([128, 2, T])
                    last = tt(kt[s][:, 2 * i:2 * i + 2, :], bank[:, :].rearrange("p (c t) -> p c t", c=2), bias,
                              ALU.add)
                else:
                    for u in range(2):
                        dst = kx[s][64 * u:64 * u + 64, :, :].rearrange("p (c u) k -> p c u k", u=2)
                        src = bank[64 * u:64 * u + 64, :].rearrange("p (c k) -> p c k", c=8)
                        last = nc.vector.tensor_copy(dst[:, :, u, :], src)
                last.then_inc(v.free(step), 1)
            elif kind == "C":
                if a is L1:
                    dve.wait_ge(*v.drained(("K", a, s, 3)))
                    for u in range(2):
                        dst = kb[64 * u:64 * u + 64, :, :].rearrange("p (c u) k -> p c u k", u=2)
                        last = nc.vector.tensor_copy(dst[:, :, u, :], kt[s][64 * u:64 * u + 64, :, :])
                elif a is L1X:
                    dve.wait_ge(*v.drained(("K", a, s, 0)))
                    last = nc.vector.tensor_copy(kxb[:, :, :], kx[s][:, :, :])
                else:
                    dve.wait_ge(*v.drained(("Q", a, s, 0)))
                    n, m0 = (16, 0) if a is L0 else (8, 16)
                    k1 = qt[s][:, 1, 0:a.keys]
                    parts = {L0: [kt[s][:, :, :], kv[s]], L0X: [kx[s][:, 0:8, :]],
                             L1F: [kv[s]]}[a]
                    for j, part in enumerate(parts):
                        m = head_mask[:, m0 + 8 * j:m0 + 8 * j + 8].unsqueeze(2).to_broadcast([128, 8, a.keys])
                        last = tt(part, k1.unsqueeze(1).to_broadcast([128, 8, a.keys]), m, ALU.mult)
                    last.then_inc(y.k_masked[s], 1)
                    dve.wait_ge(y.k_masked[s], v.it * (2 if v.tag == "p1" else 1)
                                + (1 if a is L1F else ATTN[v.tag, a] + 1))
                    k16 = {L0: kb, L0X: kxb, L1F: kbf}[a]
                    for j, part in enumerate(parts):
                        last = nc.vector.tensor_copy(k16[:, 8 * j:8 * j + 8, :], part)
                last.then_inc(y.k16[s], 1)
            elif kind == "V" and a in (L1, L1F):
                i, bank = step[3], v.bank(step)
                dve.wait_ge(*v.filled(step))
                if a is L1:
                    t, half = i // 2, i % 2
                    last = tt(v_big[s][:, t, 512 * half:512 * half + 512], bank[:, :],
                              b1_v[:, 512 * half:512 * half + 512], ALU.add)
                else:
                    for t in range(2):
                        last = tt(va[s][:, t, 0:8, 0:16], bank[:, t * 128:(t + 1) * 128].rearrange("p (h d) -> p h d", h=8),
                                  bf_v[:, :].rearrange("p (h d) -> p h d", h=8), ALU.add)
                last.then_inc(v.free(step), 1)
            elif kind == "S":
                qtile, h0, n, keys = a.s_chunks()[step[3]]
                dve.wait_ge(*v.filled(step))
                nc.vector.tensor_reduce(peak[s][:, qtile, h0:h0 + n],
                                        v.bank(step)[:, 0:n * keys].rearrange("p (h k) -> p h k", h=n),
                                        axis=AX.X, op=ALU.max).then_inc(v.free(step), 1)
            elif kind == "D":
                fill = ("P", a, s, 0) if a.big else ("X", a, s, 0)
                rows = 128 if a.big else 32 * a.units
                dve.wait_ge(*v.filled(fill))
                nc.vector.reciprocal(rsum[s][0:rows, :], v.bank(fill)[0:rows, 0:256]).then_inc(v.free(fill), 1)
            elif kind == "B":
                i = step[3]
                dve.wait_ge(*v.filled(step))
                if a.big:
                    dve.wait_ge(*v.drained(("P", a, s, a.groups - 1)))
                unit = o_unit(a, s, 2 * i, 2)
                tt(unit, unit, v.bank(step)[:, :].rearrange("p (c t) -> p c t", c=2), ALU.mult).then_inc(
                    v.free(step), 1)
            elif kind == "W":
                dve.wait_ge(*v.filled(step))
                dve.wait_ge(y.res_ready[s], v.attn(a))
                tt(summed[s][:, :, :], v.bank(step)[:, 0:256].rearrange("p (t d) -> p t d", t=2), x_res[s][:, :, :],
                   ALU.add).then_inc(v.free(step), 1)
                dve.wait_ge(*v.drained(step))
                if a is L1F:
                    tt(summed[s][:, :, :], summed[s][:, :, :], x_tok[s][:, :, :], ALU.add).then_inc(y.twice[s], 1)
                    dve.wait_ge(y.twice[s], v.once())
                layer_norm_sums(dve, v, s, a, summed[s])
            elif kind == "L":
                if a is L0X:
                    dve.wait_ge(y.out_done[s], v.it * 16 + 1)
                    layer_norm_apply(dve, v, s, a, summed[s], xs[s][:, :, 0:D])
                elif a is L1F:
                    dve.wait_ge(y.out_done[s], v.it * 16 + 1)
                    layer_norm_apply(dve, v, s, a, summed[s], x_out[s])
                else:
                    layer_norm_apply(dve, v, s, a, summed[s], x_tok[s])
            elif kind == "LN":
                dve.wait_ge(y.x_ready[s], v.ln(L1X))
                layer_norm_sums(dve, v, s, "LN", x_tok[s])
                layer_norm_apply(dve, v, s, "LN", x_tok[s], summed[s])
            elif kind == "R1":
                link = [0]

                def linked(ins):
                    link[0] += 1
                    ins.then_inc(y.r_link[s], 1)
                    dve.wait_ge(y.r_link[s], v.it * 7 + link[0])
                    carry_wait(dve)

                c = r_col[s]
                dve.wait_ge(*v.filled(step))
                linked(nc.vector.tensor_reduce(c[:, 4:6], v.bank(step)[:, 0:2 * E].rearrange("p (t e) -> p t e", t=2),
                                               axis=AX.X, op=ALU.max))
                nc.vector.tensor_scalar(c[:, 0:2], c[:, 4:6], -1.0, None, ALU.mult).then_inc(y.r_neg[s], 1)
                dve.wait_ge(*v.drained(step))
                linked(nc.vector.reciprocal(c[:, 4:6], c[:, 2:4]))
                for t in range(2):
                    last = nc.vector.tensor_scalar(xs[s][:, t, D:XW], r_exp[s][:, t, :], c[:, 4 + t:5 + t], None,
                                                   ALU.mult)
                linked(last)
                linked(tt(r_sel[s][:, :, 0:E], xs[s][:, :, D:XW], gate_b[:, :].unsqueeze(1).to_broadcast([128, 2, E]),
                          ALU.add))
                for t in range(2):
                    last = nc.vector.max(r_top[s][:, t, :], r_sel[s][:, t, 0:E])
                linked(last)
                linked(nc.vector.memset(r_top[s][:, :, TOPK:8], BIG))
                for t in range(2):
                    last = nc.vector.match_replace(r_rep[s][:, t, :], r_top[s][:, t, :], r_sel[s][:, t, :], -BIG)
                linked(last)
                tt(r_mask[s][:, :, :], r_rep[s][:, :, 0:E], r_sel[s][:, :, 0:E], ALU.not_equal).then_inc(y.r_masked[s], 1)
            elif kind == "R3":
                dve.wait_ge(*v.filled(step))
                dve.wait_ge(y.key_done[s], v.it * 16 + 1)
                if s == 0:
                    dve.wait_ge(y.tk_link, v.it * 2 + 1)
                else:
                    dve.wait_ge(y.tk_link, v.it * 2 + 2)
                tt(r_key[s], v.bank(step)[0:E, 0:256], token_key, ALU.add).then_inc(v.free(step), 1)
                dve.wait_ge(*v.drained(step))
                tt(r_key[s], r_key[s], r_maskt[s][:, :], ALU.mult).then_inc(y.r_keyed[s], 1)
                nc.vector.tensor_scalar(token_key, token_key, -8.0 * T, None, ALU.add).then_inc(y.tk_link, 1)
            elif kind == "F1":
                h1 = v.bank(step, 0)[0:FI, :].rearrange("p (c t) -> p c t", c=2)
                h3 = v.bank(step, 1)[0:FI, :].rearrange("p (c t) -> p c t", c=2)
                dve.wait_ge(y.h_exp[s], v.once())
                nc.vector.tensor_scalar(hid_e[s], hid_e[s], 1.0, None, ALU.add).then_inc(y.h_link[s], 1)
                dve.wait_ge(y.h_link[s], v.it * 2 + 1)
                nc.vector.reciprocal(hid[s], hid_e[s]).then_inc(y.h_link[s], 1)
                dve.wait_ge(y.h_link[s], v.it * 2 + 2)
                tt(hid[s], hid[s], h1, ALU.mult).then_inc(v.free(step, 0), 1)
                dve.wait_ge(*v.drained(step, 0))
                dve.wait_ge(*v.filled(step, 1))
                tt(hid[s], hid[s], h3, ALU.mult).then_inc(v.free(step, 1), 1)
                dve.wait_ge(y.x_in[s], v.it * 32 + 32)
                nc.vector.tensor_reduce(x_res[s][:, :, :], routed[s].rearrange("p t k d -> p t d k"), axis=AX.X,
                                        op=ALU.add).then_inc(y.z_sum[s], 1)
                dve.wait_ge(y.z_sum[s], v.once())
            elif kind == "F2":
                dve.wait_ge(*v.filled(step))
                tt(summed[s][:, :, :], v.bank(step)[:, 0:256].rearrange("p (t d) -> p t d", t=2), x_res[s][:, :, :],
                   ALU.add).then_inc(v.free(step), 1)
                dve.wait_ge(*v.drained(step))
                tt(summed[s][:, :, :], summed[s][:, :, :], x3_in[s][:, :, :], ALU.add).then_inc(y.x_used[s], 1)
                dve.wait_ge(y.x_used[s], v.once())
                layer_norm_sums(dve, v, s, "F", summed[s])

        def pool_step(pool, v, step):
            kind, a, s = step[0], step[1], step[2]
            y = v.y
            if kind in ("W", "F2", "LN"):
                which = {"W": a, "F2": "F", "LN": "LN"}[kind]
                pool.wait_ge(y.moments_ready[s], v.ln(which))
                nc.gpsimd.tensor_tensor(rstd[s][:, :], moments[s][:, :, 1], powers[:, 0:2], ALU.add).then_inc(
                    y.eps_added[s], 1)
                pool.wait_ge(y.eps_added[s], v.ln(which))
                nc.gpsimd.tensor_tensor(rstd[s][:, :], rstd[s][:, :], powers[:, 2:4], ALU.pow).then_inc(
                    y.rstd_ready[s], 1)
            if (kind == "Q" and step[3] == 0 and a is not L1F) or kind == "LN":
                if a is L0:
                    pool.wait_ge(y.x_in[s], v.it * 48 + 48)
                else:
                    pool.wait_ge(y.x_ready[s], v.ln(L1X if a is L1F else previous_x(a)))
                src = x_in[s] if a is L0 else x_tok[s][:, :, :]
                bias = {L0: b0_o, L0X: bx_o, L1: b1_o, L1X: b1x_o}.get(a)
                bias = bf_o[:, :, :] if bias is None else bias[:, :].unsqueeze(1).to_broadcast([128, 2, D])
                nc.gpsimd.tensor_tensor(x_res[s][:, :, :], src, bias, ALU.add).then_inc(y.res_ready[s], 1)


        NB = 8
        ROUNDS = CAP // 8
        keys_a = kt[0][:, :, :].rearrange("p a b -> p (a b)")
        keys_b = kt[1][:, :, :].rearrange("p a b -> p (a b)")
        lists = xt[0][:, 0:CAP]
        both = summed[0][0:E, 0, :]
        both_b = summed[1][0:E, 0, :]
        final = xt[1][0:E, 0:CAP]
        slot_key = sb("slot_key", [128, 32], I32)
        slot_hi = sb("slot_hi", [128, 32], I32)
        slot_lo = sb("slot_lo", [128, 32], I32)
        x_row = sb("x_row", [128, 32], I32)
        z_row = sb("z_row", [128, 32], I32)
        x_idx = sb("x_idx", [128, 2 * NB], I32)
        z_idx = sb("z_idx", [128, 2 * NB], I32)
        f32_of = lambda t, n: t.rearrange("p a b -> p (a b)")[:, 0:n]
        e_x = f32_of(prob[:, :, :], 16 * XW).rearrange("p (n w) -> p n w", w=XW)
        e_y = qt[0][:, :, :].rearrange("p a (b d) -> p (a b) d", d=D)
        e_w1 = [f32_of(v_big[p][:, :, :], 16 * FI).rearrange("p (n i) -> p n i", i=FI) for p in AB]
        e_w3 = [f32_of(qt[1][:, :, :], 16 * FI).rearrange("p (n i) -> p n i", i=FI),
                kb[:, :, :].rearrange("p a b -> p (a b)").bitcast(FP32)[:, 0:16 * FI].rearrange(
                    "p (n i) -> p n i", i=FI)]
        e_w2 = [kt[p][0:FI, :, :].rearrange("p a (b d) -> p (a b) d", d=D) for p in AB]
        e_xt = [kx[p][:, :, :].rearrange("p a b -> p (a b)") for p in AB]
        e_h = [vx[p][0:FI, :, :].rearrange("p a b -> p (a b)") for p in AB]

        keys_loaded = sem("keys_loaded")
        half_lists = sem("half_lists")
        half_moved = sem("half_moved")
        final_ready = sem("final_ready")
        slots_full = sem("slots_full")
        rows_ready = sem("rows_ready")
        w13_in = [sem(f"w13_in{p}") for p in AB]
        w2_in = [sem(f"w2_in{p}") for p in AB]
        idx_copied = sem("idx_copied")
        gathered = [sem(f"gathered{p}") for p in AB]
        e_xt_full = [sem(f"e_xt_full{p}") for p in AB]
        e_xt_ready = [sem(f"e_xt_ready{p}") for p in AB]
        e_h_full = [sem(f"e_h_full{p}") for p in AB]
        e_exp = [sem(f"e_exp{p}") for p in AB]
        e_link = sem("e_link")
        e_h_ready = [sem(f"e_h_ready{p}") for p in AB]
        e_y_full = [sem(f"e_y_full{p}") for p in AB]
        e_y_ready = [sem(f"e_y_ready{p}") for p in AB]
        scattered = [sem(f"scattered{p}") for p in AB]
        outputs_free = sem("outputs_free")
        e_started = sem("e_started")
        p3_ready = sem("p3_ready")
        E_ITERS = 32 // (2 * NB)

        def experts_tensor(pe):
            pe.wait_ge(final_ready, 1)
            for u in range(2):
                last = nc.tensor.matmul(psum[0][64 * u:64 * u + 64, 0:32], final, ident[0:E, u:E:2],
                                        start=True, stop=True)
            last.then_inc(slots_full, 1)
            with pe.Fori(0, E_ITERS) as it:
                for p in AB:
                    pe.wait_ge(gathered[p], it * 16 * NB + 16 * NB)
                    for n in range(NB):
                        last = nc.tensor.matmul(psum[p][:, (n % 4) * 128:(n % 4) * 128 + 128],
                                                e_x[:, NB * p + n, 0:D], ident[:, :], start=True, stop=True)
                        if n % 4 == 3:
                            last.then_inc(e_xt_full[p], 1)
                            if n < NB - 1:
                                pe.wait_ge(e_xt_ready[p], it * 2 + 1)
                for p in AB:
                    pe.wait_ge(e_xt_ready[p], it * 2 + 2)
                    pe.wait_ge(w13_in[p], it * 32 + 32)
                    for n in range(NB):
                        bank = psum[2 + n // 2]
                        if n % 2 == 0 and p == 1:
                            pe.wait_ge(e_h_ready[0], it * 4 + (n // 2 + 1))
                        for u in range(2):
                            xt_u = e_xt[p][:, n * 128 + 64 * u:n * 128 + 64 * u + 64]
                            for k, w in enumerate((e_w1[p], e_w3[p])):
                                c = 256 * k + (n % 2) * 128 + 64 * u
                                last = nc.tensor.matmul(bank[0:FI, c:c + 64], w[:, 2 * n + u, :], xt_u,
                                                        start=True, stop=True)
                        if n % 2 == 1:
                            last.then_inc(e_h_full[p], 1)
                for p in AB:
                    pe.wait_ge(w2_in[p], it * 16 + 16)
                    for n in range(NB):
                        bank = psum[6 + n // 4]
                        if n % 2 == 0:
                            pe.wait_ge(e_h_ready[p], it * 4 + (n // 2 + 1))
                        if n % 4 == 0 and p == 1:
                            pe.wait_ge(e_y_ready[0], it * 2 + (n // 4 + 1))
                        for u in range(2):
                            c = n * 128 + 64 * u
                            last = nc.tensor.matmul(bank[64 * u:64 * u + 64, (n % 4) * 128:(n % 4) * 128 + 128],
                                                    e_h[p][:, c:c + 64], e_w2[p][:, 2 * n + u, :],
                                                    start=True, stop=True)
                        if n % 4 == 3:
                            last.then_inc(e_y_full[p], 1)

        def experts_scalar(act):
            with act.Fori(0, E_ITERS) as it:
                for p in AB:
                    for q in range(2):
                        act.wait_ge(e_xt_full[p], it * 2 + (q + 1))
                        nc.scalar.copy(e_xt[p][:, 512 * q:512 * q + 512], psum[p][:, :]).then_inc(e_xt_ready[p], 1)
                for p in AB:
                    for q in range(NB // 2):
                        act.wait_ge(e_h_full[p], it * 4 + (q + 1))
                        nc.scalar.activation(e_h[p][:, 256 * q:256 * q + 256], psum[2 + q][0:FI, 0:256], ACT.Exp,
                                             scale=-1.0).then_inc(e_exp[p], 1)

        def experts_vector(dve):
            def linked(ins, count=[0]):
                count[0] += 1
                ins.then_inc(chain, 1)
                dve.wait_ge(chain, count[0])

            dve.wait_ge(keys_loaded, 32)
            cur, nxt = keys_a, keys_b
            for r in range(ROUNDS):
                top = lists[:, 8 * r:8 * r + 8]
                linked(nc.vector.max(top, cur))
                if r < ROUNDS - 1:
                    linked(nc.vector.match_replace(nxt, top, cur, 0.0))
                    cur, nxt = nxt, cur
            nc.vector.tensor_copy(both[:, 0:CAP], lists[0:E, :]).then_inc(half_lists, 1)
            dve.wait_ge(half_lists, 1)
            dve.wait_ge(half_moved, 16)
            cur, nxt = both, both_b
            for r in range(ROUNDS):
                top = final[:, 8 * r:8 * r + 8]
                linked(nc.vector.max(top, cur))
                if r < ROUNDS - 1:
                    linked(nc.vector.match_replace(nxt, top, cur, 0.0))
                    cur, nxt = nxt, cur
            dve.sem_inc(final_ready, 1)
            dve.wait_ge(slots_full, 1)
            ts = nc.vector.tensor_scalar
            linked(nc.vector.tensor_copy(slot_key[:, :], psum[0][:, 0:32]))
            ts(slot_hi[:, :], slot_key[:, :], 3, None, ALU.arith_shift_right)
            linked(ts(slot_lo[:, :], slot_key[:, :], 7, None, ALU.bitwise_and))
            linked(ts(slot_key[:, :], slot_hi[:, :], -1.0, float(TOK), ALU.mult, ALU.add))
            ts(x_row[:, :], slot_key[:, :], float(TOK - 1), None, ALU.min)
            linked(ts(slot_key[:, :], slot_key[:, :], float(TOPK), None, ALU.mult))
            nc.vector.tensor_tensor(z_row[:, :], slot_key[:, :], slot_lo[:, :], ALU.add).then_inc(rows_ready, 1)
            dve.sem_inc(e_started, 1)

            with dve.Fori(0, E_ITERS) as it:
                for p in AB:
                    for q in range(NB // 2):
                        h = e_h[p][:, 256 * q:256 * q + 256]
                        n = it * 24 + (12 * p + 3 * q)
                        dve.wait_ge(e_exp[p], it * 4 + (q + 1))
                        ts(h, h, 1.0, None, ALU.add).then_inc(e_link, 1)
                        dve.wait_ge(e_link, n + 1)
                        nc.vector.reciprocal(h, h).then_inc(e_link, 1)
                        dve.wait_ge(e_link, n + 2)
                        nc.vector.tensor_tensor(h, h, psum[2 + q][0:FI, 0:256], ALU.mult).then_inc(e_link, 1)
                        dve.wait_ge(e_link, n + 3)
                        nc.vector.tensor_tensor(h, h, psum[2 + q][0:FI, 256:512], ALU.mult).then_inc(e_h_ready[p], 1)
                for p in AB:
                    if p == 0:
                        dve.wait_ge(outputs_free, it + 1)
                    for n in range(NB):
                        if n % 4 == 0:
                            dve.wait_ge(e_y_full[p], it * 2 + (n // 4 + 1))
                        for u in range(2):
                            rows = slice(64 * u, 64 * u + 64)
                            score = e_x[rows, NB * p + n, bass.ds(it * 32 + (D + 2 * (NB * p + n) + u), 1)]
                            last = nc.vector.tensor_tensor(e_y[rows, NB * p + n, :],
                                                           psum[6 + n // 4][rows, (n % 4) * 128:(n % 4) * 128 + 128],
                                                           score.to_broadcast([64, D]), ALU.mult)
                        if n % 4 == 3:
                            last.then_inc(e_y_ready[p], 1)

        def experts_pool(pool):
            pool.wait_ge(rows_ready, 1)
            pool.wait_ge(zeroed, 24 * 16)
            with pool.Fori(0, E_ITERS) as it:
                nc.gpsimd.tensor_copy(x_idx[:, :], x_row[:, bass.ds(it * 2 * NB, 2 * NB)])
                nc.gpsimd.tensor_copy(z_idx[:, :], z_row[:, bass.ds(it * 2 * NB, 2 * NB)]).then_inc(idx_copied, 1)
                pool.wait_ge(idx_copied, it + 1)
                carry_wait(pool)
                for p in AB:
                    for n in range(NB * p, NB * p + NB):
                        pool.indirect_dma_start(
                            out=e_x[:, n, :], out_offset=None, in_=xg[:, :],
                            in_offset=bass.IndirectOffsetOnAxis(ap=x_idx[:, n:n + 1].bitcast(U32), axis=0),
                        ).then_inc(gathered[p], 16)
                for p in AB:
                    for n in range(NB * p, NB * p + NB):
                        if n % 4 == 0:
                            pool.wait_ge(e_y_ready[p], it * 2 + ((n % NB) // 4 + 1))
                            carry_wait(pool)
                        pool.indirect_dma_start(
                            out=zd[:, :], out_offset=bass.IndirectOffsetOnAxis(ap=z_idx[:, n:n + 1].bitcast(U32), axis=0),
                            in_=e_y[:, n, :], in_offset=None, bounds_check=TOK * TOPK - 1, oob_is_err=False,
                        ).then_inc(scattered[p], 16)
                for p in AB:
                    pool.wait_ge(scattered[p], it * 16 * NB + 16 * NB)
                carry_wait(pool)
                pool.sem_inc(outputs_free, 1)

        def experts_transfers(sp):
            sp.wait_ge(p1.out_done[0], ITERS * 16 + 1)
            sp.wait_ge(p1.out_done[1], ITERS * 16 + 1)
            sp.wait_ge(p1.key_done[0], ITERS * 16 + 1)
            sp.wait_ge(p1.key_done[1], ITERS * 16 + 1)
            for half in range(2):
                sp.dma_start(keys_a[64 * half:64 * half + 64, :],
                             keyd[:, half * TOK // 2:(half + 1) * TOK // 2]).then_inc(keys_loaded, 16)
            w = lambda name, first: inp[name][:, bass.ds(first, 16), :]

            def load_w13(it, p):
                sp.dma_start(e_w1[p], w("w1T", it * 32 + 16 * p)).then_inc(w13_in[p], 16)
                sp.dma_start(e_w3[p], w("w3T", it * 32 + 16 * p)).then_inc(w13_in[p], 16)

            for p in AB:
                load_w13(0, p)
            sp.wait_ge(half_lists, 1)
            sp.dma_start(both[:, CAP:2 * CAP], lists[E:128, :]).then_inc(half_moved, 16)
            sp.wait_ge(e_started, 1)
            for p in AB:
                sp.dma_start(e_w2[p], w("w2T", 16 * p)).then_inc(w2_in[p], 16)
            for it in range(1, E_ITERS):
                for p in AB:
                    sp.wait_ge(e_h_full[p], it * 4)
                    load_w13(it, p)
                for p in AB:
                    sp.wait_ge(e_y_full[p], it * 2)
                    sp.dma_start(e_w2[p], w("w2T", it * 32 + 16 * p)).then_inc(w2_in[p], 16)

        loads1 = [(w0_qkv[:, :], "L0_Wqkv"), (b0_o[:, :], "L0_bout")]
        loads1 += [(w0_o[32 * j:32 * j + 8, :, :], ("L0_Wout", j)) for j in range(4)]
        loads1 += [(wx_q[:, :], "L0_Wq"), (wx_kv[:, 0:128], "L0_Wk"), (wx_kv[:, 128:256], "L0_Wv"),
                   (bx_o[:, :], "L0_bo"), (gate_w[:, :], "gate_w"), (gate_b[:, :], "gate_b"),
                   (token_key, "token_key")]
        loads1 += [(wx_o[32 * j:32 * j + 16, :, :], ("L0_Wo", j)) for j in range(4)]
        loads3 = [(ws13[:, :, :], "ws13"), (ws2[:, :, :], "ws2"), (w1_qkv[:, :], "L1_Wqkv"), (b1_qk[:, :], "b1_qk"),
                  (b1_v[:, :], "b1_v"), (w1_o[:, :, :], "L1_Wout"), (b1_o[:, :], "L1_bout"), (w1x_q[:, :], "L1_Wq"),
                  (w1x_k[:, :], "L1_Wk"), (w1x_v[:, :], "L1_Wv"), (w1x_o[:, :, :], "L1_Wo"), (b1x_o[:, :], "L1_bo"),
                  (wf_qkv[:, 0:128], "q_w"), (wf_qkv[:, 128:256], "k_w"), (wf_qkv[:, 256:384], "v_w"),
                  (bf_cols[:, :], "bf_cols"), (bf_v[:, :], "v_b")]
        consts = [(ident[:, :], "ident"), (tri, "tri"), (head_mask[:, :], "head_mask"),
                  (ones_g[:, :, :], "ones_g"), (ones_u[:, :, :, :], "ones_u"), (pick_sum[:, :], "pick_sum"),
                  (spread_s[:, :, :], "spread_s"), (spread_b[:, :, :], "spread_b"), (upper[:, :], "upper")]
        consts_in = sem("consts_in")
        weights1_in = sem("weights1_in")
        zero_filled = sem("zero_filled")
        cleared = sem("cleared")

        def dram(name):
            if isinstance(name, tuple):
                w, j = name
                d = 8 if w == "L0_Wout" else 16
                return inp[w].rearrange("(u j d) o -> j d u o", j=4, d=d)[j]
            if name in ("L1_Wout", "L1_Wo"):
                return inp[name].rearrange("(c p) o -> p c o", p=128)
            return inp[name]

        block = ctx.enter_context(nc.Block())

        @block.sync
        def _(sp):
            for s in AB:
                for sems in (p1.out_done, p1.key_done, p3.out_done):
                    sp.sem_inc(sems[s], 1)
            sp.sem_inc(outputs_free, 1)

            def load1(seq, s):
                row = lambda name: inp[name][bass.ds(seq, 1), :, :]
                sp.dma_start(x_in[s], row("x").rearrange("o (t p) d -> p (o t) d", p=128)).then_inc(p1.x_in[s], 16)
                sp.dma_start(xt_in[s], row("xT").rearrange("o d t -> d (o t)")).then_inc(p1.x_in[s], 16)
                sp.dma_start(ctx_t[s][:, :, :], row("ctxT2").rearrange("o d (a k) -> d (o a) k", a=2)).then_inc(
                    p1.x_in[s], 16)

            def store1(v, s):
                seq = v.it * 2 + s
                sp.wait_ge(p1.r_masked[s], v.once())
                sp.dma_start(xg[bass.ds(seq * T, T), :].rearrange("(t p) w -> p t w", p=128), xs[s]).then_inc(
                    p1.out_done[s], 16)
                sp.wait_ge(p1.r_keyed[s], v.once())
                carry_wait(sp)
                sp.dma_start(keyd[:, bass.ds(seq * T, T)], r_key[s]).then_inc(p1.key_done[s], 16)

            for dst, name in consts:
                sp.dma_start(dst, dram(name)).then_inc(consts_in, 16)
            for s in AB:
                load1(s, s)
            sp.wait_ge(cleared, 1)
            for dst, name in loads1:
                sp.dma_start(dst, dram(name)).then_inc(weights1_in, 16)
            for dst, name in loads3:
                sp.dma_start(dst, dram(name)).then_inc(weights_in, 16)
            for e, m in NESTED:
                for h in range(max(1, m // 16)):
                    u, j = h // 4, h % 4
                    sp.dma_start(wf_o[32 * j:32 * j + 16, e + (e > 0) + u, 0:m], inp["o_w"][16 * h:16 * h + 16, 0:m]).then_inc(
                        weights_in, 16)
                p = 64 * (e % 2)
                sp.dma_start(bf_o[p:p + 64, e // 2, 0:m], inp["o_b"][p:p + 64, 0:m]).then_inc(weights_in, 16)
            sp.wait_ge(zero_filled, 1)
            zrows = zd.rearrange("(n p r) d -> n p (r d)", p=128, r=8)
            for n in range(24):
                sp.dma_start(zrows[n], zeros).then_inc(zeroed, 16)
            with sp.Fori(0, ITERS - 1) as it:
                v = View("p1", it)
                for s in AB:
                    sp.wait_ge(p1.x_ready[s], v.ln(L0X))
                    load1(it * 2 + (2 + s), s)
                    store1(v, s)
            for s in AB:
                store1(View("p1", ITERS - 1), s)

            experts_transfers(sp)
            for p in AB:
                sp.wait_ge(scattered[p], E_ITERS * 16 * NB)

            def load3(seq, s):
                sp.dma_start(x3_in[s][:, :, :], xg[bass.ds(seq * T, T), 0:D].rearrange(
                    "(t p) w -> p t w", p=128)).then_inc(p3.x_in[s], 16)
                sp.dma_start(routed[s].rearrange("p t k d -> p t (k d)"), zd[bass.ds(seq * T * TOPK, T * TOPK), :].rearrange(
                    "(t p k) d -> p t (k d)", p=128, k=TOPK)).then_inc(p3.x_in[s], 16)

            def load3_context(seq, s):
                sp.dma_start(ctx_t[s][:, :, :], inp["ctxT2"][bass.ds(seq, 1), :, :].rearrange(
                    "o d (a k) -> d (o a) k", a=2)).then_inc(p3.ctx_in[s], 16)

            def store3(v, s):
                sp.wait_ge(p3.x_ready[s], v.ln(L1F))
                sp.dma_start(out[bass.ds(v.it * 2 + s, 1), :, :].rearrange("o (t p) d -> p (o t) d", p=128),
                             x_out[s][:, :, :]).then_inc(p3.out_done[s], 16)

            for s in AB:
                load3(s, s)
                load3_context(s, s)
            with sp.Fori(0, ITERS - 1) as it:
                v = View("p3", it)
                for s in AB:
                    sp.wait_ge(p3.x_used[s], v.once())
                    load3(it * 2 + (2 + s), s)
                for s in AB:
                    sp.wait_ge(*v.drained(("V", L1X, s, 1)))
                    load3_context(it * 2 + (2 + s), s)
                for s in AB:
                    store3(v, s)
            for s in AB:
                store3(View("p3", ITERS - 1), s)
            for s in AB:
                sp.wait_ge(p3.out_done[s], ITERS * 16 + 1)

        N3 = len(loads3) + sum(max(1, m // 16) + 1 for _, m in NESTED)

        @block.tensor
        def _(pe):
            pe.wait_ge(consts_ready, 1)
            pe.wait_ge(weights1_in, 16 * len(loads1))
            with pe.Fori(0, ITERS) as it:
                v = View("p1", it)
                for step in plan["p1"]:
                    tensor_step(pe, v, step)
            experts_tensor(pe)
            pe.wait_ge(p3_ready, 1)
            with pe.Fori(0, ITERS) as it:
                v = View("p3", it)
                for step in plan["p3"]:
                    tensor_step(pe, v, step)

        @block.scalar
        def _(act):
            act.wait_ge(consts_ready, 1)
            with act.Fori(0, ITERS) as it:
                v = View("p1", it)
                for step in plan["p1"]:
                    scalar_step(act, v, step)
            experts_scalar(act)
            act.wait_ge(p3_ready, 1)
            with act.Fori(0, ITERS) as it:
                v = View("p3", it)
                for step in plan["p3"]:
                    scalar_step(act, v, step)

        @block.vector
        def _(dve):
            for y in (p1, p3):
                for b in range(8):
                    dve.sem_inc(y.free[b], 1)
            dve.sem_inc(p1.tk_link, 1)
            ms, cp, ts = nc.vector.memset, nc.vector.tensor_copy, nc.vector.tensor_scalar
            for t in (w0_o[:, :, :], wx_o[:, :, :], wf_o[:, :, :]):
                ms(t, 0.0)
            ms(bf_o[:, :, :], 0.0).then_inc(cleared, 1)
            ms(zeros, 0.0).then_inc(zero_filled, 1)
            for s in AB:
                ms(va[s][:, :, :, :], 1.0)
                ms(r_sel[s][:, :, :], BIG)
                for u in range(2):
                    mine = va_x[s][64 * u:64 * u + 64, :, :].rearrange("p (c u) d -> p c u d", u=2)
                    ms(mine[:, :, 1 - u, :], 0.0)
                    ms(mine[:, :, u, :], 1.0)
            ms(mask_s[:, 0:128], 0.0)
            ms(mask_s[:, 256:384], -250.0)
            ms(mask_t[:, 0:128], -250.0)
            ms(mask_t[:, 256:384], 0.0)
            dve.wait_ge(consts_in, 16 * len(consts))
            ts(mask_s[:, 128:256], tri[:, 0:128], -250.0, None, ALU.mult)
            ts(mask_t[:, 128:256], tri[:, 128:256], -250.0, None, ALU.mult)
            cp(ident_b[:, :], ident[:, :])
            cp(upper_b[:, :], upper[:, :])
            ts(neg_ident[:, :], ident[:, :], -1.0, None, ALU.mult)
            ts(ident_inf[:, :], ident[:, :], 1.0e28, None, ALU.mult)
            ts(ident_add[:, :], ident[:, :], 320.0, None, ALU.mult)
            cp(sel_h[:, :, :], ident[0:16, 0:16].unsqueeze(2).to_broadcast([16, 16, 128])).then_inc(consts_ready, 1)
            dve.wait_ge(weights1_in, 16 * len(loads1))
            with dve.Fori(0, ITERS) as it:
                v = View("p1", it)
                for step in plan["p1"]:
                    vector_step(dve, v, step)
            experts_vector(dve)
            for s in AB:
                dve.wait_ge(e_y_ready[s], 2 * E_ITERS)
                ms(kx[s][:, :, :], 0.0)
                ms(vx[s][:, :, :], 0.0)
            dve.wait_ge(weights_in, 16 * N3)
            ms(kb[:, :, :], 0.0).then_inc(p3_ready, 1)
            with dve.Fori(0, ITERS) as it:
                v = View("p3", it)
                for step in plan["p3"]:
                    vector_step(dve, v, step)

        @block.gpsimd
        def _(pool):
            nc.gpsimd.memset(powers[:, 0:2], EPS)
            nc.gpsimd.memset(powers[:, 2:4], -0.5)
            pool.wait_ge(weights1_in, 16 * len(loads1))
            with pool.Fori(0, ITERS) as it:
                v = View("p1", it)
                for step in plan["p1"]:
                    pool_step(pool, v, step)
            experts_pool(pool)
            pool.wait_ge(p3_ready, 1)
            with pool.Fori(0, ITERS) as it:
                v = View("p3", it)
                for step in plan["p3"]:
                    pool_step(pool, v, step)


def constants():
    c = {}
    p = np.arange(128)
    c["ident"] = np.eye(128, dtype=np.float32)
    tri = (p[None, :] > p[:, None]).astype(np.float32)
    c["tri"] = np.concatenate([tri, tri.T], 1)
    c["head_mask"] = np.concatenate([p[:, None] // 8 == np.arange(16)[None], p[:, None] // 16 == np.arange(8)[None]],
                                    1).astype(np.float32)
    r = np.arange(32)
    g = (r[None, :] % 4 == np.arange(4)[:, None]).astype(np.float32)
    c["ones_g"] = np.broadcast_to(g, (128, 4, 32)).copy()
    c["ones_u"] = (p[:, None, None, None] // 64 == np.arange(2)[None, :, None, None]) * g[None, None].astype(np.float32)
    c["pick_sum"] = (p[:, None] == 32 * (r[None] % 4) + 31).astype(np.float32)
    u = np.arange(4)
    c["spread_s"] = (p[:, None, None] == 32 * u[None, :, None] + p[None, None, :] // 32).astype(np.float32)
    h = 2 * np.arange(8)[:, None] + p[None, :] // 64
    c["spread_b"] = (p[:, None, None] == (32 * (h % 4) + h // 4)[None]).astype(np.float32)
    e = np.arange(E)
    c["upper"] = (e[:, None] < e[None, :]).astype(np.float32)
    c["token_key"] = np.broadcast_to((8.0 * (TOK - np.arange(T))).astype(np.float32), (E, T)).copy()
    return {k: np.ascontiguousarray(a, dtype=np.float32) for k, a in c.items()}


def laid_out(i):
    rows = lambda a: np.broadcast_to(a, (128, a.shape[0]))
    ctx_t = i["ctx_768"].transpose(0, 2, 1)
    return {
        "x": i["x"], "xT": i["x"].transpose(0, 2, 1), "ctxT2": np.concatenate([ctx_t, ctx_t], 2),
        "L0_Wqkv": i["L0_attn_Wqkv"].T, "L0_Wout": i["L0_attn_Wout"].T, "L0_bout": rows(i["L0_attn_bout"]),
        "L0_Wq": i["L0_xattn_Wq"], "L0_Wk": i["L0_xattn_Wk"], "L0_Wv": i["L0_xattn_Wv"],
        "L0_Wo": i["L0_xattn_Wo"], "L0_bo": rows(i["L0_xattn_bo"]),
        "gate_w": i["L0_ffn_gate_w"].T, "gate_b": rows(i["L0_ffn_gate_b"]),
        "w1T": i["L0_ffn_w1"].transpose(2, 0, 1), "w3T": i["L0_ffn_w3"].transpose(2, 0, 1),
        "w2T": i["L0_ffn_w2"].transpose(2, 0, 1),
        "ws13": np.concatenate([i["L0_ffn_ws1"].T.reshape(D, 2, FI), i["L0_ffn_ws3"].T.reshape(D, 2, FI)], 1),
        "ws2": i["L0_ffn_ws2"].T.reshape(2, FI, D).transpose(1, 0, 2),
        "L1_Wqkv": i["L1_attn_W_qkv"], "b1_qk": i["L1_attn_b_qkv"][:2048].reshape(16, 128).T,
        "b1_v": rows(i["L1_attn_b_qkv"][2048:]), "L1_Wout": i["L1_attn_W_out"], "L1_bout": rows(i["L1_attn_b_out"]),
        "L1_Wq": i["L1_xattn_Wq"], "L1_Wk": i["L1_xattn_Wk"], "L1_Wv": i["L1_xattn_Wv"],
        "L1_Wo": i["L1_xattn_Wo"], "L1_bo": rows(i["L1_xattn_bo"]),
        "q_w": i["L1_ffn_q_w"].T, "k_w": i["L1_ffn_k_w"].T, "v_w": i["L1_ffn_v_w"].T,
        "bf_cols": np.stack([i["L1_ffn_norm_w"], i["L1_ffn_norm_b"], i["L1_ffn_q_b"], i["L1_ffn_k_b"]], 1),
        "v_b": rows(i["L1_ffn_v_b"]), "o_w": i["L1_ffn_o_w"].T, "o_b": rows(i["L1_ffn_o_b"]),
    }


def kernel(**inputs):
    import concourse.bacc as _bacc
    from concourse.bass_utils import run_bass_kernel_spmd as _run

    nc = _bacc.Bacc("TRN2", target_bir_lowering=False, num_devices=1)
    given = {k: np.asarray(a) for k, a in inputs.items()}
    arrays, args = {}, {}
    for name, a in {**laid_out(given), **constants()}.items():
        a = np.ascontiguousarray(a)
        arrays[f"in_{name}"] = a
        args[name] = nc.dram_tensor(f"in_{name}", a.shape, mybir.dt.from_np(a.dtype), kind="ExternalInput").ap()
    out = nc.dram_tensor("out", (SEQS, T, D), FP32, kind="ExternalOutput").ap()
    decoder_program(nc, args, out)
    r = _run(nc, [arrays], core_ids=[0])
    return r.results[0]["out"]
```

```python
import numpy as np
import concourse.bass as bass
from concourse import mybir
from contextlib import ExitStack

FP32 = mybir.dt.float32
BF16 = mybir.dt.bfloat16
I32 = mybir.dt.int32
U32 = mybir.dt.uint32
ALU = mybir.AluOpType
ACT = mybir.ActivationFunctionType
AX = mybir.AxisListType

SEQS, T, D = 16, 256, 128
TOK = SEQS * T
CTX, DC = 64, 96
E, TOPK, CAP = 64, 6, 64
FI = 88
EPS = 1e-5
XW = D + E
BIG = 3.0e38
AB = (0, 1)
ITERS = SEQS // 2


class Attn:

    def __init__(self, name, heads, dh, ctx=False, causal=None, scale=None):
        self.name, self.heads, self.dh, self.ctx, self.causal = name, heads, dh, ctx, causal
        self.scale = scale
        self.big = dh == 64
        self.groups = heads // 4
        self.units = heads // 2 if self.big else heads // 4
        self.keys = CTX if ctx else T
        self.quads = 0 if self.big or ctx else self.groups

    def s_chunks(self):
        out = []
        for qt in range(2):
            keys = self.keys
            if self.causal == "inf" and qt == 0:
                keys = 128
            n = 512 // keys
            out += [(qt, h, n, keys) for h in range(0, self.heads, n)]
        return sorted(out, key=lambda c: c[1] // 4) if self.quads else out

    def t_chunks(self):
        if self.ctx:
            return [(0, (0, 1, 2, 3), 256)]
        if self.causal == "inf":
            return [(0, (0, 1), 256), (0, (2, 3), 256), (1, (0, 1, 2, 3), 128)]
        halves = ((0, 2), (1, 3)) if self.big else ((0, 1), (2, 3))
        return [(k, heads, 256) for k in range(2) for heads in halves]

    def place(self, ktile, j):
        if self.ctx:
            return 0, (j // 2) * 256, 0
        for i, (k, heads, queries) in enumerate(self.t_chunks()):
            if k == ktile and j in heads:
                return i, heads.index(j) * queries, T - queries


L0 = Attn("L0", 16, 8, causal="inf", scale=8.0 ** -0.5)
L0X = Attn("L0X", 8, 16, ctx=True, scale=0.25)
L1 = Attn("L1", 16, 64, causal="add", scale=0.125)
L1X = Attn("L1X", 16, 64, ctx=True, scale=0.125)
L1F = Attn("L1F", 8, 16, scale=float(D) ** -0.5)
NESTED = [(e, D >> e) for e in range(4)]


def project_steps(a, s):
    out = [("Q", a, s, i) for i in range(4 if a.big else 1)]
    if a is L1:
        out += [("K", a, s, i) for i in range(4)]
    elif a is L1X:
        out += [("K", a, s, 0)]
    out += [("C", a, s, 0)]
    nv = {L1: 4, L1X: 2}.get(a, 1)
    out += [("V", a, s, i) for i in range(nv)]
    if a.quads:
        per = len(a.s_chunks()) // a.quads
        for g in range(a.quads):
            out += [("C", a, s, g + 1)] if g + 1 < a.quads else []
            out += [("S", a, s, i) for i in range(g * per, (g + 1) * per)] + [("H", a, s, g)]
    else:
        out += [("S", a, s, i) for i in range(len(a.s_chunks()))]
    return out + [("N", a, s, 0)]


def head_steps(a, s):
    out = []
    for g in range(a.groups):
        out += [("T", a, s, g, i) for i in range(len(a.t_chunks()))]
        if g:
            out.append(("P", a, s, g - 1))
    return out + [("P", a, s, a.groups - 1)]


def tail_steps(a, s):
    out = [] if a.big else [("X", a, s, 0)]
    out += [("D", a, s, 0)] + [("B", a, s, i) for i in range(a.units // 2)]
    return out + [("W", a, s, 0), ("L", a, s, 0)]


def phase1_streams():
    main = lambda s: (project_steps(L0, s) + head_steps(L0, s) + tail_steps(L0, s) + [("XT", L0X, s, 0)]
                      + project_steps(L0X, s) + head_steps(L0X, s) + tail_steps(L0X, s))
    router = lambda s: [("XT", "R", s, 0)] + [(k, "R", s, 0) for k in ("R1", "RN", "R2", "R3")]
    return [main(s) for s in AB] + [router(s) for s in AB]


def phase3_streams():
    main = lambda s: ([("XT", "F", s, 0), ("Z", "F", s, 0), ("F1", "F", s, 0), ("F2", "F", s, 0), ("L", "F", s, 0),
                       ("XT", L1, s, 0)] + project_steps(L1, s) + head_steps(L1, s) + tail_steps(L1, s)
                      + [("XT", L1X, s, 0)] + project_steps(L1X, s) + head_steps(L1X, s) + tail_steps(L1X, s)
                      + [("LN", L1F, s, 0), ("XT", L1F, s, 0)] + project_steps(L1F, s) + head_steps(L1F, s)
                      + tail_steps(L1F, s))
    return [main(s) for s in AB]


TURNS1 = ("A B A C A2 C A2 B C A C A4 C B A5 B2 A2 B A4 B A2 B A B A2 B D B D B A B4 A D B2 A D B3 D A B2 A "
          "B3 A B4 A B2 A B A4 B A2 B2 A2 B A B2 A5 B2 A2 B A B9 A2 B2 A B A2 B A B2 A B2 A B2 A")
TURNS3 = ("A B A2 B3 A B2 A B A B A8 B A3 B A4 B A2 B A12 B A3 B A B A B3 A B A4 B A2 B A B A B8 A B7 A B6 "
          "A B2 A B2 A B2 A B2 A B A B2 A2 B A2 B A B2 A2 B A5 B A3 B A2 B A2 B A B10 A3 B2 A B2 A B A2 B2 "
          "A B A B3 A4 B A B3 A2 B4 A B A B A2 B A3 B A3 B A2 B A3 B A B3 A3 B2 A B2 A B A2 B A B A2 B A2 "
          "B3 A B3 A B8 A")
B_AHEAD1, B_AHEAD3 = 51, 108


def interleaved(streams, turns, b_ahead):
    at = [0, b_ahead] + [0] * (len(streams) - 2)
    n_ahead = [len(streams[0]), b_ahead] + [0] * (len(streams) - 2)
    out = []
    for turn in turns.split():
        k = "ABCD".index(turn[0])
        for _ in range(int(turn[1:] or 1)):
            out.append((streams[k][at[k]], 1 if at[k] < n_ahead[k] else 0))
            at[k] = (at[k] + 1) % len(streams[k])
    assert sorted(map(str, out)) == sorted(str(x) for st, n in zip(streams, n_ahead) for x in
                                           [(step, 1 if i < n else 0) for i, step in enumerate(st)])
    return out


BANKS = {"S": (0, 1), "T": (2, 3), "O": (4,), "D": (5,), "M": (6, 7)}


def fills(step):
    kind, a = step[0], step[1]
    if kind == "P":
        g = step[3]
        if g == 0 and a.big:
            return ["D", "O"]
        if a.big or g % 2 == 0:
            return ["O"]
        return []
    if kind == "F1":
        return ["M", "M"]
    if kind in ("D", "L", "C", "H", "LN", "RN", "Z"):
        return []
    return [{"S": "S", "T": "T", "X": "D"}.get(kind, "M")]


class Ledger:

    def __init__(self, steps):
        self.use, self.per, self.ahead = {}, [0] * 8, dict(steps)
        turn = {k: 0 for k in BANKS}
        for step, _ in steps:
            for i, kind in enumerate(fills(step)):
                ring = BANKS[kind]
                b = ring[turn[kind] % len(ring)]
                turn[kind] += 1
                self.use[step, i] = (b, self.per[b])
                self.per[b] += 1


def decoder_program(nc, inp, out):
    ctx = ExitStack()
    with ctx:
        def sb(name, shape, dt=FP32):
            return ctx.enter_context(nc.sbuf_tensor(name, shape, dt))

        def sem(name):
            return ctx.enter_context(nc.semaphore(name))

        def pair(name, shape, dt=FP32):
            return [sb(f"{name}{s}", shape, dt) for s in AB]

        xg = nc.dram_tensor("xg", [TOK, XW], FP32, kind="Internal").ap()
        keyd = nc.dram_tensor("keyd", [E, TOK], FP32, kind="Internal").ap()
        zd = nc.dram_tensor("zd", [TOK * TOPK, D], FP32, kind="Internal").ap()

        ident = sb("ident", [128, 128])
        ident_b = sb("ident_b", [128, 128], BF16)
        neg_ident = sb("neg_ident", [128, 128], BF16)
        ident_inf = sb("ident_inf", [128, 128], BF16)
        ident_add = sb("ident_add", [128, 128], BF16)
        mask_s = sb("mask_s", [128, 256], BF16)
        mask_t = sb("mask_t", [128, 128], BF16)
        sel_h = sb("sel_h", [128, 16, 128], BF16)
        sel_flat = sel_h[:, :, :].rearrange("i h k -> i (h k)")
        head_mask = sb("head_mask", [128, 24])
        ones_g = sb("ones_g", [128, 4, 32])
        ones_u = sb("ones_u", [128, 2, 4, 32])
        pick_sum = sb("pick_sum", [128, 32])
        spread_s = sb("spread_s", [128, 4, 128], BF16)
        spread_b = sb("spread_b", [128, 8, 128], BF16)
        part_cols = sb("part_cols", [128, 2])
        upper = sb("upper", [64, 64])
        upper_b = sb("upper_b", [64, 64], BF16)

        w0_qkv = sb("w0_qkv", [128, 384])
        w0_o = sb("w0_o", [128, 4, 128])
        b0_o = sb("b0_o", [128, 128])
        wx_q = sb("wx_q", [128, 128])
        wx_kv = sb("wx_kv", [DC, 256])
        wx_o = sb("wx_o", [128, 2, 128])
        bx_o = sb("bx_o", [128, 128])
        gate_w = sb("gate_w", [128, E])
        gate_b = sb("gate_b", [128, E])
        ws13 = sb("ws13", [128, 4, FI])
        ws2 = sb("ws2", [FI, 2, 128])
        w1_qkv = sb("w1_qkv", [128, 3072])
        b1_qk = sb("b1_qk", [128, 16])
        b1_v = sb("b1_v", [128, 1024])
        w1_o = sb("w1_o", [128, 8, 128])
        b1_o = sb("b1_o", [128, 128])
        w1x_q = sb("w1x_q", [128, 1024])
        w1x_k = sb("w1x_k", [DC, 1024])
        w1x_v = sb("w1x_v", [DC, 1024])
        w1x_o = sb("w1x_o", [128, 8, 128])
        b1x_o = sb("b1x_o", [128, 128])
        wf_qkv = sb("wf_qkv", [128, 384])
        bf_cols = sb("bf_cols", [128, 4])
        bf_v = sb("bf_v", [128, 128])
        wf_o = sb("wf_o", [128, 5, 128])
        bf_o = sb("bf_o", [128, 2, 128])

        union = pair("union", [128, 1536])
        x_in = [u[:, 0:256].rearrange("p (t d) -> p t d", t=2) for u in union]
        xt_in = [u[:, 256:512] for u in union]
        xs = [u[:, 512:512 + 2 * XW].rearrange("p (t d) -> p t d", t=2) for u in union]
        va_x = [u[:, 1024:1280].rearrange("p (h d) -> p h d", h=8) for u in union]
        routed = [u[:, :].rearrange("p (t k d) -> p t k d", t=2, k=TOPK) for u in union]
        x3_in = pair("x3_in", [128, 2, D])
        tri = x3_in[0][:, :, :].rearrange("p t d -> p (t d)")
        x_tok = pair("x_tok", [128, 2, D])
        x_res = pair("x_res", [128, 2, D])
        xt = pair("xt", [128, T])
        summed = pair("summed", [128, 2, D])
        x_out = pair("x_out", [128, 2, D])
        ctx_t = pair("ctx_t", [DC, 2, CTX])
        qt = pair("qt", [128, 8, T])
        kt = pair("kt", [128, 8, T])
        v_big = pair("v_big", [128, 2, 1024])
        kx = pair("kx", [128, 16, CTX])
        vx = pair("vx", [128, 8, 128])
        va = pair("va", [128, 2, 16, 32])
        qb = sb("qb", [128, 8, T], BF16)
        kb = sb("kb", [128, 16, T], BF16)
        kbf = sb("kbf", [128, 8, T], BF16)
        zeros = kbf[:, :, :].rearrange("p a b -> p (a b)").bitcast(FP32)
        kxb = sb("kxb", [128, 16, CTX], BF16)
        prob = sb("prob", [128, 8, 512])
        peak = pair("peak", [128, 2, 16], BF16)
        shift = pair("shift", [128, 2, T], BF16)
        rsum = pair("rsum", [128, T])
        rpart = pair("rpart", [128, T], BF16)
        stats = pair("stats", [128, 2, 6])
        moments = pair("moments", [128, 2, 2])
        powers = sb("powers", [128, 4])
        rstd = pair("rstd", [128, 2])
        hid = [t[0:FI, 0, 0:512].rearrange("p (c t) -> p c t", c=2) for t in v_big]
        hid_e = [t[0:FI, 1, 0:512].rearrange("p (c t) -> p c t", c=2) for t in v_big]
        r_exp = pair("r_exp", [128, 2, E])
        r_sel = pair("r_sel", [128, 2, E + 2])
        r_top = pair("r_top", [128, 2, 8])
        r_rep = pair("r_rep", [128, 2, E + 2])
        r_mask = pair("r_mask", [128, 2, E], BF16)
        r_maskt = pair("r_maskt", [E, T], BF16)
        r_col = pair("r_col", [128, 6])
        r_key = [t[0:E, :, :].rearrange("p t d -> p (t d)") for t in x_out]
        token_key = x3_in[1][0:E, :, :].rearrange("p t d -> p (t d)")

        kv = [v_big[s][:, :, :].rearrange("p a (b t) -> p (a b) t", t=T) for s in AB]

        def k_of(a, s, h):
            if a is L0:
                return (kt[s] if h < 8 else kv[s])[:, h % 8, :]
            if a is L1F:
                return kv[s][:, h, :]
            return kx[s][:, h, :]

        psum = [ctx.enter_context(nc.psum_tensor(f"bank{b}", [128, 512], FP32)) for b in range(8)]

        weights_in = sem("weights_in")
        consts_ready = sem("consts_ready")
        zeroed = sem("zeroed")
        passed = sem("passed")
        chain = sem("chain")

        class Sync:

            def __init__(self, tag):
                n = lambda name: [sem(f"{tag}_{name}{s}") for s in AB]
                self.full = [sem(f"{tag}_full{b}") for b in range(8)]
                self.free = [sem(f"{tag}_free{b}") for b in range(8)]
                self.x_in = n("x_in")
                self.ctx_in = n("ctx_in")
                self.x_used = n("x_used")
                self.x_ready = n("x_ready")
                self.res_ready = n("res_ready")
                self.moments_ready = n("moments_ready")
                self.stats_ready = n("stats_ready")
                self.rstd_ready = n("rstd_ready")
                self.eps_added = n("eps_added")
                self.q16 = n("q16")
                self.k_masked = n("k_masked")
                self.k16 = n("k16")
                self.r_split = n("r_split")
                self.r_parts = n("r_parts")
                self.out_done = n("out_done")
                if tag == "p1":
                    self.r_neg = n("r_neg")
                    self.r_link = n("r_link")
                    self.r_masked = n("r_masked")
                    self.r_keyed = n("r_keyed")
                    self.key_done = n("key_done")
                    self.tk_link = sem(f"{tag}_tk_link")
                else:
                    self.twice = n("twice")
                    self.h_exp = n("h_exp")
                    self.h_link = n("h_link")
                    self.z_sum = n("z_sum")

        p1, p3 = Sync("p1"), Sync("p3")

        LNS = {("p1", L0): 0, ("p1", L0X): 1,
               ("p3", "F"): 0, ("p3", L1): 1, ("p3", L1X): 2, ("p3", "LN"): 3, ("p3", L1F): 4}
        LN_PER = {"p1": 2, "p3": 5}
        ATTN = {("p1", L0): 0, ("p1", L0X): 1, ("p3", L1): 0, ("p3", L1X): 1, ("p3", L1F): 2}
        ATTN_PER = {"p1": 2, "p3": 3}

        plan = {"p1": interleaved(phase1_streams(), TURNS1, B_AHEAD1),
                "p3": interleaved(phase3_streams(), TURNS3, B_AHEAD3)}

        def carry_wait(eng):
            eng.sem_inc(passed, 1)

        ledger = {tag: Ledger(steps) for tag, steps in plan.items()}
        sync = {"p1": p1, "p3": p3}

        class View:

            def __init__(self, tag, it, later=0):
                self.tag, self.it, self.later, self.y = tag, it, later, sync[tag]

            def at(self, per, n):
                return self.it * per + (self.later * per + n)

            def bank_at(self, step, i, extra):
                b, n = ledger[self.tag].use[step, i]
                per = ledger[self.tag].per[b]
                return self.it * per + ((self.later + 1 - ledger[self.tag].ahead[step]) * per + n + extra)

            def may_fill(self, step, i=0):
                return self.free(step, i), self.bank_at(step, i, 1)

            def filled(self, step, i=0):
                return self.full(step, i), self.bank_at(step, i, 1)

            def drained(self, step, i=0):
                return self.free(step, i), self.bank_at(step, i, 2)

            def bank(self, step, i=0):
                return psum[ledger[self.tag].use[step, i][0]]

            def full(self, step, i=0):
                return self.y.full[ledger[self.tag].use[step, i][0]]

            def free(self, step, i=0):
                return self.y.free[ledger[self.tag].use[step, i][0]]

            def ln(self, which):
                return self.at(LN_PER[self.tag], LNS[self.tag, which] + 1)

            def attn(self, a):
                return self.at(ATTN_PER[self.tag], ATTN[self.tag, a] + 1)

            def k16(self, a, quad):
                return self.at({"p1": 5, "p3": 4}[self.tag], {L0: 1, L0X: 5, L1: 1, L1X: 2, L1F: 3}[a] + quad)

            def masked(self, a, quad):
                return self.at({"p1": 5, "p3": 2}[self.tag], {L0: 1, L0X: 5, L1F: 1}[a] + quad)

            def once(self):
                return self.at(1, 1)

        def previous_x(a):
            return {L0X: L0, "R": L0X, L1: "F", L1X: L1, L1F: "LN"}[a]

        def x_source(tag, a, s):
            if a is L0:
                return x_in[s][:, :, :]
            if a == "F":
                return x3_in[s][:, :, :]
            if a == "R":
                return xs[s][:, :, 0:D]
            if a is L1F:
                return summed[s][:, :, :]
            return x_tok[s][:, :, :]

        def o_unit(a, s, u, n=1):
            base = {L0: 2, L0X: 2, L1F: 2}.get(a, 0)
            return qt[s][:, base + u:base + u + n, :]

        def tensor_step(pe, v, step):
            kind, a, s = step[0], step[1], step[2]
            y, mm = v.y, nc.tensor.matmul
            if kind == "XT":
                if a == "F":
                    pe.wait_ge(y.x_in[s], v.at(32, 32))
                else:
                    pe.wait_ge(y.x_ready[s], v.ln(previous_x(a)))
                pe.wait_ge(*v.may_fill(step))
                src, bank = x_source(v.tag, a, s), v.bank(step)
                for t in range(2):
                    last = mm(bank[:, t * 128:(t + 1) * 128], src[:, t, :], ident[:, :], start=True, stop=True)
                last.then_inc(v.full(step), 1)
            elif kind == "Q":
                i, bank = step[3], v.bank(step)
                x = xt_in[s] if a is L0 else xt[s][:, :]
                if a is L0:
                    pe.wait_ge(y.x_in[s], v.at(32, 32))
                elif i == 0:
                    pe.wait_ge(*v.drained(("XT", a, s, 0)))
                    if a is L0X:
                        pe.wait_ge(y.ctx_in[s], v.at(16, 16))
                pe.wait_ge(*v.may_fill(step))
                if a.big:
                    w = w1_qkv if a is L1 else w1x_q
                    for j in range(2):
                        c = 2 * i + j
                        last = mm(bank[:, j * 256:(j + 1) * 256], w[:, c * 128:(c + 1) * 128], x,
                                  start=True, stop=True)
                elif a is L0:
                    for j in range(2):
                        last = mm(bank[:, j * 256:(j + 1) * 256], w0_qkv[:, j * 128:(j + 1) * 128], x,
                                  start=True, stop=True)
                elif a is L0X:
                    mm(bank[:, 0:256], wx_q[:, :], x, start=True, stop=True)
                    last = mm(bank[:, 256:256 + CTX], wx_kv[:, 0:128], ctx_t[s][:, 0, :], start=True, stop=True)
                else:
                    for j in range(2):
                        for e, m in NESTED:
                            last = mm(bank[:, j * 256 + 64 * e:j * 256 + 64 * e + 64],
                                      wf_qkv[0:m, j * 128:(j + 1) * 128], xt[s][0:m, 64 * e:64 * e + 64],
                                      start=True, stop=True)
                last.then_inc(v.full(step), 1)
            elif kind == "K":
                i, bank = step[3], v.bank(step)
                if a is L1X:
                    pe.wait_ge(y.ctx_in[s], v.at(16, 16))
                pe.wait_ge(*v.may_fill(step))
                if a is L1:
                    for j in range(2):
                        c = 8 + 2 * i + j
                        last = mm(bank[:, j * 256:(j + 1) * 256], w1_qkv[:, c * 128:(c + 1) * 128], xt[s][:, :],
                                  start=True, stop=True)
                else:
                    for c in range(8):
                        last = mm(bank[:, c * CTX:(c + 1) * CTX], w1x_k[:, c * 128:(c + 1) * 128],
                                  ctx_t[s][:, 0, :], start=True, stop=True)
                last.then_inc(v.full(step), 1)
            elif kind == "V":
                i, bank = step[3], v.bank(step)
                pe.wait_ge(*v.may_fill(step))
                if a is L1:
                    t, half = i // 2, i % 2
                    last = mm(bank[:, :], xt[s][:, t * 128:(t + 1) * 128],
                              w1_qkv[:, 2048 + 512 * half:2560 + 512 * half], start=True, stop=True)
                elif a is L1X:
                    last = mm(bank[:, :], ctx_t[s][:, :, :], w1x_v[:, 512 * i:512 * i + 512], start=True, stop=True)
                elif a is L0:
                    for t in range(2):
                        last = mm(bank[:, t * 128:(t + 1) * 128], xt_in[s][:, t * 128:(t + 1) * 128],
                                  w0_qkv[:, 256:384], start=True, stop=True)
                elif a is L0X:
                    last = mm(bank[:, 0:128], ctx_t[s][:, :, :], wx_kv[:, 128:256], start=True, stop=True)
                else:
                    for e, m in NESTED:
                        p = 64 * (e % 2)
                        last = mm(bank[p:p + 64, (e // 2) * 128:(e // 2) * 128 + 128],
                                  xt[s][0:m, 64 * e:64 * e + 64], wf_qkv[0:m, 256:384], start=True, stop=True)
                last.then_inc(v.full(step), 1)
            elif kind == "S":
                qtile, h0, n, keys = a.s_chunks()[step[3]]
                bank = v.bank(step)
                if step[3] == 0:
                    pe.wait_ge(y.q16[s], v.attn(a))
                if step[3] == 0 or (a.quads and h0 % 4 == 0 and h0 != a.s_chunks()[step[3] - 1][1] // 4 * 4):
                    pe.wait_ge(y.k16[s], v.k16(a, h0 // 4 if a.quads else 0))
                pe.wait_ge(*v.may_fill(step))
                q0 = qtile * 128
                if a.ctx and a.big:
                    for j in range(n // 2):
                        c = h0 // 2 + j
                        last = mm(bank[:, j * 128:(j + 1) * 128], qb[:, c, q0:q0 + 128],
                                  kxb[:, 2 * c:2 * c + 2, :], start=True, stop=True)
                else:
                    k16 = (kxb if a.ctx else kbf if a is L1F else kb)[:, h0:h0 + n, 0:keys]
                    c = h0 // 2 if a.big else 0
                    last = mm(bank[:, 0:n * keys].rearrange("p (h k) -> p h k", h=n), qb[:, c, q0:q0 + 128], k16,
                              start=True, stop=not a.causal)
                    if a.causal:
                        neg = ident_inf if a.causal == "inf" else ident_add
                        c = 0 if qtile == 0 else keys - 128
                        last = mm(bank[:, :].rearrange("p (h k) -> p h k", h=n)[:, :, c:keys], neg[:, :],
                                  mask_s[:, 0:keys - c].unsqueeze(1).to_broadcast([128, n, keys - c]),
                                  start=False, stop=True)
                last.then_inc(v.full(step), 1)
            elif kind == "N":
                bank = v.bank(step)
                pe.wait_ge(*v.drained(("S", a, s, len(a.s_chunks()) - 1)))
                pe.wait_ge(*v.may_fill(step))
                for t in range(2):
                    last = mm(bank[0:a.heads, t * 128:(t + 1) * 128], peak[s][:, t, 0:a.heads], neg_ident[:, :],
                              start=True, stop=True)
                last.then_inc(v.full(step), 1)
            elif kind == "T":
                g, i = step[3], step[4]
                ktile, heads, queries = a.t_chunks()[i]
                n = len(heads)
                bank = v.bank(step)
                if g == 0 and i == 0:
                    pe.wait_ge(*v.drained(("N", a, s, 0)))
                if a.quads and i == 0:
                    pe.wait_ge(y.k_masked[s], v.masked(a, g))
                pe.wait_ge(*v.may_fill(step))
                q0 = 256 - queries
                if a.ctx:
                    for j in range(2):
                        c = 2 * g + j
                        cols = bank[:, j * 256:(j + 1) * 256]
                        pair_sel = sel_flat[:, 256 * c + CTX:256 * c + 3 * CTX]
                        mm(cols, pair_sel, shift[s][:, 0, :], start=True, stop=False)
                        q = qt[s][:, c, :] if a.big else qt[s][:, 0, :]
                        last = mm(cols, kx[s][:, 2 * c:2 * c + 2, :], q, start=False, stop=True)
                else:
                    full = 1 if a is L1 and ktile == 1 else 0
                    for j in range(n):
                        h = 4 * g + heads[j]
                        cols = bank[:, j * queries:(j + 1) * queries]
                        mm(cols, sel_h[:, h, :], shift[s][:, full, q0:256], start=True, stop=False)
                        if a.big:
                            r = 64 * (h % 2)
                            lhs = kt[s][r:r + 64, h // 2, ktile * 128:(ktile + 1) * 128]
                            rhs = qt[s][r:r + 64, h // 2, :]
                        else:
                            lhs = k_of(a, s, h)[:, ktile * 128:(ktile + 1) * 128]
                            rhs = qt[s][:, 0, q0:256]
                        last = mm(cols, lhs, rhs, start=False, stop=not a.causal)
                        if a.causal:
                            neg = ident_inf if a.causal == "inf" else ident_add
                            c = 128 * ktile - q0
                            last = mm(cols[:, c:c + 128], neg[:, :], mask_t[:, :], start=False, stop=True)
                last.then_inc(v.full(step), 1)
            elif kind == "P":
                g = step[3]
                nt = len(a.t_chunks())
                for i in range(max(0, nt - 2), nt):
                    pe.wait_ge(*v.drained(("T", a, s, g, i)))
                if g == 0:
                    if a is L1:
                        pe.wait_ge(*v.drained(("V", a, s, 3)))
                    elif a is L1X:
                        pe.wait_ge(*v.drained(("V", a, s, 1)))
                    else:
                        pe.wait_ge(*v.drained(("V", a, s, 0)))
                slot = 4 * (g % 2)

                def p_of(ktile, j):
                    i, col, q0 = a.place(ktile, j)
                    return prob[:, slot + i, col:col + T - q0], q0

                kts = 1 if a.ctx else 2
                if a.big:
                    o_fill = step, 1 if g == 0 else 0
                    pe.wait_ge(*v.may_fill(*o_fill))
                    bank = v.bank(*o_fill)
                    for j in range(2):
                        cols = bank[:, j * 256:(j + 1) * 256]
                        if a.ctx:
                            last = mm(cols, vx[s][:, 2 * g + j, :], p_of(0, 2 * j)[0], start=True, stop=True)
                        else:
                            for k in range(2):
                                for u in range(2):
                                    h = 4 * g + 2 * j + u
                                    last = mm(cols[64 * u:64 * u + 64, :], v_big[s][:, k, h * 64:(h + 1) * 64],
                                              p_of(k, 2 * j + u)[0], start=(k == 0), stop=(k == 1))
                    last.then_inc(v.full(*o_fill), 1)
                    d_fill = ("P", a, s, 0), 0
                    if g == 0:
                        pe.wait_ge(*v.may_fill(*d_fill))
                    sums = v.bank(*d_fill)
                    for k in range(kts):
                        for j in range(4):
                            lhs = ones_u[:, j % 2, g, :] if a.ctx else ones_g[:, g, :]
                            last = mm(sums[32 * j:32 * j + 32, 0:256], lhs, p_of(k, j)[0],
                                      start=(g == 0 and k == 0), stop=(g == a.groups - 1 and k == kts - 1))
                    if g == a.groups - 1:
                        last.then_inc(v.full(*d_fill), 1)
                else:
                    fill = ("P", a, s, g - g % 2), 0
                    if g % 2 == 0:
                        pe.wait_ge(*v.may_fill(*fill))
                    bank = v.bank(*fill)
                    for k in range(kts):
                        for j in range(4):
                            p, q0 = p_of(k, j)
                            h = 4 * g + j
                            lhs = va_x[s][:, h, :] if a.ctx else va[s][:, k, h, :]
                            last = mm(bank[32 * j:32 * j + 32, (g % 2) * 256 + q0:(g % 2) * 256 + 256], lhs, p,
                                      start=(k == 0), stop=(k == kts - 1))
                    if g % 2 == 1:
                        last.then_inc(v.full(*fill), 1)
            elif kind == "X":
                bank = v.bank(step)
                for u in range(0, a.units, 2):
                    pe.wait_ge(*v.drained(("P", a, s, u)))
                pe.wait_ge(*v.may_fill(step))
                for u in range(a.units):
                    last = mm(bank[32 * u:32 * u + 32, 0:256], pick_sum[:, :], o_unit(a, s, u)[:, 0, :],
                              start=True, stop=True)
                last.then_inc(v.full(step), 1)
            elif kind == "B":
                i, bank = step[3], v.bank(step)
                if i == 0:
                    pe.wait_ge(y.r_parts[s], v.attn(a))
                pe.wait_ge(*v.may_fill(step))
                rows = 128 if a.big else 32 * a.units
                for j in range(2):
                    u = 2 * i + j
                    lhs = (spread_b if a.big else spread_s)[0:rows, u, :]
                    last = mm(bank[:, j * 256:(j + 1) * 256], lhs, rpart[s][0:rows, :], start=True, stop=True)
                last.then_inc(v.full(step), 1)
            elif kind == "W":
                bank = v.bank(step)
                pe.wait_ge(*v.drained(("B", a, s, a.units // 2 - 1)))
                pe.wait_ge(*v.may_fill(step))
                if a is L1F:
                    for e, m in NESTED:
                        p = 64 * (e % 2)
                        rows = [(u, 128) for u in range(2)] if e == 0 else [(0, {1: 128, 2: 64, 3: 32}[e])]
                        for n, (u, r) in enumerate(rows):
                            last = mm(bank[p:p + 64, (e // 2) * 128:(e // 2) * 128 + 128],
                                      o_unit(a, s, u)[0:r, 0, 64 * e:64 * e + 64], wf_o[0:r, e + (e > 0) + u, :],
                                      start=(n == 0), stop=(n == len(rows) - 1))
                else:
                    w = {L0: w0_o, L0X: wx_o, L1: w1_o, L1X: w1x_o}[a]
                    for t in range(2):
                        for u in range(a.units):
                            last = mm(bank[:, t * 128:(t + 1) * 128], o_unit(a, s, u)[:, 0, t * 128:(t + 1) * 128],
                                      w[:, u, :], start=(u == 0), stop=(u == a.units - 1))
                last.then_inc(v.full(step), 1)
            elif kind == "R1":
                pe.wait_ge(*v.drained(("XT", "R", s, 0)))
                pe.wait_ge(*v.may_fill(step))
                bank = v.bank(step)
                for t in range(2):
                    last = mm(bank[:, t * E:(t + 1) * E], xt[s][:, t * 128:(t + 1) * 128], gate_w[:, :],
                              start=True, stop=True)
                last.then_inc(v.full(step), 1)
            elif kind == "R2":
                pe.wait_ge(y.r_masked[s], v.once())
                pe.wait_ge(*v.may_fill(step))
                bank = v.bank(step)
                for t in range(2):
                    last = mm(bank[0:E, t * 128:(t + 1) * 128], r_mask[s][:, t, :], ident_b[:, :],
                              start=True, stop=True)
                last.then_inc(v.full(step), 1)
            elif kind == "R3":
                pe.wait_ge(*v.drained(("R2", "R", s, 0)))
                pe.wait_ge(*v.may_fill(step))
                carry_wait(pe)
                mm(v.bank(step)[0:E, 0:256], upper_b[:, :], r_maskt[s][:, :],
                   start=True, stop=True).then_inc(v.full(step), 1)
            elif kind == "F1":
                pe.wait_ge(*v.drained(("XT", "F", s, 0)))
                for i in range(2):
                    pe.wait_ge(*v.may_fill(step, i))
                    for c in range(2):
                        last = mm(v.bank(step, i)[0:FI, c * 256:(c + 1) * 256], ws13[:, 2 * i + c, :], xt[s][:, :],
                                  start=True, stop=True)
                    last.then_inc(v.full(step, i), 1)
            elif kind == "F2":
                pe.wait_ge(*v.drained(("F1", "F", s, 0), 1))
                pe.wait_ge(*v.may_fill(step))
                for t in range(2):
                    for c in range(2):
                        last = mm(v.bank(step)[:, t * 128:(t + 1) * 128], hid[s][:, c, t * 128:(t + 1) * 128],
                                  ws2[:, c, :], start=(c == 0), stop=(c == 1))
                last.then_inc(v.full(step), 1)

        def absent_step(pe, v, step):
            for i in range(len(fills(step))):
                pe.wait_ge(*v.may_fill(step, i))
                pe.sem_inc(v.full(step, i), 1)
                pe.sem_inc(v.free(step, i), 1)

        def scalar_step(act, v, step):
            kind, a, s = step[0], step[1], step[2]
            y, copy = v.y, nc.scalar.copy
            if kind == "XT":
                act.wait_ge(*v.filled(step))
                if a is L1F:
                    nc.scalar.activation(xt[s][:, :], v.bank(step)[:, 0:256], ACT.Identity, bias=bf_cols[:, 1:2],
                                         scale=bf_cols[:, 0:1]).then_inc(v.free(step), 1)
                else:
                    copy(xt[s][:, :], v.bank(step)[:, 0:256]).then_inc(v.free(step), 1)
            elif kind == "Q":
                i, bank = step[3], v.bank(step)
                act.wait_ge(*v.filled(step))
                if a is L1:
                    for j in range(2):
                        c = 2 * i + j
                        last = nc.scalar.activation(qt[s][:, c, :], bank[:, j * 256:(j + 1) * 256], ACT.Identity,
                                                    bias=b1_qk[:, c:c + 1])
                elif a is L1X:
                    last = copy(qt[s][:, 2 * i:2 * i + 2, :], bank[:, :].rearrange("p (c t) -> p c t", c=2))
                elif a is L1F:
                    for j in range(2):
                        last = nc.scalar.activation(qt[s][:, j, :], bank[:, j * 256:(j + 1) * 256], ACT.Identity,
                                                    bias=bf_cols[:, 2 + j:3 + j])
                elif a is L0:
                    last = copy(qt[s][:, 0:2, :], bank[:, :].rearrange("p (c t) -> p c t", c=2))
                else:
                    flat = qt[s][:, :, :].rearrange("p c t -> p (c t)")
                    last = copy(flat[:, 0:256 + CTX], bank[:, 0:256 + CTX])
                last.then_inc(v.free(step), 1)
            elif kind == "C":
                if step[3]:
                    return
                last_q = ("Q", a, s, 3 if a.big else 0)
                act.wait_ge(*v.drained(last_q))
                n = 8 if a.big else 1
                copy(qb[:, 0:n, :], qt[s][:, 0:n, :]).then_inc(y.q16[s], 1)
            elif kind == "H":
                m0 = 0 if a is L0 else 16
                for h in range(4 * step[3], 4 * step[3] + 4):
                    last = nc.scalar.activation(k_of(a, s, h), qt[s][:, 1, :], ACT.Copy,
                                                scale=head_mask[:, m0 + h:m0 + h + 1])
                last.then_inc(y.k_masked[s], 1)
            elif kind == "V" and a not in (L1, L1F):
                i, bank = step[3], v.bank(step)
                act.wait_ge(*v.filled(step))
                if a is L0:
                    last = copy(va[s][:, :, :, 0:8], bank[:, 0:256].rearrange("p (t h d) -> p t h d", t=2, h=16))
                elif a is L0X:
                    for u in range(2):
                        src = bank[64 * u:64 * u + 64, 0:128].rearrange("p (c u d) -> p c u d", u=2, d=16)
                        dst = va_x[s][64 * u:64 * u + 64, :, 0:16].rearrange("p (c u) d -> p c u d", u=2)
                        last = copy(dst[:, :, u, :], src[:, :, u, :])
                else:
                    for u in range(2):
                        src = bank[64 * u:64 * u + 64, :].rearrange("p (c u d) -> p c u d", u=2, d=64)
                        last = copy(vx[s][64 * u:64 * u + 64, 4 * i:4 * i + 4, 64 * u:64 * u + 64], src[:, :, u, :])
                last.then_inc(v.free(step), 1)
            elif kind == "N":
                act.wait_ge(*v.filled(step))
                minus = v.bank(step)[0:a.heads, 0:256].unsqueeze(1).to_broadcast([a.heads, 2, T])
                copy(shift[s][0:a.heads, :, :], minus).then_inc(v.free(step), 1)
            elif kind == "T":
                g, i = step[3], step[4]
                act.wait_ge(*v.filled(step))
                nc.scalar.activation(prob[:, 4 * (g % 2) + i, :], v.bank(step)[:, :], ACT.Exp,
                                     scale=a.scale).then_inc(v.free(step), 1)
            elif kind == "P":
                g = step[3]
                if a.big:
                    fill = step, 1 if g == 0 else 0
                elif g % 2 == 1:
                    fill = ("P", a, s, g - 1), 0
                else:
                    return
                act.wait_ge(*v.filled(*fill))
                u0 = 2 * g if a.big else g - 1
                copy(o_unit(a, s, u0, 2), v.bank(*fill)[:, :].rearrange("p (c t) -> p c t", c=2)).then_inc(
                    v.free(*fill), 1)
            elif kind == "R1":
                act.wait_ge(y.r_neg[s], v.once())
                for t in range(2):
                    last = nc.scalar.activation(r_exp[s][:, t, :], v.bank(step)[:, t * E:(t + 1) * E], ACT.Exp,
                                                bias=r_col[s][:, t:t + 1], accum_out=r_col[s][:, 2 + t:3 + t])
                last.then_inc(v.free(step), 1)
            elif kind == "R2":
                act.wait_ge(*v.filled(step))
                copy(r_maskt[s][:, :], v.bank(step)[0:E, 0:256]).then_inc(v.free(step), 1)
            elif kind == "F1":
                act.wait_ge(*v.filled(step, 0))
                nc.scalar.activation(hid_e[s], v.bank(step, 0)[0:FI, :].rearrange("p (c t) -> p c t", c=2),
                                     ACT.Exp, scale=-1.0).then_inc(y.h_exp[s], 1)

        def layer_norm_sums(dve, v, s, which, src):
            y = v.y
            for t in range(2):
                last = nc.vector.bn_stats(stats[s][:, t, :], src[:, t, :])
            last.then_inc(y.stats_ready[s], 1)
            dve.wait_ge(y.stats_ready[s], v.ln(which))
            carry_wait(dve)
            for t in range(2):
                last = nc.vector.bn_aggr(moments[s][:, t, :], stats[s][:, t, :])
            last.then_inc(y.moments_ready[s], 1)

        def layer_norm_apply(dve, v, s, which, src, dst):
            y = v.y
            dve.wait_ge(y.rstd_ready[s], v.ln(which))
            for t in range(2):
                last = nc.vector.tensor_scalar(dst[:, t, :], src[:, t, :], moments[s][:, t, 0:1],
                                               rstd[s][:, t:t + 1], ALU.subtract, ALU.mult)
            last.then_inc(y.x_ready[s], 1)

        def vector_step(dve, v, step):
            kind, a, s = step[0], step[1], step[2]
            y, tt = v.y, nc.vector.tensor_tensor
            if kind == "K":
                i, bank = step[3], v.bank(step)
                dve.wait_ge(*v.filled(step))
                if a is L1:
                    bias = b1_qk[:, 8 + 2 * i:10 + 2 * i].unsqueeze(2).to_broadcast([128, 2, T])
                    last = tt(kt[s][:, 2 * i:2 * i + 2, :], bank[:, :].rearrange("p (c t) -> p c t", c=2), bias,
                              ALU.add)
                else:
                    for u in range(2):
                        dst = kx[s][64 * u:64 * u + 64, :, :].rearrange("p (c u) k -> p c u k", u=2)
                        src = bank[64 * u:64 * u + 64, :].rearrange("p (c k) -> p c k", c=8)
                        last = nc.vector.tensor_copy(dst[:, :, u, :], src)
                last.then_inc(v.free(step), 1)
            elif kind == "C":
                if a is L1:
                    dve.wait_ge(*v.drained(("K", a, s, 3)))
                    for u in range(2):
                        dst = kb[64 * u:64 * u + 64, :, :].rearrange("p (c u) k -> p c u k", u=2)
                        last = nc.vector.tensor_copy(dst[:, :, u, :], kt[s][64 * u:64 * u + 64, :, :])
                elif a is L1X:
                    dve.wait_ge(*v.drained(("K", a, s, 0)))
                    last = nc.vector.tensor_copy(kxb[:, :, :], kx[s][:, :, :])
                else:
                    dve.wait_ge(*v.drained(("Q", a, s, 0)))
                    k1 = qt[s][:, 1, 0:a.keys]
                    if a.quads:
                        m0, k16 = (0, kb) if a is L0 else (16, kbf)
                        for h in range(4 * step[3], 4 * step[3] + 4):
                            last = nc.vector.tensor_scalar(k16[:, h, :], k1, head_mask[:, m0 + h:m0 + h + 1], None,
                                                           ALU.mult)
                    else:
                        m = head_mask[:, 16:24].unsqueeze(2).to_broadcast([128, 8, CTX])
                        tt(kx[s][:, 0:8, :], k1.unsqueeze(1).to_broadcast([128, 8, CTX]), m, ALU.mult).then_inc(
                            y.k_masked[s], 1)
                        dve.wait_ge(y.k_masked[s], v.masked(a, 0))
                        last = nc.vector.tensor_copy(kxb[:, 0:8, :], kx[s][:, 0:8, :])
                last.then_inc(y.k16[s], 1)
            elif kind == "V" and a in (L1, L1F):
                i, bank = step[3], v.bank(step)
                dve.wait_ge(*v.filled(step))
                if a is L1:
                    t, half = i // 2, i % 2
                    last = tt(v_big[s][:, t, 512 * half:512 * half + 512], bank[:, :],
                              b1_v[:, 512 * half:512 * half + 512], ALU.add)
                else:
                    for t in range(2):
                        last = tt(va[s][:, t, 0:8, 0:16], bank[:, t * 128:(t + 1) * 128].rearrange("p (h d) -> p h d", h=8),
                                  bf_v[:, :].rearrange("p (h d) -> p h d", h=8), ALU.add)
                last.then_inc(v.free(step), 1)
            elif kind == "S":
                qtile, h0, n, keys = a.s_chunks()[step[3]]
                dve.wait_ge(*v.filled(step))
                nc.vector.tensor_reduce(peak[s][:, qtile, h0:h0 + n],
                                        v.bank(step)[:, 0:n * keys].rearrange("p (h k) -> p h k", h=n),
                                        axis=AX.X, op=ALU.max).then_inc(v.free(step), 1)
            elif kind == "D":
                fill = ("P", a, s, 0) if a.big else ("X", a, s, 0)
                rows = 128 if a.big else 32 * a.units
                dve.wait_ge(*v.filled(fill))
                r, part = rsum[s][0:rows, :], rpart[s][0:rows, :]
                nc.vector.reciprocal(r, v.bank(fill)[0:rows, 0:256]).then_inc(v.free(fill), 1)
                dve.wait_ge(*v.drained(fill))
                for i in range(2):
                    nc.vector.tensor_copy(part, r).then_inc(y.r_split[s], 1)
                    dve.wait_ge(y.r_split[s], v.at(3 * ATTN_PER[v.tag], 3 * ATTN[v.tag, a] + 2 * i + 1))
                    out = r if i == 0 else part
                    last = nc.vector.scalar_tensor_tensor(out, part, part_cols[0:rows, i:i + 1], r, ALU.mult, ALU.add)
                    if i == 0:
                        last.then_inc(y.r_split[s], 1)
                        dve.wait_ge(y.r_split[s], v.at(3 * ATTN_PER[v.tag], 3 * ATTN[v.tag, a] + 2))
                last.then_inc(y.r_parts[s], 1)
            elif kind == "B":
                i = step[3]
                dve.wait_ge(*v.filled(step))
                if a.big:
                    dve.wait_ge(*v.drained(("P", a, s, a.groups - 1)))
                unit = o_unit(a, s, 2 * i, 2)
                tt(unit, unit, v.bank(step)[:, :].rearrange("p (c t) -> p c t", c=2), ALU.mult).then_inc(
                    v.free(step), 1)
            elif kind == "W":
                dve.wait_ge(*v.filled(step))
                dve.wait_ge(y.res_ready[s], v.attn(a))
                tt(summed[s][:, :, :], v.bank(step)[:, 0:256].rearrange("p (t d) -> p t d", t=2), x_res[s][:, :, :],
                   ALU.add).then_inc(v.free(step), 1)
                dve.wait_ge(*v.drained(step))
                if a is L1F:
                    tt(summed[s][:, :, :], summed[s][:, :, :], x_tok[s][:, :, :], ALU.add).then_inc(y.twice[s], 1)
                    dve.wait_ge(y.twice[s], v.once())
                layer_norm_sums(dve, v, s, a, summed[s])
            elif kind == "L":
                if a is L0X:
                    dve.wait_ge(y.out_done[s], v.at(16, 1))
                    layer_norm_apply(dve, v, s, a, summed[s], xs[s][:, :, 0:D])
                elif a is L1F:
                    dve.wait_ge(y.out_done[s], v.at(16, 1))
                    layer_norm_apply(dve, v, s, a, summed[s], x_out[s])
                else:
                    layer_norm_apply(dve, v, s, a, summed[s], x_tok[s])
            elif kind == "LN":
                dve.wait_ge(y.x_ready[s], v.ln(L1X))
                layer_norm_sums(dve, v, s, "LN", x_tok[s])
                layer_norm_apply(dve, v, s, "LN", x_tok[s], summed[s])
            elif kind == "R1":
                c = r_col[s]
                dve.wait_ge(*v.filled(step))
                nc.vector.tensor_reduce(c[:, 4:6], v.bank(step)[:, 0:2 * E].rearrange("p (t e) -> p t e", t=2),
                                        axis=AX.X, op=ALU.max).then_inc(y.r_link[s], 1)
                dve.wait_ge(y.r_link[s], v.at(7, 1))
                nc.vector.tensor_scalar(c[:, 0:2], c[:, 4:6], -1.0, None, ALU.mult).then_inc(y.r_neg[s], 1)
            elif kind == "RN":
                link = [1]

                def linked(ins):
                    link[0] += 1
                    ins.then_inc(y.r_link[s], 1)
                    dve.wait_ge(y.r_link[s], v.at(7, link[0]))
                    carry_wait(dve)

                c = r_col[s]
                dve.wait_ge(*v.drained(("R1", "R", s, 0)))
                linked(nc.vector.reciprocal(c[:, 4:6], c[:, 2:4]))
                for t in range(2):
                    last = nc.vector.tensor_scalar(xs[s][:, t, D:XW], r_exp[s][:, t, :], c[:, 4 + t:5 + t], None,
                                                   ALU.mult)
                linked(last)
                linked(tt(r_sel[s][:, :, 0:E], xs[s][:, :, D:XW], gate_b[:, :].unsqueeze(1).to_broadcast([128, 2, E]),
                          ALU.add))
                for t in range(2):
                    last = nc.vector.max(r_top[s][:, t, :], r_sel[s][:, t, 0:E])
                linked(last)
                linked(nc.vector.memset(r_top[s][:, :, TOPK:8], BIG))
                for t in range(2):
                    last = nc.vector.match_replace(r_rep[s][:, t, :], r_top[s][:, t, :], r_sel[s][:, t, :], -BIG)
                linked(last)
                tt(r_mask[s][:, :, :], r_rep[s][:, :, 0:E], r_sel[s][:, :, 0:E], ALU.not_equal).then_inc(y.r_masked[s], 1)
            elif kind == "R3":
                dve.wait_ge(*v.filled(step))
                dve.wait_ge(y.key_done[s], v.at(16, 1))
                if s == 0:
                    dve.wait_ge(y.tk_link, v.at(2, 1))
                else:
                    dve.wait_ge(y.tk_link, v.at(2, 2))
                tt(r_key[s], v.bank(step)[0:E, 0:256], token_key, ALU.add).then_inc(v.free(step), 1)
                dve.wait_ge(*v.drained(step))
                tt(r_key[s], r_key[s], r_maskt[s][:, :], ALU.mult).then_inc(y.r_keyed[s], 1)
                nc.vector.tensor_scalar(token_key, token_key, -8.0 * T, None, ALU.add).then_inc(y.tk_link, 1)
            elif kind == "F1":
                h1 = v.bank(step, 0)[0:FI, :].rearrange("p (c t) -> p c t", c=2)
                h3 = v.bank(step, 1)[0:FI, :].rearrange("p (c t) -> p c t", c=2)
                dve.wait_ge(y.h_exp[s], v.once())
                nc.vector.tensor_scalar(hid_e[s], hid_e[s], 1.0, None, ALU.add).then_inc(y.h_link[s], 1)
                dve.wait_ge(y.h_link[s], v.at(2, 1))
                nc.vector.reciprocal(hid[s], hid_e[s]).then_inc(y.h_link[s], 1)
                dve.wait_ge(y.h_link[s], v.at(2, 2))
                tt(hid[s], hid[s], h1, ALU.mult).then_inc(v.free(step, 0), 1)
                dve.wait_ge(*v.drained(step, 0))
                dve.wait_ge(*v.filled(step, 1))
                tt(hid[s], hid[s], h3, ALU.mult).then_inc(v.free(step, 1), 1)
            elif kind == "Z":
                dve.wait_ge(y.x_in[s], v.at(32, 32))
                nc.vector.tensor_reduce(x_res[s][:, :, :], routed[s].rearrange("p t k d -> p t d k"), axis=AX.X,
                                        op=ALU.add).then_inc(y.z_sum[s], 1)
            elif kind == "F2":
                dve.wait_ge(*v.filled(step))
                dve.wait_ge(y.z_sum[s], v.once())
                tt(summed[s][:, :, :], v.bank(step)[:, 0:256].rearrange("p (t d) -> p t d", t=2), x_res[s][:, :, :],
                   ALU.add).then_inc(v.free(step), 1)
                dve.wait_ge(*v.drained(step))
                tt(summed[s][:, :, :], summed[s][:, :, :], x3_in[s][:, :, :], ALU.add).then_inc(y.x_used[s], 1)
                dve.wait_ge(y.x_used[s], v.once())
                layer_norm_sums(dve, v, s, "F", summed[s])

        def pool_step(pool, v, step):
            kind, a, s = step[0], step[1], step[2]
            y = v.y
            if kind in ("W", "F2", "LN"):
                which = {"W": a, "F2": "F", "LN": "LN"}[kind]
                pool.wait_ge(y.moments_ready[s], v.ln(which))
                nc.gpsimd.tensor_tensor(rstd[s][:, :], moments[s][:, :, 1], powers[:, 0:2], ALU.add).then_inc(
                    y.eps_added[s], 1)
                pool.wait_ge(y.eps_added[s], v.ln(which))
                nc.gpsimd.tensor_tensor(rstd[s][:, :], rstd[s][:, :], powers[:, 2:4], ALU.pow).then_inc(
                    y.rstd_ready[s], 1)
            if (kind == "Q" and step[3] == 0 and a is not L1F) or kind == "LN":
                if a is L0:
                    pool.wait_ge(y.x_in[s], v.at(32, 32))
                else:
                    pool.wait_ge(y.x_ready[s], v.ln(L1X if a is L1F else previous_x(a)))
                src = x_in[s] if a is L0 else x_tok[s][:, :, :]
                bias = {L0: b0_o, L0X: bx_o, L1: b1_o, L1X: b1x_o}.get(a)
                bias = bf_o[:, :, :] if bias is None else bias[:, :].unsqueeze(1).to_broadcast([128, 2, D])
                nc.gpsimd.tensor_tensor(x_res[s][:, :, :], src, bias, ALU.add).then_inc(y.res_ready[s], 1)


        NB = 8
        ROUNDS = CAP // 8
        keys_a = kt[0][:, :, :].rearrange("p a b -> p (a b)")
        keys_b = kt[1][:, :, :].rearrange("p a b -> p (a b)")
        lists = xt[0][:, 0:CAP]
        both = summed[0][0:E, 0, :]
        both_b = summed[1][0:E, 0, :]
        final = xt[1][0:E, 0:CAP]
        slot_key = sb("slot_key", [128, 32], I32)
        slot_hi = sb("slot_hi", [128, 32], I32)
        slot_lo = sb("slot_lo", [128, 32], I32)
        x_row = sb("x_row", [128, 32], I32)
        z_row = sb("z_row", [128, 32], I32)
        x_idx = sb("x_idx", [128, 2 * NB], I32)
        z_idx = sb("z_idx", [128, 2 * NB], I32)
        f32_of = lambda t, n: t.rearrange("p a b -> p (a b)")[:, 0:n]
        e_x = f32_of(prob[:, :, :], 16 * XW).rearrange("p (n w) -> p n w", w=XW)
        e_y = qt[0][:, :, :].rearrange("p a (b d) -> p (a b) d", d=D)
        e_w1 = [f32_of(v_big[p][:, :, :], 16 * FI).rearrange("p (n i) -> p n i", i=FI) for p in AB]
        e_w3 = [f32_of(qt[1][:, :, :], 16 * FI).rearrange("p (n i) -> p n i", i=FI),
                kb[:, :, :].rearrange("p a b -> p (a b)").bitcast(FP32)[:, 0:16 * FI].rearrange(
                    "p (n i) -> p n i", i=FI)]
        e_w2 = [kt[p][0:FI, :, :].rearrange("p a (b d) -> p (a b) d", d=D) for p in AB]
        e_xt = [kx[p][:, :, :].rearrange("p a b -> p (a b)") for p in AB]
        e_h = [vx[p][0:FI, :, :].rearrange("p a b -> p (a b)") for p in AB]

        keys_loaded = sem("keys_loaded")
        half_lists = sem("half_lists")
        half_moved = sem("half_moved")
        final_ready = sem("final_ready")
        slots_full = sem("slots_full")
        rows_ready = sem("rows_ready")
        w13_in = [sem(f"w13_in{p}") for p in AB]
        w2_in = [sem(f"w2_in{p}") for p in AB]
        idx_copied = sem("idx_copied")
        gathered = [sem(f"gathered{p}") for p in AB]
        e_xt_full = [sem(f"e_xt_full{p}") for p in AB]
        e_xt_ready = [sem(f"e_xt_ready{p}") for p in AB]
        e_h_full = [sem(f"e_h_full{p}") for p in AB]
        e_exp = [sem(f"e_exp{p}") for p in AB]
        e_link = sem("e_link")
        e_h_ready = [sem(f"e_h_ready{p}") for p in AB]
        e_y_full = [sem(f"e_y_full{p}") for p in AB]
        e_y_ready = [sem(f"e_y_ready{p}") for p in AB]
        scattered = [sem(f"scattered{p}") for p in AB]
        outputs_free = sem("outputs_free")
        e_started = sem("e_started")
        p3_ready = sem("p3_ready")
        E_ITERS = 32 // (2 * NB)

        def experts_tensor(pe):
            pe.wait_ge(final_ready, 1)
            for u in range(2):
                last = nc.tensor.matmul(psum[0][64 * u:64 * u + 64, 0:32], final, ident[0:E, u:E:2],
                                        start=True, stop=True)
            last.then_inc(slots_full, 1)
            with pe.Fori(0, E_ITERS) as it:
                for p in AB:
                    pe.wait_ge(gathered[p], it * 16 * NB + 16 * NB)
                    for n in range(NB):
                        last = nc.tensor.matmul(psum[p][:, (n % 4) * 128:(n % 4) * 128 + 128],
                                                e_x[:, NB * p + n, 0:D], ident[:, :], start=True, stop=True)
                        if n % 4 == 3:
                            last.then_inc(e_xt_full[p], 1)
                            if n < NB - 1:
                                pe.wait_ge(e_xt_ready[p], it * 2 + 1)
                for p in AB:
                    pe.wait_ge(e_xt_ready[p], it * 2 + 2)
                    pe.wait_ge(w13_in[p], it * 32 + 32)
                    for n in range(NB):
                        bank = psum[2 + n // 2]
                        if n % 2 == 0 and p == 1:
                            pe.wait_ge(e_h_ready[0], it * 4 + (n // 2 + 1))
                        for u in range(2):
                            xt_u = e_xt[p][:, n * 128 + 64 * u:n * 128 + 64 * u + 64]
                            for k, w in enumerate((e_w1[p], e_w3[p])):
                                c = 256 * k + (n % 2) * 128 + 64 * u
                                last = nc.tensor.matmul(bank[0:FI, c:c + 64], w[:, 2 * n + u, :], xt_u,
                                                        start=True, stop=True)
                        if n % 2 == 1:
                            last.then_inc(e_h_full[p], 1)
                for p in AB:
                    pe.wait_ge(w2_in[p], it * 16 + 16)
                    for n in range(NB):
                        bank = psum[6 + n // 4]
                        if n % 2 == 0:
                            pe.wait_ge(e_h_ready[p], it * 4 + (n // 2 + 1))
                        if n % 4 == 0 and p == 1:
                            pe.wait_ge(e_y_ready[0], it * 2 + (n // 4 + 1))
                        for u in range(2):
                            c = n * 128 + 64 * u
                            last = nc.tensor.matmul(bank[64 * u:64 * u + 64, (n % 4) * 128:(n % 4) * 128 + 128],
                                                    e_h[p][:, c:c + 64], e_w2[p][:, 2 * n + u, :],
                                                    start=True, stop=True)
                        if n % 4 == 3:
                            last.then_inc(e_y_full[p], 1)

        def experts_scalar(act):
            with act.Fori(0, E_ITERS) as it:
                for p in AB:
                    for q in range(2):
                        act.wait_ge(e_xt_full[p], it * 2 + (q + 1))
                        nc.scalar.copy(e_xt[p][:, 512 * q:512 * q + 512], psum[p][:, :]).then_inc(e_xt_ready[p], 1)
                for p in AB:
                    for q in range(NB // 2):
                        act.wait_ge(e_h_full[p], it * 4 + (q + 1))
                        nc.scalar.activation(e_h[p][:, 256 * q:256 * q + 256], psum[2 + q][0:FI, 0:256], ACT.Exp,
                                             scale=-1.0).then_inc(e_exp[p], 1)

        def experts_vector(dve):
            def linked(ins, count=[0]):
                count[0] += 1
                ins.then_inc(chain, 1)
                dve.wait_ge(chain, count[0])

            dve.wait_ge(keys_loaded, 32)
            cur, nxt = keys_a, keys_b
            for r in range(ROUNDS):
                top = lists[:, 8 * r:8 * r + 8]
                linked(nc.vector.max(top, cur))
                if r < ROUNDS - 1:
                    linked(nc.vector.match_replace(nxt, top, cur, 0.0))
                    cur, nxt = nxt, cur
            nc.vector.tensor_copy(both[:, 0:CAP], lists[0:E, :]).then_inc(half_lists, 1)
            dve.wait_ge(half_lists, 1)
            dve.wait_ge(half_moved, 16)
            cur, nxt = both, both_b
            for r in range(ROUNDS):
                top = final[:, 8 * r:8 * r + 8]
                linked(nc.vector.max(top, cur))
                if r < ROUNDS - 1:
                    linked(nc.vector.match_replace(nxt, top, cur, 0.0))
                    cur, nxt = nxt, cur
            dve.sem_inc(final_ready, 1)
            dve.wait_ge(slots_full, 1)
            ts = nc.vector.tensor_scalar
            linked(nc.vector.tensor_copy(slot_key[:, :], psum[0][:, 0:32]))
            ts(slot_hi[:, :], slot_key[:, :], 3, None, ALU.arith_shift_right)
            linked(ts(slot_lo[:, :], slot_key[:, :], 7, None, ALU.bitwise_and))
            linked(ts(slot_key[:, :], slot_hi[:, :], -1.0, float(TOK), ALU.mult, ALU.add))
            ts(x_row[:, :], slot_key[:, :], float(TOK - 1), None, ALU.min)
            linked(ts(slot_key[:, :], slot_key[:, :], float(TOPK), None, ALU.mult))
            nc.vector.tensor_tensor(z_row[:, :], slot_key[:, :], slot_lo[:, :], ALU.add).then_inc(rows_ready, 1)
            dve.sem_inc(e_started, 1)

            with dve.Fori(0, E_ITERS) as it:
                for p in AB:
                    for q in range(NB // 2):
                        h = e_h[p][:, 256 * q:256 * q + 256]
                        n = it * 24 + (12 * p + 3 * q)
                        dve.wait_ge(e_exp[p], it * 4 + (q + 1))
                        ts(h, h, 1.0, None, ALU.add).then_inc(e_link, 1)
                        dve.wait_ge(e_link, n + 1)
                        nc.vector.reciprocal(h, h).then_inc(e_link, 1)
                        dve.wait_ge(e_link, n + 2)
                        nc.vector.tensor_tensor(h, h, psum[2 + q][0:FI, 0:256], ALU.mult).then_inc(e_link, 1)
                        dve.wait_ge(e_link, n + 3)
                        nc.vector.tensor_tensor(h, h, psum[2 + q][0:FI, 256:512], ALU.mult).then_inc(e_h_ready[p], 1)
                for p in AB:
                    if p == 0:
                        dve.wait_ge(outputs_free, it + 1)
                    for n in range(NB):
                        if n % 4 == 0:
                            dve.wait_ge(e_y_full[p], it * 2 + (n // 4 + 1))
                        for u in range(2):
                            rows = slice(64 * u, 64 * u + 64)
                            score = e_x[rows, NB * p + n, bass.ds(it * 32 + (D + 2 * (NB * p + n) + u), 1)]
                            last = nc.vector.tensor_tensor(e_y[rows, NB * p + n, :],
                                                           psum[6 + n // 4][rows, (n % 4) * 128:(n % 4) * 128 + 128],
                                                           score.to_broadcast([64, D]), ALU.mult)
                        if n % 4 == 3:
                            last.then_inc(e_y_ready[p], 1)

        def experts_pool(pool):
            pool.wait_ge(rows_ready, 1)
            pool.wait_ge(zeroed, 24 * 16)
            with pool.Fori(0, E_ITERS) as it:
                nc.gpsimd.tensor_copy(x_idx[:, :], x_row[:, bass.ds(it * 2 * NB, 2 * NB)])
                nc.gpsimd.tensor_copy(z_idx[:, :], z_row[:, bass.ds(it * 2 * NB, 2 * NB)]).then_inc(idx_copied, 1)
                pool.wait_ge(idx_copied, it + 1)
                carry_wait(pool)
                for p in AB:
                    for n in range(NB * p, NB * p + NB):
                        pool.indirect_dma_start(
                            out=e_x[:, n, :], out_offset=None, in_=xg[:, :],
                            in_offset=bass.IndirectOffsetOnAxis(ap=x_idx[:, n:n + 1].bitcast(U32), axis=0),
                        ).then_inc(gathered[p], 16)
                for p in AB:
                    for n in range(NB * p, NB * p + NB):
                        if n % 4 == 0:
                            pool.wait_ge(e_y_ready[p], it * 2 + ((n % NB) // 4 + 1))
                            carry_wait(pool)
                        pool.indirect_dma_start(
                            out=zd[:, :], out_offset=bass.IndirectOffsetOnAxis(ap=z_idx[:, n:n + 1].bitcast(U32), axis=0),
                            in_=e_y[:, n, :], in_offset=None, bounds_check=TOK * TOPK - 1, oob_is_err=False,
                        ).then_inc(scattered[p], 16)
                for p in AB:
                    pool.wait_ge(scattered[p], it * 16 * NB + 16 * NB)
                carry_wait(pool)
                pool.sem_inc(outputs_free, 1)

        def experts_transfers(sp):
            sp.wait_ge(p1.out_done[0], ITERS * 16 + 1)
            sp.wait_ge(p1.out_done[1], ITERS * 16 + 1)
            sp.wait_ge(p1.key_done[0], ITERS * 16 + 1)
            sp.wait_ge(p1.key_done[1], ITERS * 16 + 1)
            for half in range(2):
                sp.dma_start(keys_a[64 * half:64 * half + 64, :],
                             keyd[:, half * TOK // 2:(half + 1) * TOK // 2]).then_inc(keys_loaded, 16)
            w = lambda name, first: inp[name][:, bass.ds(first, 16), :]

            def load_w13(it, p):
                sp.dma_start(e_w1[p], w("w1T", it * 32 + 16 * p)).then_inc(w13_in[p], 16)
                sp.dma_start(e_w3[p], w("w3T", it * 32 + 16 * p)).then_inc(w13_in[p], 16)

            for p in AB:
                load_w13(0, p)
            sp.wait_ge(half_lists, 1)
            sp.dma_start(both[:, CAP:2 * CAP], lists[E:128, :]).then_inc(half_moved, 16)
            sp.wait_ge(e_started, 1)
            for p in AB:
                sp.dma_start(e_w2[p], w("w2T", 16 * p)).then_inc(w2_in[p], 16)
            for it in range(1, E_ITERS):
                for p in AB:
                    sp.wait_ge(e_h_full[p], it * 4)
                    load_w13(it, p)
                for p in AB:
                    sp.wait_ge(e_y_full[p], it * 2)
                    sp.dma_start(e_w2[p], w("w2T", it * 32 + 16 * p)).then_inc(w2_in[p], 16)

        loads1 = [(w0_qkv[:, :], "L0_Wqkv"), (b0_o[:, :], "L0_bout")]
        loads1 += [(w0_o[32 * j:32 * j + 8, :, :], ("L0_Wout", j)) for j in range(4)]
        loads1 += [(wx_q[:, :], "L0_Wq"), (wx_kv[:, 0:128], "L0_Wk"), (wx_kv[:, 128:256], "L0_Wv"),
                   (bx_o[:, :], "L0_bo"), (gate_w[:, :], "gate_w"), (gate_b[:, :], "gate_b"),
                   (token_key, "token_key")]
        loads1 += [(wx_o[32 * j:32 * j + 16, :, :], ("L0_Wo", j)) for j in range(4)]
        loads3 = [(ws13[:, :, :], "ws13"), (ws2[:, :, :], "ws2"), (w1_qkv[:, :], "L1_Wqkv"), (b1_qk[:, :], "b1_qk"),
                  (b1_v[:, :], "b1_v"), (w1_o[:, :, :], "L1_Wout"), (b1_o[:, :], "L1_bout"), (w1x_q[:, :], "L1_Wq"),
                  (w1x_k[:, :], "L1_Wk"), (w1x_v[:, :], "L1_Wv"), (w1x_o[:, :, :], "L1_Wo"), (b1x_o[:, :], "L1_bo"),
                  (wf_qkv[:, 0:128], "q_w"), (wf_qkv[:, 128:256], "k_w"), (wf_qkv[:, 256:384], "v_w"),
                  (bf_cols[:, :], "bf_cols"), (bf_v[:, :], "v_b")]
        stage = prob[:, :, :].rearrange("p a (b c) -> p (a b) c", c=128)
        consts = [(ident[:, :], "ident"), (tri, "tri"), (head_mask[:, :], "head_mask"),
                  (ones_g[:, :, :], "ones_g"), (ones_u[:, :, :, :], "ones_u"), (pick_sum[:, :], "pick_sum"),
                  (stage[:, 0:4, :], "spread_s"), (stage[:, 4:12, :], "spread_b"), (part_cols[:, :], "part_cols"), (upper[:, :], "upper")]
        consts_in = sem("consts_in")
        weights1_in = sem("weights1_in")
        zero_filled = sem("zero_filled")
        cleared = sem("cleared")

        def dram(name):
            if isinstance(name, tuple):
                w, j = name
                d = 8 if w == "L0_Wout" else 16
                return inp[w].rearrange("(u j d) o -> j d u o", j=4, d=d)[j]
            if name in ("L1_Wout", "L1_Wo"):
                return inp[name].rearrange("(c p) o -> p c o", p=128)
            return inp[name]

        block = ctx.enter_context(nc.Block())

        @block.sync
        def _(sp):
            for s in AB:
                for sems in (p1.out_done, p1.key_done, p3.out_done):
                    sp.sem_inc(sems[s], 1)
            sp.sem_inc(outputs_free, 1)

            def load1(seq, s):
                row = lambda name: inp[name][bass.ds(seq, 1), :, :]
                sp.dma_start(x_in[s], row("x").rearrange("o (t p) d -> p (o t) d", p=128)).then_inc(p1.x_in[s], 16)
                sp.dma_start(xt_in[s], row("xT").rearrange("o d t -> d (o t)")).then_inc(p1.x_in[s], 16)

            def load_context(y, seq, s):
                sp.dma_start(ctx_t[s][:, :, :], inp["ctxT2"][bass.ds(seq, 1), :, :].rearrange(
                    "o d (a k) -> d (o a) k", a=2)).then_inc(y.ctx_in[s], 16)

            def store1(v, s):
                seq = v.it * 2 + s
                sp.wait_ge(p1.r_masked[s], v.once())
                sp.dma_start(xg[bass.ds(seq * T, T), :].rearrange("(t p) w -> p t w", p=128), xs[s]).then_inc(
                    p1.out_done[s], 16)
                sp.wait_ge(p1.r_keyed[s], v.once())
                carry_wait(sp)
                sp.dma_start(keyd[:, bass.ds(seq * T, T)], r_key[s]).then_inc(p1.key_done[s], 16)

            for dst, name in consts:
                sp.dma_start(dst, dram(name)).then_inc(consts_in, 16)
            for s in AB:
                load1(s, s)
                load_context(p1, s, s)
            sp.wait_ge(cleared, 1)
            for dst, name in loads1:
                sp.dma_start(dst, dram(name)).then_inc(weights1_in, 16)
            for dst, name in loads3:
                sp.dma_start(dst, dram(name)).then_inc(weights_in, 16)
            for e, m in NESTED:
                for h in range(max(1, m // 16)):
                    u, j = h // 4, h % 4
                    sp.dma_start(wf_o[32 * j:32 * j + 16, e + (e > 0) + u, 0:m], inp["o_w"][16 * h:16 * h + 16, 0:m]).then_inc(
                        weights_in, 16)
                p = 64 * (e % 2)
                sp.dma_start(bf_o[p:p + 64, e // 2, 0:m], inp["o_b"][p:p + 64, 0:m]).then_inc(weights_in, 16)
            sp.wait_ge(zero_filled, 1)
            zrows = zd.rearrange("(n p r) d -> n p (r d)", p=128, r=8)
            for n in range(24):
                sp.dma_start(zrows[n], zeros).then_inc(zeroed, 16)
            with sp.Fori(0, ITERS - 1) as it:
                v = View("p1", it)
                for s in AB:
                    sp.wait_ge(*v.drained(("V", L0, s, 0)))
                    sp.wait_ge(p1.res_ready[s], v.attn(L0))
                    load1(it * 2 + (2 + s), s)
                for s in AB:
                    sp.wait_ge(*v.drained(("V", L0X, s, 0)))
                    load_context(p1, it * 2 + (2 + s), s)
                for s in AB:
                    store1(v, s)
            for s in AB:
                store1(View("p1", ITERS - 1), s)

            experts_transfers(sp)
            for p in AB:
                sp.wait_ge(scattered[p], E_ITERS * 16 * NB)

            def load3(seq, s):
                sp.dma_start(x3_in[s][:, :, :], xg[bass.ds(seq * T, T), 0:D].rearrange(
                    "(t p) w -> p t w", p=128)).then_inc(p3.x_in[s], 16)
                sp.dma_start(routed[s].rearrange("p t k d -> p t (k d)"), zd[bass.ds(seq * T * TOPK, T * TOPK), :].rearrange(
                    "(t p k) d -> p t (k d)", p=128, k=TOPK)).then_inc(p3.x_in[s], 16)

            def store3(v, s):
                sp.wait_ge(p3.x_ready[s], v.ln(L1F))
                sp.dma_start(out[bass.ds(v.it * 2 + s, 1), :, :].rearrange("o (t p) d -> p (o t) d", p=128),
                             x_out[s][:, :, :]).then_inc(p3.out_done[s], 16)

            for s in AB:
                load3(s, s)
                load_context(p3, s, s)
            with sp.Fori(0, ITERS - 1) as it:
                v = View("p3", it)
                for s in AB:
                    sp.wait_ge(p3.x_used[s], v.once())
                    load3(it * 2 + (2 + s), s)
                for s in AB:
                    sp.wait_ge(*v.drained(("V", L1X, s, 1)))
                    load_context(p3, it * 2 + (2 + s), s)
                for s in AB:
                    store3(v, s)
            for s in AB:
                store3(View("p3", ITERS - 1), s)
            for s in AB:
                sp.wait_ge(p3.out_done[s], ITERS * 16 + 1)

        N3 = len(loads3) + sum(max(1, m // 16) + 1 for _, m in NESTED)

        def run_phase(eng, tag, do_step):
            def body(it, aheads):
                for step, ahead in plan[tag]:
                    if ahead in aheads:
                        do_step(eng, View(tag, it, ahead), step)
                    elif do_step is tensor_step:
                        absent_step(eng, View(tag, it, ahead), step)

            body(-1, (1,))
            with eng.Fori(0, ITERS - 1) as it:
                body(it, (0, 1))
            body(ITERS - 1, (0,))

        @block.tensor
        def _(pe):
            pe.wait_ge(consts_ready, 1)
            pe.wait_ge(weights1_in, 16 * len(loads1))
            run_phase(pe, "p1", tensor_step)
            experts_tensor(pe)
            pe.wait_ge(p3_ready, 1)
            run_phase(pe, "p3", tensor_step)

        @block.scalar
        def _(act):
            act.wait_ge(consts_ready, 1)
            run_phase(act, "p1", scalar_step)
            experts_scalar(act)
            act.wait_ge(p3_ready, 1)
            run_phase(act, "p3", scalar_step)

        @block.vector
        def _(dve):
            for y in (p1, p3):
                for b in range(8):
                    dve.sem_inc(y.free[b], 1)
            dve.sem_inc(p1.tk_link, 1)
            ms, cp, ts = nc.vector.memset, nc.vector.tensor_copy, nc.vector.tensor_scalar
            for t in (w0_o[:, :, :], wx_o[:, :, :], wf_o[:, :, :]):
                ms(t, 0.0)
            ms(sel_h[:, :, :], 0.0)
            for s in AB:
                ms(shift[s][:, :, :], 0.0)
            ms(bf_o[:, :, :], 0.0).then_inc(cleared, 1)
            ms(zeros, 0.0).then_inc(zero_filled, 1)
            for s in AB:
                ms(va[s][:, :, :, :], 1.0)
                ms(r_sel[s][:, :, :], BIG)
                for u in range(2):
                    mine = va_x[s][64 * u:64 * u + 64, :, :].rearrange("p (c u) d -> p c u d", u=2)
                    ms(mine[:, :, 1 - u, :], 0.0)
                    ms(mine[:, :, u, :], 1.0)
            ms(mask_s[:, 128:256], -250.0)
            dve.wait_ge(consts_in, 16 * len(consts))
            ts(mask_s[:, 0:128], tri[:, 0:128], -250.0, None, ALU.mult)
            ts(mask_t[:, :], tri[:, 128:256], -250.0, None, ALU.mult)
            cp(ident_b[:, :], ident[:, :])
            cp(upper_b[:, :], upper[:, :])
            cp(spread_s[:, :, :], stage[:, 0:4, :])
            cp(spread_b[:, :, :], stage[:, 4:12, :])
            ts(neg_ident[:, :], ident[:, :], -1.0, None, ALU.mult)
            ts(ident_inf[:, :], ident[:, :], 1.0e28, None, ALU.mult)
            ts(ident_add[:, :], ident[:, :], 320.0, None, ALU.mult)
            dve.wait_ge(cleared, 1)
            ms(sel_h[32:33, :, :], 320.0)
            for s in AB:
                ms(shift[s][32:33, 1, 0:128], -250.0)
            cp(sel_h[0:16, :, :], ident[0:16, 0:16].unsqueeze(2).to_broadcast([16, 16, 128])).then_inc(consts_ready, 1)
            dve.wait_ge(weights1_in, 16 * len(loads1))
            run_phase(dve, "p1", vector_step)
            experts_vector(dve)
            for s in AB:
                dve.wait_ge(e_y_ready[s], 2 * E_ITERS)
                ms(kx[s][:, :, :], 0.0)
                ms(vx[s][:, :, :], 0.0)
            dve.wait_ge(weights_in, 16 * N3)
            ms(kb[:, :, :], 0.0).then_inc(p3_ready, 1)
            run_phase(dve, "p3", vector_step)

        @block.gpsimd
        def _(pool):
            nc.gpsimd.memset(powers[:, 0:2], EPS)
            nc.gpsimd.memset(powers[:, 2:4], -0.5)
            pool.wait_ge(weights1_in, 16 * len(loads1))
            run_phase(pool, "p1", pool_step)
            experts_pool(pool)
            pool.wait_ge(p3_ready, 1)
            run_phase(pool, "p3", pool_step)


def constants():
    c = {}
    p = np.arange(128)
    c["ident"] = np.eye(128, dtype=np.float32)
    tri = (p[None, :] > p[:, None]).astype(np.float32)
    c["tri"] = np.concatenate([tri, tri.T], 1)
    c["head_mask"] = np.concatenate([p[:, None] // 8 == np.arange(16)[None], p[:, None] // 16 == np.arange(8)[None]],
                                    1).astype(np.float32)
    r = np.arange(32)
    g = (r[None, :] % 4 == np.arange(4)[:, None]).astype(np.float32)
    c["ones_g"] = np.broadcast_to(g, (128, 4, 32)).copy()
    c["ones_u"] = (p[:, None, None, None] // 64 == np.arange(2)[None, :, None, None]) * g[None, None].astype(np.float32)
    c["pick_sum"] = (p[:, None] == 32 * (r[None] % 4) + 31).astype(np.float32)
    u = np.arange(4)
    rows = np.isin(p % 32 // 4, np.arange(3))[:, None, None]
    own = lambda block, j: rows & (p[:, None, None] // 32 == block) & (p[:, None, None] % 4 == j)
    c["spread_s"] = own(u[None, :, None], p[None, None, :] // 32)
    h = 2 * np.arange(8)[:, None] + p[None, :] // 64
    c["spread_b"] = own((h % 4)[None], (h // 4)[None])
    c["part_cols"] = -1.0 * (p[:, None] % 32 // 4 >= np.array([[1, 2]]))
    e = np.arange(E)
    c["upper"] = (e[:, None] < e[None, :]).astype(np.float32)
    c["token_key"] = np.broadcast_to((8.0 * (TOK - np.arange(T))).astype(np.float32), (E, T)).copy()
    return {k: np.ascontiguousarray(a, dtype=np.float32) for k, a in c.items()}


def laid_out(i):
    rows = lambda a: np.broadcast_to(a, (128, a.shape[0]))
    ctx_t = i["ctx_768"].transpose(0, 2, 1)
    return {
        "x": i["x"], "xT": i["x"].transpose(0, 2, 1), "ctxT2": np.concatenate([ctx_t, ctx_t], 2),
        "L0_Wqkv": i["L0_attn_Wqkv"].T, "L0_Wout": i["L0_attn_Wout"].T, "L0_bout": rows(i["L0_attn_bout"]),
        "L0_Wq": i["L0_xattn_Wq"], "L0_Wk": i["L0_xattn_Wk"], "L0_Wv": i["L0_xattn_Wv"],
        "L0_Wo": i["L0_xattn_Wo"], "L0_bo": rows(i["L0_xattn_bo"]),
        "gate_w": i["L0_ffn_gate_w"].T, "gate_b": rows(i["L0_ffn_gate_b"]),
        "w1T": i["L0_ffn_w1"].transpose(2, 0, 1), "w3T": i["L0_ffn_w3"].transpose(2, 0, 1),
        "w2T": i["L0_ffn_w2"].transpose(2, 0, 1),
        "ws13": np.concatenate([i["L0_ffn_ws1"].T.reshape(D, 2, FI), i["L0_ffn_ws3"].T.reshape(D, 2, FI)], 1),
        "ws2": i["L0_ffn_ws2"].T.reshape(2, FI, D).transpose(1, 0, 2),
        "L1_Wqkv": i["L1_attn_W_qkv"], "b1_qk": i["L1_attn_b_qkv"][:2048].reshape(16, 128).T,
        "b1_v": rows(i["L1_attn_b_qkv"][2048:]), "L1_Wout": i["L1_attn_W_out"], "L1_bout": rows(i["L1_attn_b_out"]),
        "L1_Wq": i["L1_xattn_Wq"], "L1_Wk": i["L1_xattn_Wk"], "L1_Wv": i["L1_xattn_Wv"],
        "L1_Wo": i["L1_xattn_Wo"], "L1_bo": rows(i["L1_xattn_bo"]),
        "q_w": i["L1_ffn_q_w"].T, "k_w": i["L1_ffn_k_w"].T, "v_w": i["L1_ffn_v_w"].T,
        "bf_cols": np.stack([i["L1_ffn_norm_w"], i["L1_ffn_norm_b"], i["L1_ffn_q_b"], i["L1_ffn_k_b"]], 1),
        "v_b": rows(i["L1_ffn_v_b"]), "o_w": i["L1_ffn_o_w"].T, "o_b": rows(i["L1_ffn_o_b"]),
    }


def kernel(**inputs):
    import concourse.bacc as _bacc
    from concourse.bass_utils import run_bass_kernel_spmd as _run

    nc = _bacc.Bacc("TRN2", target_bir_lowering=False, num_devices=1)
    given = {k: np.asarray(a) for k, a in inputs.items()}
    arrays, args = {}, {}
    for name, a in {**laid_out(given), **constants()}.items():
        a = np.ascontiguousarray(a)
        arrays[f"in_{name}"] = a
        args[name] = nc.dram_tensor(f"in_{name}", a.shape, mybir.dt.from_np(a.dtype), kind="ExternalInput").ap()
    out = nc.dram_tensor("out", (SEQS, T, D), FP32, kind="ExternalOutput").ap()
    decoder_program(nc, args, out)
    r = _run(nc, [arrays], core_ids=[0])
    return r.results[0]["out"]
```

```python
import numpy as np
import concourse.bass as bass
from concourse import mybir
from contextlib import ExitStack

FP32 = mybir.dt.float32
BF16 = mybir.dt.bfloat16
I32 = mybir.dt.int32
U32 = mybir.dt.uint32
ALU = mybir.AluOpType
ACT = mybir.ActivationFunctionType
AX = mybir.AxisListType

SEQS, T, D = 16, 256, 128
TOK = SEQS * T
CTX, DC = 64, 96
E, TOPK, CAP = 64, 6, 64
FI = 88
EPS = 1e-5
ROUNDS = CAP // 8
XW = D + E
BIG = 3.0e38
AB = (0, 1)
ITERS = SEQS // 2


class Attn:

    def __init__(self, name, heads, dh, ctx=False, causal=None, scale=None):
        self.name, self.heads, self.dh, self.ctx, self.causal = name, heads, dh, ctx, causal
        self.scale = scale
        self.big = dh == 64
        self.groups = heads // 4
        self.units = heads // 2 if self.big else heads // 4
        self.keys = CTX if ctx else T
        self.quads = 0 if self.big or ctx else self.groups

    def s_chunks(self):
        out = []
        for qt in range(2):
            keys = self.keys
            if self.causal == "inf" and qt == 0:
                keys = 128
            n = 512 // keys
            out += [(qt, h, n, keys) for h in range(0, self.heads, n)]
        return sorted(out, key=lambda c: c[1] // 4) if self.quads else out

    def t_chunks(self):
        if self.ctx:
            return [(0, (0, 1, 2, 3), 256)]
        if self.causal == "inf":
            return [(0, (0, 1), 256), (0, (2, 3), 256), (1, (0, 1, 2, 3), 128)]
        halves = ((0, 2), (1, 3)) if self.big else ((0, 1), (2, 3))
        return [(k, heads, 256) for k in range(2) for heads in halves]

    def place(self, ktile, j):
        if self.ctx:
            return 0, (j // 2) * 256, 0
        for i, (k, heads, queries) in enumerate(self.t_chunks()):
            if k == ktile and j in heads:
                return i, heads.index(j) * queries, T - queries


L0 = Attn("L0", 16, 8, causal="inf", scale=8.0 ** -0.5)
L0X = Attn("L0X", 8, 16, ctx=True, scale=0.25)
L1 = Attn("L1", 16, 64, causal="add", scale=0.125)
L1X = Attn("L1X", 16, 64, ctx=True, scale=0.125)
L1F = Attn("L1F", 8, 16, scale=float(D) ** -0.5)
NESTED = [(e, D >> e) for e in range(4)]


def project_steps(a, s):
    out = [("Q", a, s, i) for i in range(4 if a.big else 1)]
    if a is L1:
        out += [("K", a, s, i) for i in range(4)]
    elif a is L1X:
        out += [("K", a, s, 0)]
    out += [("C", a, s, 0)]
    nv = {L1: 4, L1X: 2}.get(a, 1)
    out += [("V", a, s, i) for i in range(nv)]
    if a.quads:
        per = len(a.s_chunks()) // a.quads
        for g in range(a.quads):
            out += [("C", a, s, g + 1)] if g + 1 < a.quads else []
            out += [("S", a, s, i) for i in range(g * per, (g + 1) * per)] + [("H", a, s, g)]
    else:
        out += [("S", a, s, i) for i in range(len(a.s_chunks()))]
    return out + [("N", a, s, 0)]


def head_steps(a, s):
    out = []
    for g in range(a.groups):
        out += [("T", a, s, g, i) for i in range(len(a.t_chunks()))]
        if g:
            out.append(("P", a, s, g - 1))
    return out + [("P", a, s, a.groups - 1)]


def tail_steps(a, s):
    out = [] if a.big else [("X", a, s, 0)]
    out += [("D", a, s, 0)] + [("B", a, s, i) for i in range(a.units // 2)]
    return out + [("W", a, s, 0), ("L", a, s, 0)]


def phase1_streams():
    main = lambda s: (project_steps(L0, s) + head_steps(L0, s) + tail_steps(L0, s) + [("XT", L0X, s, 0)]
                      + project_steps(L0X, s) + head_steps(L0X, s) + tail_steps(L0X, s))
    router = lambda s: ([("XT", "R", s, 0)] + [(k, "R", s, 0) for k in ("R1", "RN", "R2", "R3")]
                        + ([("RL", "R", s, i) for i in range(4)] if s == 1 else []))
    return [main(s) for s in AB] + [router(s) for s in AB]


def phase3_streams():
    main = lambda s: ([("XT", "F", s, 0), ("Z", "F", s, 0), ("F1", "F", s, 0), ("F2", "F", s, 0), ("L", "F", s, 0),
                       ("XT", L1, s, 0)] + project_steps(L1, s) + head_steps(L1, s) + tail_steps(L1, s)
                      + [("XT", L1X, s, 0)] + project_steps(L1X, s) + head_steps(L1X, s) + tail_steps(L1X, s)
                      + [("LN", L1F, s, 0), ("XT", L1F, s, 0)] + project_steps(L1F, s) + head_steps(L1F, s)
                      + tail_steps(L1F, s))
    return [main(s) for s in AB]


TURNS1 = ("A B2 A2 B2 C A2 B A C B A B A4 B A5 B A2 B A4 B A3 C B A2 B A C A B2 C A D B3 A B2 A B2 D A B3 A "
          "B2 A B3 A B3 A B3 A B D A B A2 D B D B2 A2 B A B D B3 A2 D B A D B2 A2 B A2 B A D B2 A B2 A3 B2 "
          "A2 B A B A B2 A")
TURNS3 = ("A B A2 B6 A B2 A B A B A2 B A B A5 B A7 B A14 B2 A B2 A5 B A2 B A B A B11 A2 B4 A B2 A B2 A B2 A "
          "B2 A B2 A B2 A B2 A B A2 B3 A2 B A2 B A B2 A B A B A5 B A3 B A2 B A2 B A B8 A3 B2 A B2 A B A2 B2 "
          "A B A B3 A B A B5 A2 B2 A B2 A2 B2 A B A B A3 B A2 B A8 B A B A2 B2 A B2 A B A3 B2 A3 B A2 B3 A "
          "B3 A B8 A")
B_AHEAD1, B_AHEAD3 = 47, 108


def interleaved(streams, turns, b_ahead):
    at = [0, b_ahead] + [0] * (len(streams) - 2)
    n_ahead = [len(streams[0]), b_ahead] + [0] * (len(streams) - 2)
    out = []
    for turn in turns.split():
        k = "ABCD".index(turn[0])
        for _ in range(int(turn[1:] or 1)):
            out.append((streams[k][at[k]], 1 if at[k] < n_ahead[k] else 0))
            at[k] = (at[k] + 1) % len(streams[k])
    assert sorted(map(str, out)) == sorted(str(x) for st, n in zip(streams, n_ahead) for x in
                                           [(step, 1 if i < n else 0) for i, step in enumerate(st)])
    return out


BANKS = {"S": (0, 1), "T": (2, 3), "O": (4,), "D": (5,), "M": (6, 7)}


def fills(step):
    kind, a = step[0], step[1]
    if kind == "P":
        g = step[3]
        if g == 0 and a.big:
            return ["D", "O"]
        if a.big or g % 2 == 0:
            return ["O"]
        return []
    if kind == "F1":
        return ["M", "M"]
    if kind in ("D", "L", "C", "H", "LN", "RN", "RL", "Z"):
        return []
    return [{"S": "S", "T": "T", "X": "D"}.get(kind, "M")]


class Ledger:

    def __init__(self, steps):
        self.use, self.per, self.ahead = {}, [0] * 8, dict(steps)
        turn = {k: 0 for k in BANKS}
        for step, _ in steps:
            for i, kind in enumerate(fills(step)):
                ring = BANKS[kind]
                b = ring[turn[kind] % len(ring)]
                turn[kind] += 1
                self.use[step, i] = (b, self.per[b])
                self.per[b] += 1


def decoder_program(nc, inp, out):
    ctx = ExitStack()
    with ctx:
        def sb(name, shape, dt=FP32):
            return ctx.enter_context(nc.sbuf_tensor(name, shape, dt))

        def sem(name):
            return ctx.enter_context(nc.semaphore(name))

        def pair(name, shape, dt=FP32):
            return [sb(f"{name}{s}", shape, dt) for s in AB]

        xg = nc.dram_tensor("xg", [TOK, XW], FP32, kind="Internal").ap()
        zd = nc.dram_tensor("zd", [TOK * TOPK, D], FP32, kind="Internal").ap()

        ident = sb("ident", [128, 128])
        ident_b = sb("ident_b", [128, 128], BF16)
        neg_ident = sb("neg_ident", [128, 128], BF16)
        ident_inf = sb("ident_inf", [128, 128], BF16)
        ident_add = sb("ident_add", [128, 128], BF16)
        mask_s = sb("mask_s", [128, 256], BF16)
        mask_t = sb("mask_t", [128, 128], BF16)
        sel_h = sb("sel_h", [128, 16, 128], BF16)
        sel_flat = sel_h[:, :, :].rearrange("i h k -> i (h k)")
        head_mask = sb("head_mask", [128, 24])
        ones_g = sb("ones_g", [128, 2, 4, 32])
        ones_u = sb("ones_u", [128, 2, 4, 32])
        pick_sum = sb("pick_sum", [128, 3, 32])
        spread_s = sb("spread_s", [128, 4, 128], BF16)
        spread_b = sb("spread_b", [128, 8, 128], BF16)
        part_cols = sb("part_cols", [128, 2])
        upper = sb("upper", [128, 64])
        upper_b = sb("upper_b", [128, 64], BF16)

        w0_qkv = sb("w0_qkv", [128, 384])
        w0_o = sb("w0_o", [128, 4, 128])
        b0_o = sb("b0_o", [128, 128])
        wx_q = sb("wx_q", [128, 128])
        wx_kv = sb("wx_kv", [DC, 256])
        wx_o = sb("wx_o", [128, 2, 128])
        bx_o = sb("bx_o", [128, 128])
        gate_w = sb("gate_w", [128, E])
        gate_b = sb("gate_b", [128, E])
        ws13 = sb("ws13", [128, 4, FI])
        ws2 = wx_o[0:FI, :, :]
        w1_qkv = sb("w1_qkv", [128, 3072])
        b1_qk = sb("b1_qk", [128, 16])
        b1_v = sb("b1_v", [128, 1024])
        w1_o = sb("w1_o", [128, 8, 128])
        b1_o = sb("b1_o", [128, 128])
        w1x_q = sb("w1x_q", [128, 1024])
        w1x_k = sb("w1x_k", [DC, 1024])
        w1x_v = sb("w1x_v", [DC, 1024])
        w1x_o = sb("w1x_o", [128, 8, 128])
        b1x_o = sb("b1x_o", [128, 128])
        wf_qkv = w0_qkv
        bf_cols = sb("bf_cols", [128, 4])
        bf_v = b0_o
        wf_o = sb("wf_o", [128, 5, 128])
        bf_o = sb("bf_o", [128, 2, 128])

        union_ab = sb("union", [128, 2, 1536])
        union = [union_ab[:, s, :] for s in AB]
        x_in = [u[:, 0:256].rearrange("p (t d) -> p t d", t=2) for u in union]
        xt_in = [u[:, 256:512] for u in union]
        xs = [u[:, 512:512 + 2 * XW].rearrange("p (t d) -> p t d", t=2) for u in union]
        va_x = [u[:, 1024:1280].rearrange("p (h d) -> p h d", h=8) for u in union]
        routed = [u[:, :].rearrange("p (t k d) -> p t k d", t=2, k=TOPK) for u in union]
        x3_in = pair("x3_in", [128, 2, D])
        tri = x3_in[0][:, :, :].rearrange("p t d -> p (t d)")
        x_tok = pair("x_tok", [128, 2, D])
        x_res = pair("x_res", [128, 2, D])
        xt = pair("xt", [128, T])
        summed = pair("summed", [128, 2, D])
        x_out = pair("x_out", [128, 2, D])
        ctx_t = pair("ctx_t", [DC, 2, CTX])
        qt = pair("qt", [128, 8, T])
        kt = pair("kt", [128, 8, T])
        v_big = pair("v_big", [128, 2, 1024])
        kx = pair("kx", [128, 16, CTX])
        vx = pair("vx", [128, 8, 128])
        va = pair("va", [128, 2, 16, 32])
        qb = pair("qb", [128, 8, T], BF16)
        kb = sb("kb", [128, 16, T], BF16)
        kbf = sb("kbf", [128, 8, T], BF16)
        zeros = kbf[:, :, :].rearrange("p a b -> p (a b)").bitcast(FP32)
        kxb = sb("kxb", [128, 16, CTX], BF16)
        prob = sb("prob", [128, 8, 512])
        peak = pair("peak", [128, 2, 16], BF16)
        shift = pair("shift", [128, 2, T], BF16)
        rsum = pair("rsum", [128, 128])
        rpart = pair("rpart", [128, 128], BF16)
        rdiag = pair("rdiag", [128, 2, 128], BF16)
        stats = pair("stats", [128, 2, 6])
        moments = pair("moments", [128, 2, 2])
        powers = sb("powers", [128, 4])
        rstd = pair("rstd", [128, 2])
        hid = [t[0:FI, 0, 0:512].rearrange("p (c t) -> p c t", c=2) for t in v_big]
        hid_e = [t[0:FI, 1, 0:512].rearrange("p (c t) -> p c t", c=2) for t in v_big]
        r_exp = pair("r_exp", [128, 2, E])
        r_sel = pair("r_sel", [128, 2, E + 2])
        r_top = pair("r_top", [128, 2, 8])
        r_rep = pair("r_rep", [128, 2, E + 2])
        r_mask = pair("r_mask", [128, 2, E], BF16)
        r_maskt = pair("r_maskt", [128, T], BF16)
        r_col = pair("r_col", [128, 6])
        token_key = x3_in[1][:, :, :].rearrange("p t d -> p (t d)")
        halves = [slice(E * s, E * s + E) for s in AB]
        key_list = zeros[:, 0:CAP + T]
        key_list_next = zeros[:, CAP + T:2 * (CAP + T)]
        greatest = zeros[:, 2 * (CAP + T):2 * (CAP + T) + CAP]

        kv = [v_big[s][:, :, :].rearrange("p a (b t) -> p (a b) t", t=T) for s in AB]

        def k_of(a, s, h):
            if a is L0:
                return (kt[s] if h < 8 else kv[s])[:, h % 8, :]
            if a is L1F:
                return kv[s][:, h, :]
            return kx[s][:, h, :]

        psum = [ctx.enter_context(nc.psum_tensor(f"bank{b}", [128, 512], FP32)) for b in range(8)]

        weights_in = sem("weights_in")
        consts_ready = sem("consts_ready")
        zeroed = sem("zeroed")
        passed = sem("passed")
        chain = sem("chain")

        class Sync:

            def __init__(self, tag):
                n = lambda name: [sem(f"{tag}_{name}{s}") for s in AB]
                self.full = [sem(f"{tag}_full{b}") for b in range(8)]
                self.free = [sem(f"{tag}_free{b}") for b in range(8)]
                self.x_in = n("x_in")
                self.ctx_in = n("ctx_in")
                self.x_used = n("x_used")
                self.x_ready = n("x_ready")
                self.res_ready = n("res_ready")
                self.moments_ready = n("moments_ready")
                self.stats_ready = n("stats_ready")
                self.rstd_ready = n("rstd_ready")
                self.eps_added = n("eps_added")
                self.q16 = n("q16")
                self.k_masked = n("k_masked")
                self.k16 = n("k16")
                self.r_split = n("r_split")
                self.r_parts = n("r_parts")
                self.out_done = n("out_done")
                if tag == "p1":
                    self.r_neg = n("r_neg")
                    self.r_link = n("r_link")
                    self.r_masked = n("r_masked")
                    self.r_keyed = n("r_keyed")
                    self.key_moved = n("key_moved")
                    self.sorted = sem(f"{tag}_sorted")
                else:
                    self.twice = n("twice")
                    self.h_exp = n("h_exp")
                    self.h_link = n("h_link")
                    self.z_sum = n("z_sum")
                    self.routed_in = n("routed_in")

        p1, p3 = Sync("p1"), Sync("p3")

        LNS = {("p1", L0): 0, ("p1", L0X): 1,
               ("p3", "F"): 0, ("p3", L1): 1, ("p3", L1X): 2, ("p3", "LN"): 3, ("p3", L1F): 4}
        LN_PER = {"p1": 2, "p3": 5}
        ATTN = {("p1", L0): 0, ("p1", L0X): 1, ("p3", L1): 0, ("p3", L1X): 1, ("p3", L1F): 2}
        ATTN_PER = {"p1": 2, "p3": 3}

        plan = {"p1": interleaved(phase1_streams(), TURNS1, B_AHEAD1),
                "p3": interleaved(phase3_streams(), TURNS3, B_AHEAD3)}

        def carry_wait(eng):
            eng.sem_inc(passed, 1)

        ledger = {tag: Ledger(steps) for tag, steps in plan.items()}
        sync = {"p1": p1, "p3": p3}

        class View:

            def __init__(self, tag, it, later=0):
                self.tag, self.it, self.later, self.y = tag, it, later, sync[tag]

            def at(self, per, n):
                return self.it * per + (self.later * per + n)

            def bank_at(self, step, i, extra):
                b, n = ledger[self.tag].use[step, i]
                per = ledger[self.tag].per[b]
                return self.it * per + ((self.later + 1 - ledger[self.tag].ahead[step]) * per + n + extra)

            def may_fill(self, step, i=0):
                return self.free(step, i), self.bank_at(step, i, 1)

            def filled(self, step, i=0):
                return self.full(step, i), self.bank_at(step, i, 1)

            def drained(self, step, i=0):
                return self.free(step, i), self.bank_at(step, i, 2)

            def bank(self, step, i=0):
                return psum[ledger[self.tag].use[step, i][0]]

            def full(self, step, i=0):
                return self.y.full[ledger[self.tag].use[step, i][0]]

            def free(self, step, i=0):
                return self.y.free[ledger[self.tag].use[step, i][0]]

            def ln(self, which):
                return self.at(LN_PER[self.tag], LNS[self.tag, which] + 1)

            def attn(self, a):
                return self.at(ATTN_PER[self.tag], ATTN[self.tag, a] + 1)

            def k16(self, a, quad):
                return self.at({"p1": 5, "p3": 4}[self.tag], {L0: 1, L0X: 5, L1: 1, L1X: 2, L1F: 3}[a] + quad)

            def masked(self, a, quad):
                return self.at({"p1": 5, "p3": 2}[self.tag], {L0: 1, L0X: 5, L1F: 1}[a] + quad)

            def once(self):
                return self.at(1, 1)

        def previous_x(a):
            return {L0X: L0, "R": L0X, L1: "F", L1X: L1, L1F: "LN"}[a]

        def x_source(tag, a, s):
            if a is L0:
                return x_in[s][:, :, :]
            if a == "F":
                return x3_in[s][:, :, :]
            if a == "R":
                return xs[s][:, :, 0:D]
            if a is L1F:
                return summed[s][:, :, :]
            return x_tok[s][:, :, :]

        def o_unit(a, s, u, n=1):
            base = {L0: 2, L0X: 2, L1F: 2}.get(a, 0)
            return qt[s][:, base + u:base + u + n, :]

        def tensor_step(pe, v, step):
            kind, a, s = step[0], step[1], step[2]
            y, mm = v.y, nc.tensor.matmul
            if kind == "XT":
                if a == "F":
                    pe.wait_ge(y.x_in[s], v.at(16, 16))
                else:
                    pe.wait_ge(y.x_ready[s], v.ln(previous_x(a)))
                pe.wait_ge(*v.may_fill(step))
                src, bank = x_source(v.tag, a, s), v.bank(step)
                for t in range(2):
                    last = mm(bank[:, t * 128:(t + 1) * 128], src[:, t, :], ident[:, :], start=True, stop=True)
                last.then_inc(v.full(step), 1)
            elif kind == "Q":
                i, bank = step[3], v.bank(step)
                x = xt_in[s] if a is L0 else xt[s][:, :]
                if a is L0:
                    pe.wait_ge(y.x_in[s], v.at(32, 32))
                elif i == 0:
                    pe.wait_ge(*v.drained(("XT", a, s, 0)))
                    if a is L0X:
                        pe.wait_ge(y.ctx_in[s], v.at(16, 16))
                pe.wait_ge(*v.may_fill(step))
                if a.big:
                    w = w1_qkv if a is L1 else w1x_q
                    for j in range(2):
                        c = 2 * i + j
                        last = mm(bank[:, j * 256:(j + 1) * 256], w[:, c * 128:(c + 1) * 128], x,
                                  start=True, stop=True)
                elif a is L0:
                    for j in range(2):
                        last = mm(bank[:, j * 256:(j + 1) * 256], w0_qkv[:, j * 128:(j + 1) * 128], x,
                                  start=True, stop=True)
                elif a is L0X:
                    mm(bank[:, 0:256], wx_q[:, :], x, start=True, stop=True)
                    last = mm(bank[:, 256:256 + CTX], wx_kv[:, 0:128], ctx_t[s][:, 0, :], start=True, stop=True)
                else:
                    for j in range(2):
                        for e, m in NESTED:
                            last = mm(bank[:, j * 256 + 64 * e:j * 256 + 64 * e + 64],
                                      wf_qkv[0:m, j * 128:(j + 1) * 128], xt[s][0:m, 64 * e:64 * e + 64],
                                      start=True, stop=True)
                last.then_inc(v.full(step), 1)
            elif kind == "K":
                i, bank = step[3], v.bank(step)
                if a is L1X:
                    pe.wait_ge(y.ctx_in[s], v.at(16, 16))
                pe.wait_ge(*v.may_fill(step))
                if a is L1:
                    for j in range(2):
                        c = 8 + 2 * i + j
                        last = mm(bank[:, j * 256:(j + 1) * 256], w1_qkv[:, c * 128:(c + 1) * 128], xt[s][:, :],
                                  start=True, stop=True)
                else:
                    for c in range(8):
                        last = mm(bank[:, c * CTX:(c + 1) * CTX], w1x_k[:, c * 128:(c + 1) * 128],
                                  ctx_t[s][:, 0, :], start=True, stop=True)
                last.then_inc(v.full(step), 1)
            elif kind == "V":
                i, bank = step[3], v.bank(step)
                pe.wait_ge(*v.may_fill(step))
                if a is L1:
                    t, half = i // 2, i % 2
                    last = mm(bank[:, :], xt[s][:, t * 128:(t + 1) * 128],
                              w1_qkv[:, 2048 + 512 * half:2560 + 512 * half], start=True, stop=True)
                elif a is L1X:
                    last = mm(bank[:, :], ctx_t[s][:, :, :], w1x_v[:, 512 * i:512 * i + 512], start=True, stop=True)
                elif a is L0:
                    for t in range(2):
                        last = mm(bank[:, t * 128:(t + 1) * 128], xt_in[s][:, t * 128:(t + 1) * 128],
                                  w0_qkv[:, 256:384], start=True, stop=True)
                elif a is L0X:
                    last = mm(bank[:, 0:128], ctx_t[s][:, :, :], wx_kv[:, 128:256], start=True, stop=True)
                else:
                    for e, m in NESTED:
                        p = 64 * (e % 2)
                        last = mm(bank[p:p + 64, (e // 2) * 128:(e // 2) * 128 + 128],
                                  xt[s][0:m, 64 * e:64 * e + 64], wf_qkv[0:m, 256:384], start=True, stop=True)
                last.then_inc(v.full(step), 1)
            elif kind == "S":
                qtile, h0, n, keys = a.s_chunks()[step[3]]
                bank = v.bank(step)
                if step[3] == 0:
                    pe.wait_ge(y.q16[s], v.attn(a))
                if step[3] == 0 or (a.quads and h0 % 4 == 0 and h0 != a.s_chunks()[step[3] - 1][1] // 4 * 4):
                    pe.wait_ge(y.k16[s], v.k16(a, h0 // 4 if a.quads else 0))
                pe.wait_ge(*v.may_fill(step))
                q0 = qtile * 128
                if a.ctx and a.big:
                    for j in range(n // 2):
                        c = h0 // 2 + j
                        last = mm(bank[:, j * 128:(j + 1) * 128], qb[s][:, c, q0:q0 + 128],
                                  kxb[:, 2 * c:2 * c + 2, :], start=True, stop=True)
                else:
                    k16 = (kxb if a.ctx else kbf if a is L1F else kb)[:, h0:h0 + n, 0:keys]
                    c = h0 // 2 if a.big else 0
                    last = mm(bank[:, 0:n * keys].rearrange("p (h k) -> p h k", h=n), qb[s][:, c, q0:q0 + 128], k16,
                              start=True, stop=not a.causal)
                    if a.causal:
                        neg = ident_inf if a.causal == "inf" else ident_add
                        c = 0 if qtile == 0 else keys - 128
                        last = mm(bank[:, :].rearrange("p (h k) -> p h k", h=n)[:, :, c:keys], neg[:, :],
                                  mask_s[:, 0:keys - c].unsqueeze(1).to_broadcast([128, n, keys - c]),
                                  start=False, stop=True)
                last.then_inc(v.full(step), 1)
            elif kind == "N":
                bank = v.bank(step)
                pe.wait_ge(*v.drained(("S", a, s, len(a.s_chunks()) - 1)))
                pe.wait_ge(*v.may_fill(step))
                for t in range(2):
                    last = mm(bank[0:a.heads, t * 128:(t + 1) * 128], peak[s][:, t, 0:a.heads], neg_ident[:, :],
                              start=True, stop=True)
                last.then_inc(v.full(step), 1)
            elif kind == "T":
                g, i = step[3], step[4]
                ktile, heads, queries = a.t_chunks()[i]
                n = len(heads)
                bank = v.bank(step)
                if g == 0 and i == 0:
                    pe.wait_ge(*v.drained(("N", a, s, 0)))
                if a.quads and i == 0:
                    pe.wait_ge(y.k_masked[s], v.masked(a, g))
                pe.wait_ge(*v.may_fill(step))
                q0 = 256 - queries
                if a.ctx:
                    for j in range(2):
                        c = 2 * g + j
                        cols = bank[:, j * 256:(j + 1) * 256]
                        pair_sel = sel_flat[:, 256 * c + CTX:256 * c + 3 * CTX]
                        mm(cols, pair_sel, shift[s][:, 0, :], start=True, stop=False)
                        q = qt[s][:, c, :] if a.big else qt[s][:, 0, :]
                        last = mm(cols, kx[s][:, 2 * c:2 * c + 2, :], q, start=False, stop=True)
                else:
                    full = 1 if a is L1 and ktile == 1 else 0
                    for j in range(n):
                        h = 4 * g + heads[j]
                        cols = bank[:, j * queries:(j + 1) * queries]
                        mm(cols, sel_h[:, h, :], shift[s][:, full, q0:256], start=True, stop=False)
                        if a.big:
                            r = 64 * (h % 2)
                            lhs = kt[s][r:r + 64, h // 2, ktile * 128:(ktile + 1) * 128]
                            rhs = qt[s][r:r + 64, h // 2, :]
                        else:
                            lhs = k_of(a, s, h)[:, ktile * 128:(ktile + 1) * 128]
                            rhs = qt[s][:, 0, q0:256]
                        last = mm(cols, lhs, rhs, start=False, stop=not a.causal)
                        if a.causal:
                            neg = ident_inf if a.causal == "inf" else ident_add
                            c = 128 * ktile - q0
                            last = mm(cols[:, c:c + 128], neg[:, :], mask_t[:, :], start=False, stop=True)
                last.then_inc(v.full(step), 1)
            elif kind == "P":
                g = step[3]
                nt = len(a.t_chunks())
                for i in range(max(0, nt - 2), nt):
                    pe.wait_ge(*v.drained(("T", a, s, g, i)))
                if g == 0:
                    if a is L1:
                        pe.wait_ge(*v.drained(("V", a, s, 3)))
                    elif a is L1X:
                        pe.wait_ge(*v.drained(("V", a, s, 1)))
                    else:
                        pe.wait_ge(*v.drained(("V", a, s, 0)))
                slot = 4 * (g % 2)

                def p_of(ktile, j):
                    i, col, q0 = a.place(ktile, j)
                    return prob[:, slot + i, col:col + T - q0], q0

                kts = 1 if a.ctx else 2
                if a.big:
                    o_fill = step, 1 if g == 0 else 0
                    pe.wait_ge(*v.may_fill(*o_fill))
                    bank = v.bank(*o_fill)
                    for j in range(2):
                        cols = bank[:, j * 256:(j + 1) * 256]
                        if a.ctx:
                            last = mm(cols, vx[s][:, 2 * g + j, :], p_of(0, 2 * j)[0], start=True, stop=True)
                        else:
                            for k in range(2):
                                for u in range(2):
                                    h = 4 * g + 2 * j + u
                                    last = mm(cols[64 * u:64 * u + 64, :], v_big[s][:, k, h * 64:(h + 1) * 64],
                                              p_of(k, 2 * j + u)[0], start=(k == 0), stop=(k == 1))
                    last.then_inc(v.full(*o_fill), 1)
                    d_fill = ("P", a, s, 0), 0
                    if g == 0:
                        pe.wait_ge(*v.may_fill(*d_fill))
                    sums = v.bank(*d_fill)
                    for k in range(kts):
                        for u in range(2):
                            for t in range(2):
                                for j in (u, u + 2):
                                    r = 64 * t + 32 * (j // 2)
                                    last = mm(sums[r:r + 32, 0:128], (ones_u if a.ctx else ones_g)[:, u, g, :],
                                              p_of(k, j)[0][:, 128 * t:128 * t + 128],
                                              start=(g == 0 and k == 0 and u == 0),
                                              stop=(g == a.groups - 1 and k == kts - 1 and u == 1))
                    if g == a.groups - 1:
                        last.then_inc(v.full(*d_fill), 1)
                else:
                    fill = ("P", a, s, g - g % 2), 0
                    if g % 2 == 0:
                        pe.wait_ge(*v.may_fill(*fill))
                    bank = v.bank(*fill)
                    for k in range(kts):
                        for j in range(4):
                            p, q0 = p_of(k, j)
                            h = 4 * g + j
                            lhs = va_x[s][:, h, :] if a.ctx else va[s][:, k, h, :]
                            last = mm(bank[32 * j:32 * j + 32, (g % 2) * 256 + q0:(g % 2) * 256 + 256], lhs, p,
                                      start=(k == 0), stop=(k == kts - 1))
                    if g % 2 == 1:
                        last.then_inc(v.full(*fill), 1)
            elif kind == "X":
                bank = v.bank(step)
                for u in range(0, a.units, 2):
                    pe.wait_ge(*v.drained(("P", a, s, u)))
                pe.wait_ge(*v.may_fill(step))
                for u in range(a.units):
                    parity, block = (u % 2, u // 2) if a.units == 4 else (2, u)
                    for t in range(2):
                        r = 64 * t + 32 * block
                        last = mm(bank[r:r + 32, 0:128], pick_sum[:, parity, :],
                                  o_unit(a, s, u)[:, 0, 128 * t:128 * t + 128],
                                  start=(parity != 1), stop=(parity != 0))
                last.then_inc(v.full(step), 1)
            elif kind == "B":
                i, bank = step[3], v.bank(step)
                if i == 0:
                    pe.wait_ge(y.r_parts[s], v.attn(a))
                pe.wait_ge(*v.may_fill(step))
                for j in range(2):
                    u = 2 * i + j
                    lhs = spread_b[:, u, :] if a.big else spread_s[:, u if a.units == 4 else 2 * u, :]
                    last = mm(bank[:, j * 256:(j + 1) * 256], lhs, rdiag[s][:, :, :], start=True, stop=True)
                last.then_inc(v.full(step), 1)
            elif kind == "W":
                bank = v.bank(step)
                pe.wait_ge(*v.drained(("B", a, s, a.units // 2 - 1)))
                pe.wait_ge(*v.may_fill(step))
                if a is L1F:
                    for e, m in NESTED:
                        p = 64 * (e % 2)
                        rows = [(u, 128) for u in range(2)] if e == 0 else [(0, {1: 128, 2: 64, 3: 32}[e])]
                        for n, (u, r) in enumerate(rows):
                            last = mm(bank[p:p + 64, (e // 2) * 128:(e // 2) * 128 + 128],
                                      o_unit(a, s, u)[0:r, 0, 64 * e:64 * e + 64], wf_o[0:r, e + (e > 0) + u, :],
                                      start=(n == 0), stop=(n == len(rows) - 1))
                else:
                    w = {L0: w0_o, L0X: wx_o, L1: w1_o, L1X: w1x_o}[a]
                    for t in range(2):
                        for u in range(a.units):
                            last = mm(bank[:, t * 128:(t + 1) * 128], o_unit(a, s, u)[:, 0, t * 128:(t + 1) * 128],
                                      w[:, u, :], start=(u == 0), stop=(u == a.units - 1))
                last.then_inc(v.full(step), 1)
            elif kind == "R1":
                pe.wait_ge(*v.drained(("XT", "R", s, 0)))
                pe.wait_ge(*v.may_fill(step))
                bank = v.bank(step)
                for t in range(2):
                    last = mm(bank[:, t * E:(t + 1) * E], xt[s][:, t * 128:(t + 1) * 128], gate_w[:, :],
                              start=True, stop=True)
                last.then_inc(v.full(step), 1)
            elif kind == "R2":
                pe.wait_ge(y.r_masked[s], v.once())
                pe.wait_ge(*v.may_fill(step))
                bank = v.bank(step)
                for t in range(2):
                    last = mm(bank[halves[s], t * 128:(t + 1) * 128], r_mask[s][:, t, :], ident_b[:, :],
                              start=True, stop=True)
                last.then_inc(v.full(step), 1)
            elif kind == "R3":
                pe.wait_ge(*v.drained(("R2", "R", s, 0)))
                pe.wait_ge(*v.may_fill(step))
                carry_wait(pe)
                mm(v.bank(step)[halves[s], 0:256], upper_b[halves[s], :], r_maskt[s][halves[s], :],
                   start=True, stop=True).then_inc(v.full(step), 1)
            elif kind == "F1":
                pe.wait_ge(*v.drained(("XT", "F", s, 0)))
                for i in range(2):
                    pe.wait_ge(*v.may_fill(step, i))
                    for c in range(2):
                        last = mm(v.bank(step, i)[0:FI, c * 256:(c + 1) * 256], ws13[:, 2 * i + c, :], xt[s][:, :],
                                  start=True, stop=True)
                    last.then_inc(v.full(step, i), 1)
            elif kind == "F2":
                pe.wait_ge(*v.drained(("F1", "F", s, 0), 1))
                pe.wait_ge(*v.may_fill(step))
                for t in range(2):
                    for c in range(2):
                        last = mm(v.bank(step)[:, t * 128:(t + 1) * 128], hid[s][:, c, t * 128:(t + 1) * 128],
                                  ws2[:, c, :], start=(c == 0), stop=(c == 1))
                last.then_inc(v.full(step), 1)

        def absent_step(pe, v, step):
            for i in range(len(fills(step))):
                pe.wait_ge(*v.may_fill(step, i))
                pe.sem_inc(v.full(step, i), 1)
                pe.sem_inc(v.free(step, i), 1)

        def scalar_step(act, v, step):
            kind, a, s = step[0], step[1], step[2]
            y, copy = v.y, nc.scalar.copy
            if kind == "XT":
                act.wait_ge(*v.filled(step))
                if a is L1F:
                    nc.scalar.activation(xt[s][:, :], v.bank(step)[:, 0:256], ACT.Identity, bias=bf_cols[:, 1:2],
                                         scale=bf_cols[:, 0:1]).then_inc(v.free(step), 1)
                else:
                    copy(xt[s][:, :], v.bank(step)[:, 0:256]).then_inc(v.free(step), 1)
            elif kind == "Q":
                i, bank = step[3], v.bank(step)
                act.wait_ge(*v.filled(step))
                if a is L1:
                    for j in range(2):
                        c = 2 * i + j
                        last = nc.scalar.activation(qt[s][:, c, :], bank[:, j * 256:(j + 1) * 256], ACT.Identity,
                                                    bias=b1_qk[:, c:c + 1])
                elif a is L1X:
                    last = copy(qt[s][:, 2 * i:2 * i + 2, :], bank[:, :].rearrange("p (c t) -> p c t", c=2))
                elif a is L1F:
                    for j in range(2):
                        last = nc.scalar.activation(qt[s][:, j, :], bank[:, j * 256:(j + 1) * 256], ACT.Identity,
                                                    bias=bf_cols[:, 2 + j:3 + j])
                elif a is L0:
                    last = copy(qt[s][:, 0:2, :], bank[:, :].rearrange("p (c t) -> p c t", c=2))
                else:
                    flat = qt[s][:, :, :].rearrange("p c t -> p (c t)")
                    last = copy(flat[:, 0:256 + CTX], bank[:, 0:256 + CTX])
                last.then_inc(v.free(step), 1)
            elif kind == "K" and a is L1:
                i, bank = step[3], v.bank(step)
                act.wait_ge(*v.filled(step))
                for j in range(2):
                    c = 2 * i + j
                    last = nc.scalar.activation(kt[s][:, c, :], bank[:, j * 256:(j + 1) * 256], ACT.Identity,
                                                bias=b1_qk[:, 8 + c:9 + c])
                last.then_inc(v.free(step), 1)
            elif kind == "C":
                if step[3]:
                    return
                last_q = ("Q", a, s, 3 if a.big else 0)
                act.wait_ge(*v.drained(last_q))
                n = 8 if a.big else 1
                copy(qb[s][:, 0:n, :], qt[s][:, 0:n, :]).then_inc(y.q16[s], 1)
            elif kind == "H":
                m0 = 0 if a is L0 else 16
                for h in range(4 * step[3], 4 * step[3] + 4):
                    last = nc.scalar.activation(k_of(a, s, h), qt[s][:, 1, :], ACT.Copy,
                                                scale=head_mask[:, m0 + h:m0 + h + 1])
                last.then_inc(y.k_masked[s], 1)
            elif kind == "V" and a not in (L1, L1F):
                i, bank = step[3], v.bank(step)
                act.wait_ge(*v.filled(step))
                if a is L0:
                    last = copy(va[s][:, :, :, 0:8], bank[:, 0:256].rearrange("p (t h d) -> p t h d", t=2, h=16))
                elif a is L0X:
                    for u in range(2):
                        src = bank[64 * u:64 * u + 64, 0:128].rearrange("p (c u d) -> p c u d", u=2, d=16)
                        dst = va_x[s][64 * u:64 * u + 64, :, 0:16].rearrange("p (c u) d -> p c u d", u=2)
                        last = copy(dst[:, :, u, :], src[:, :, u, :])
                else:
                    for u in range(2):
                        src = bank[64 * u:64 * u + 64, :].rearrange("p (c u d) -> p c u d", u=2, d=64)
                        last = copy(vx[s][64 * u:64 * u + 64, 4 * i:4 * i + 4, 64 * u:64 * u + 64], src[:, :, u, :])
                last.then_inc(v.free(step), 1)
            elif kind == "N":
                act.wait_ge(*v.filled(step))
                minus = v.bank(step)[0:a.heads, 0:256].unsqueeze(1).to_broadcast([a.heads, 2, T])
                copy(shift[s][0:a.heads, :, :], minus).then_inc(v.free(step), 1)
            elif kind == "T":
                g, i = step[3], step[4]
                act.wait_ge(*v.filled(step))
                nc.scalar.activation(prob[:, 4 * (g % 2) + i, :], v.bank(step)[:, :], ACT.Exp,
                                     scale=a.scale).then_inc(v.free(step), 1)
            elif kind == "P":
                g = step[3]
                if a.big:
                    fill = step, 1 if g == 0 else 0
                elif g % 2 == 1:
                    fill = ("P", a, s, g - 1), 0
                else:
                    return
                act.wait_ge(*v.filled(*fill))
                u0 = 2 * g if a.big else g - 1
                copy(o_unit(a, s, u0, 2), v.bank(*fill)[:, :].rearrange("p (c t) -> p c t", c=2)).then_inc(
                    v.free(*fill), 1)
            elif kind == "R1":
                act.wait_ge(y.r_neg[s], v.once())
                for t in range(2):
                    last = nc.scalar.activation(r_exp[s][:, t, :], v.bank(step)[:, t * E:(t + 1) * E], ACT.Exp,
                                                bias=r_col[s][:, t:t + 1], accum_out=r_col[s][:, 2 + t:3 + t])
                last.then_inc(v.free(step), 1)
            elif kind == "R2":
                act.wait_ge(*v.filled(step))
                copy(r_maskt[s][halves[s], :], v.bank(step)[halves[s], 0:256]).then_inc(v.free(step), 1)
            elif kind == "F1":
                act.wait_ge(*v.filled(step, 0))
                nc.scalar.activation(hid_e[s], v.bank(step, 0)[0:FI, :].rearrange("p (c t) -> p c t", c=2),
                                     ACT.Exp, scale=-1.0).then_inc(y.h_exp[s], 1)

        def layer_norm_sums(dve, v, s, which, src):
            y = v.y
            for t in range(2):
                last = nc.vector.bn_stats(stats[s][:, t, :], src[:, t, :])
            last.then_inc(y.stats_ready[s], 1)
            dve.wait_ge(y.stats_ready[s], v.ln(which))
            carry_wait(dve)
            for t in range(2):
                last = nc.vector.bn_aggr(moments[s][:, t, :], stats[s][:, t, :])
            last.then_inc(y.moments_ready[s], 1)

        def layer_norm_apply(dve, v, s, which, src, dst):
            y = v.y
            dve.wait_ge(y.rstd_ready[s], v.ln(which))
            for t in range(2):
                last = nc.vector.tensor_scalar(dst[:, t, :], src[:, t, :], moments[s][:, t, 0:1],
                                               rstd[s][:, t:t + 1], ALU.subtract, ALU.mult)
            last.then_inc(y.x_ready[s], 1)

        def vector_step(dve, v, step):
            kind, a, s = step[0], step[1], step[2]
            y, tt = v.y, nc.vector.tensor_tensor
            if kind == "K" and a is L1X:
                dve.wait_ge(*v.filled(step))
                for u in range(2):
                    dst = kx[s][64 * u:64 * u + 64, :, :].rearrange("p (c u) k -> p c u k", u=2)
                    src = v.bank(step)[64 * u:64 * u + 64, :].rearrange("p (c k) -> p c k", c=8)
                    last = nc.vector.tensor_copy(dst[:, :, u, :], src)
                last.then_inc(v.free(step), 1)
            elif kind == "C":
                if a is L1:
                    dve.wait_ge(*v.drained(("K", a, s, 3)))
                    for u in range(2):
                        dst = kb[64 * u:64 * u + 64, :, :].rearrange("p (c u) k -> p c u k", u=2)
                        last = nc.vector.tensor_copy(dst[:, :, u, :], kt[s][64 * u:64 * u + 64, :, :])
                elif a is L1X:
                    dve.wait_ge(*v.drained(("K", a, s, 0)))
                    last = nc.vector.tensor_copy(kxb[:, :, :], kx[s][:, :, :])
                else:
                    dve.wait_ge(*v.drained(("Q", a, s, 0)))
                    k1 = qt[s][:, 1, 0:a.keys]
                    if a.quads:
                        m0, k16 = (0, kb) if a is L0 else (16, kbf)
                        for h in range(4 * step[3], 4 * step[3] + 4):
                            last = nc.vector.tensor_scalar(k16[:, h, :], k1, head_mask[:, m0 + h:m0 + h + 1], None,
                                                           ALU.mult)
                    else:
                        m = head_mask[:, 16:24].unsqueeze(2).to_broadcast([128, 8, CTX])
                        tt(kx[s][:, 0:8, :], k1.unsqueeze(1).to_broadcast([128, 8, CTX]), m, ALU.mult).then_inc(
                            y.k_masked[s], 1)
                        dve.wait_ge(y.k_masked[s], v.masked(a, 0))
                        last = nc.vector.tensor_copy(kxb[:, 0:8, :], kx[s][:, 0:8, :])
                last.then_inc(y.k16[s], 1)
            elif kind == "V" and a in (L1, L1F):
                i, bank = step[3], v.bank(step)
                dve.wait_ge(*v.filled(step))
                if a is L1:
                    t, half = i // 2, i % 2
                    last = tt(v_big[s][:, t, 512 * half:512 * half + 512], bank[:, :],
                              b1_v[:, 512 * half:512 * half + 512], ALU.add)
                else:
                    for t in range(2):
                        last = tt(va[s][:, t, 0:8, 0:16], bank[:, t * 128:(t + 1) * 128].rearrange("p (h d) -> p h d", h=8),
                                  bf_v[:, :].rearrange("p (h d) -> p h d", h=8), ALU.add)
                last.then_inc(v.free(step), 1)
            elif kind == "S":
                qtile, h0, n, keys = a.s_chunks()[step[3]]
                dve.wait_ge(*v.filled(step))
                nc.vector.tensor_reduce(peak[s][:, qtile, h0:h0 + n],
                                        v.bank(step)[:, 0:n * keys].rearrange("p (h k) -> p h k", h=n),
                                        axis=AX.X, op=ALU.max).then_inc(v.free(step), 1)
            elif kind == "D":
                fill = ("P", a, s, 0) if a.big else ("X", a, s, 0)
                dve.wait_ge(*v.filled(fill))
                r, part, per = rsum[s][:, :], rpart[s][:, :], 3 * ATTN_PER[v.tag]
                split = nc.vector.scalar_tensor_tensor
                nc.vector.reciprocal(r, v.bank(fill)[:, 0:128]).then_inc(v.free(fill), 1)
                dve.wait_ge(*v.drained(fill))
                for i in range(2):
                    n = 3 * ATTN[v.tag, a] + 2 * i
                    nc.vector.tensor_copy(part, r).then_inc(y.r_split[s], 1)
                    dve.wait_ge(y.r_split[s], v.at(per, n + 1))
                    if i == 0:
                        split(r, part, part_cols[:, 0:1], r, ALU.mult, ALU.add).then_inc(y.r_split[s], 1)
                        dve.wait_ge(y.r_split[s], v.at(per, n + 2))
                for t in range(2):
                    h = slice(64 * t, 64 * t + 64)
                    last = split(rdiag[s][h, t, :], part[h], part_cols[h, 1:2], r[h], ALU.mult, ALU.add)
                last.then_inc(y.r_parts[s], 1)
            elif kind == "B":
                i = step[3]
                dve.wait_ge(*v.filled(step))
                if a.big:
                    dve.wait_ge(*v.drained(("P", a, s, a.groups - 1)))
                unit = o_unit(a, s, 2 * i, 2)
                tt(unit, unit, v.bank(step)[:, :].rearrange("p (c t) -> p c t", c=2), ALU.mult).then_inc(
                    v.free(step), 1)
            elif kind == "W":
                dve.wait_ge(*v.filled(step))
                dve.wait_ge(y.res_ready[s], v.attn(a))
                tt(summed[s][:, :, :], v.bank(step)[:, 0:256].rearrange("p (t d) -> p t d", t=2), x_res[s][:, :, :],
                   ALU.add).then_inc(v.free(step), 1)
                dve.wait_ge(*v.drained(step))
                if a is L1F:
                    tt(summed[s][:, :, :], summed[s][:, :, :], x_tok[s][:, :, :], ALU.add).then_inc(y.twice[s], 1)
                    dve.wait_ge(y.twice[s], v.once())
                layer_norm_sums(dve, v, s, a, summed[s])
            elif kind == "L":
                if a is L0X:
                    dve.wait_ge(y.out_done[s], v.at(16, 1))
                    layer_norm_apply(dve, v, s, a, summed[s], xs[s][:, :, 0:D])
                elif a is L1F:
                    dve.wait_ge(y.out_done[s], v.at(16, 1))
                    layer_norm_apply(dve, v, s, a, summed[s], x_out[s])
                else:
                    layer_norm_apply(dve, v, s, a, summed[s], x_tok[s])
            elif kind == "LN":
                dve.wait_ge(y.x_ready[s], v.ln(L1X))
                layer_norm_sums(dve, v, s, "LN", x_tok[s])
                layer_norm_apply(dve, v, s, "LN", x_tok[s], summed[s])
            elif kind == "R1":
                c = r_col[s]
                dve.wait_ge(*v.filled(step))
                nc.vector.tensor_reduce(c[:, 4:6], v.bank(step)[:, 0:2 * E].rearrange("p (t e) -> p t e", t=2),
                                        axis=AX.X, op=ALU.max).then_inc(y.r_link[s], 1)
                dve.wait_ge(y.r_link[s], v.at(7, 1))
                nc.vector.tensor_scalar(c[:, 0:2], c[:, 4:6], -1.0, None, ALU.mult).then_inc(y.r_neg[s], 1)
            elif kind == "RN":
                link = [1]

                def linked(ins):
                    link[0] += 1
                    ins.then_inc(y.r_link[s], 1)
                    dve.wait_ge(y.r_link[s], v.at(7, link[0]))
                    carry_wait(dve)

                c = r_col[s]
                dve.wait_ge(*v.drained(("R1", "R", s, 0)))
                linked(nc.vector.reciprocal(c[:, 4:6], c[:, 2:4]))
                for t in range(2):
                    last = nc.vector.tensor_scalar(xs[s][:, t, D:XW], r_exp[s][:, t, :], c[:, 4 + t:5 + t], None,
                                                   ALU.mult)
                linked(last)
                linked(tt(r_sel[s][:, :, 0:E], xs[s][:, :, D:XW], gate_b[:, :].unsqueeze(1).to_broadcast([128, 2, E]),
                          ALU.add))
                for t in range(2):
                    last = nc.vector.max(r_top[s][:, t, :], r_sel[s][:, t, 0:E])
                linked(last)
                linked(nc.vector.memset(r_top[s][:, :, TOPK:8], BIG))
                for t in range(2):
                    last = nc.vector.match_replace(r_rep[s][:, t, :], r_top[s][:, t, :], r_sel[s][:, t, :], -BIG)
                linked(last)
                tt(r_mask[s][:, :, :], r_rep[s][:, :, 0:E], r_sel[s][:, :, 0:E], ALU.not_equal).then_inc(y.r_masked[s], 1)
            elif kind == "R3":
                dve.wait_ge(*v.filled(step))
                rows = halves[s]
                new = key_list[rows, CAP:CAP + T]
                dve.wait_ge(y.sorted, v.at(2 * ROUNDS, 1))
                dve.wait_ge(y.key_moved[s], v.once())
                dve.wait_ge(zeroed, 24 * 16)
                tt(new, v.bank(step)[rows, 0:256], token_key[rows, :], ALU.add).then_inc(v.free(step), 1)
                dve.wait_ge(*v.drained(step))
                tt(new, new, r_maskt[s][rows, :], ALU.mult).then_inc(y.r_keyed[s], 1)
                nc.vector.tensor_scalar(token_key[rows, :], token_key[rows, :], -16.0 * T, None, ALU.add).then_inc(
                    y.key_moved[s], 1)
            elif kind == "RL":
                if step[3] == 0:
                    for u in AB:
                        dve.wait_ge(y.r_keyed[u], v.once())
                for r in (2 * step[3], 2 * step[3] + 1):
                    cur, nxt = (key_list, key_list_next)[::1 if r % 2 == 0 else -1]
                    top = greatest[:, 8 * r:8 * r + 8]
                    if r == 0:
                        carry_wait(dve)
                    nc.vector.max(top, cur).then_inc(y.sorted, 1)
                    dve.wait_ge(y.sorted, v.at(2 * ROUNDS, 2 * r + 2))
                    carry_wait(dve)
                    if r < ROUNDS - 1:
                        last = nc.vector.match_replace(nxt, top, cur, 0.0)
                    else:
                        last = nc.vector.tensor_copy(key_list[:, 0:CAP], greatest)
                    last.then_inc(y.sorted, 1)
                    dve.wait_ge(y.sorted, v.at(2 * ROUNDS, 2 * r + 3))
                    carry_wait(dve)
            elif kind == "F1":
                h1 = v.bank(step, 0)[0:FI, :].rearrange("p (c t) -> p c t", c=2)
                h3 = v.bank(step, 1)[0:FI, :].rearrange("p (c t) -> p c t", c=2)
                dve.wait_ge(y.h_exp[s], v.once())
                nc.vector.tensor_scalar(hid_e[s], hid_e[s], 1.0, None, ALU.add).then_inc(y.h_link[s], 1)
                dve.wait_ge(y.h_link[s], v.at(2, 1))
                nc.vector.reciprocal(hid[s], hid_e[s]).then_inc(y.h_link[s], 1)
                dve.wait_ge(y.h_link[s], v.at(2, 2))
                tt(hid[s], hid[s], h1, ALU.mult).then_inc(v.free(step, 0), 1)
                dve.wait_ge(*v.drained(step, 0))
                dve.wait_ge(*v.filled(step, 1))
                tt(hid[s], hid[s], h3, ALU.mult).then_inc(v.free(step, 1), 1)
            elif kind == "Z":
                dve.wait_ge(y.routed_in[s], v.at(16, 16))
                nc.vector.tensor_reduce(x_res[s][:, :, :], routed[s].rearrange("p t k d -> p t d k"), axis=AX.X,
                                        op=ALU.add).then_inc(y.z_sum[s], 1)
            elif kind == "F2":
                dve.wait_ge(*v.filled(step))
                dve.wait_ge(y.z_sum[s], v.once())
                tt(summed[s][:, :, :], v.bank(step)[:, 0:256].rearrange("p (t d) -> p t d", t=2), x_res[s][:, :, :],
                   ALU.add).then_inc(v.free(step), 1)
                dve.wait_ge(*v.drained(step))
                tt(summed[s][:, :, :], summed[s][:, :, :], x3_in[s][:, :, :], ALU.add).then_inc(y.x_used[s], 1)
                dve.wait_ge(y.x_used[s], v.once())
                layer_norm_sums(dve, v, s, "F", summed[s])

        def pool_step(pool, v, step):
            kind, a, s = step[0], step[1], step[2]
            y = v.y
            if kind in ("W", "F2", "LN"):
                which = {"W": a, "F2": "F", "LN": "LN"}[kind]
                pool.wait_ge(y.moments_ready[s], v.ln(which))
                nc.gpsimd.tensor_tensor(rstd[s][:, :], moments[s][:, :, 1], powers[:, 0:2], ALU.add).then_inc(
                    y.eps_added[s], 1)
                pool.wait_ge(y.eps_added[s], v.ln(which))
                nc.gpsimd.tensor_tensor(rstd[s][:, :], rstd[s][:, :], powers[:, 2:4], ALU.pow).then_inc(
                    y.rstd_ready[s], 1)
            if (kind == "Q" and step[3] == 0 and a is not L1F) or kind == "LN":
                if a is L0:
                    pool.wait_ge(y.x_in[s], v.at(32, 32))
                else:
                    pool.wait_ge(y.x_ready[s], v.ln(L1X if a is L1F else previous_x(a)))
                src = x_in[s] if a is L0 else x_tok[s][:, :, :]
                bias = {L0: b0_o, L0X: bx_o, L1: b1_o, L1X: b1x_o}.get(a)
                bias = bf_o[:, :, :] if bias is None else bias[:, :].unsqueeze(1).to_broadcast([128, 2, D])
                nc.gpsimd.tensor_tensor(x_res[s][:, :, :], src, bias, ALU.add).then_inc(y.res_ready[s], 1)


        NB = 8
        lists = key_list[:, 0:CAP]
        both = summed[0][0:E, 0, :]
        both_b = summed[1][0:E, 0, :]
        final = xt[1][0:E, 0:CAP]
        slot_key = sb("slot_key", [128, 32], I32)
        slot_hi = sb("slot_hi", [128, 32], I32)
        slot_lo = sb("slot_lo", [128, 32], I32)
        x_row = sb("x_row", [128, 32], I32)
        z_row = sb("z_row", [128, 32], I32)
        f32_of = lambda t, n: t.rearrange("p a b -> p (a b)")[:, 0:n]
        e_x = [f32_of(t, 16 * XW).rearrange("p (n w) -> p n w", w=XW)
               for t in (prob[:, :, :], union_ab[:, :, :])]
        e_y = qt[0][:, :, :].rearrange("p a (b d) -> p (a b) d", d=D)
        e_w1 = [f32_of(v_big[p][:, :, :], 16 * FI).rearrange("p (n i) -> p n i", i=FI) for p in AB]
        e_w3 = [f32_of(qt[1][:, :, :], 16 * FI).rearrange("p (n i) -> p n i", i=FI),
                kb[:, :, :].rearrange("p a b -> p (a b)").bitcast(FP32)[:, 0:16 * FI].rearrange(
                    "p (n i) -> p n i", i=FI)]
        e_w2 = [kt[p][0:FI, :, :].rearrange("p a (b d) -> p (a b) d", d=D) for p in AB]
        e_xt = [kx[p][:, :, :].rearrange("p a b -> p (a b)") for p in AB]
        e_h = [vx[p][0:FI, :, :].rearrange("p a b -> p (a b)") for p in AB]

        half_lists = sem("half_lists")
        half_moved = sem("half_moved")
        final_ready = sem("final_ready")
        slots_full = sem("slots_full")
        rows_ready = sem("rows_ready")
        w13_in = [sem(f"w13_in{p}") for p in AB]
        w2_in = [sem(f"w2_in{p}") for p in AB]
        E_ITERS = 32 // (2 * NB)
        gathered = [[sem(f"gathered{it}{p}") for p in AB] for it in range(E_ITERS)]
        e_xt_full = [sem(f"e_xt_full{p}") for p in AB]
        e_xt_ready = [sem(f"e_xt_ready{p}") for p in AB]
        e_h_full = [sem(f"e_h_full{p}") for p in AB]
        e_exp = [sem(f"e_exp{p}") for p in AB]
        e_link = sem("e_link")
        e_h_ready = [sem(f"e_h_ready{p}") for p in AB]
        e_y_full = [sem(f"e_y_full{p}") for p in AB]
        e_y_ready = [sem(f"e_y_ready{p}") for p in AB]
        scattered = [sem(f"scattered{p}") for p in AB]
        outputs_free = [sem(f"outputs_free{p}") for p in AB]
        p3_ready = sem("p3_ready")

        def experts_tensor(pe):
            pe.wait_ge(final_ready, 1)
            for u in range(2):
                last = nc.tensor.matmul(psum[0][64 * u:64 * u + 64, 0:32], final, ident[0:E, u:E:2],
                                        start=True, stop=True)
            last.then_inc(slots_full, 1)

            def to_features(it, p):
                pe.wait_ge(gathered[it][p], 16 * NB)
                for n in range(NB):
                    last = nc.tensor.matmul(psum[p][:, (n % 4) * 128:(n % 4) * 128 + 128],
                                            e_x[p][:, it * NB + n, 0:D], ident[:, :], start=True, stop=True)
                    if n % 4 == 3:
                        last.then_inc(e_xt_full[p], 1)
                        if n < NB - 1:
                            pe.wait_ge(e_xt_ready[p], it * 2 + 1)

            def up(it, p):
                pe.wait_ge(e_xt_ready[p], it * 2 + 2)
                pe.wait_ge(w13_in[p], it * 32 + 32)
                for n in range(NB):
                    bank = psum[2 + n // 2]
                    if n % 2 == 0 and p == 1:
                        pe.wait_ge(e_h_ready[0], it * 4 + (n // 2 + 1))
                    for u in range(2):
                        xt_u = e_xt[p][:, n * 128 + 64 * u:n * 128 + 64 * u + 64]
                        for k, w in enumerate((e_w1[p], e_w3[p])):
                            c = 256 * k + (n % 2) * 128 + 64 * u
                            last = nc.tensor.matmul(bank[0:FI, c:c + 64], w[:, 2 * n + u, :], xt_u,
                                                    start=True, stop=True)
                    if n % 2 == 1:
                        last.then_inc(e_h_full[p], 1)

            def down(it, p):
                pe.wait_ge(w2_in[p], it * 16 + 16)
                for n in range(NB):
                    bank = psum[6 + n // 4]
                    if n % 2 == 0:
                        pe.wait_ge(e_h_ready[p], it * 4 + (n // 2 + 1))
                    if n % 4 == 0 and p == 1:
                        pe.wait_ge(e_y_ready[0], it * 2 + (n // 4 + 1))
                    for u in range(2):
                        c = n * 128 + 64 * u
                        last = nc.tensor.matmul(bank[64 * u:64 * u + 64, (n % 4) * 128:(n % 4) * 128 + 128],
                                                e_h[p][:, c:c + 64], e_w2[p][:, 2 * n + u, :],
                                                start=True, stop=True)
                    if n % 4 == 3:
                        last.then_inc(e_y_full[p], 1)

            for it in range(E_ITERS):
                to_features(it, 0)
                up(it, 0)
                to_features(it, 1)
                down(it, 0)
                up(it, 1)
                down(it, 1)

        def experts_scalar(act):
            with act.Fori(0, E_ITERS) as it:
                for p in AB:
                    for q in range(2):
                        act.wait_ge(e_xt_full[p], it * 2 + (q + 1))
                        nc.scalar.copy(e_xt[p][:, 512 * q:512 * q + 512], psum[p][:, :]).then_inc(e_xt_ready[p], 1)
                    for q in range(NB // 2):
                        act.wait_ge(e_h_full[p], it * 4 + (q + 1))
                        nc.scalar.activation(e_h[p][:, 256 * q:256 * q + 256], psum[2 + q][0:FI, 0:256], ACT.Exp,
                                             scale=-1.0).then_inc(e_exp[p], 1)

        def experts_vector(dve):
            def linked(ins, count=[0]):
                count[0] += 1
                ins.then_inc(chain, 1)
                dve.wait_ge(chain, count[0])

            dve.wait_ge(p1.sorted, ITERS * 2 * ROUNDS + 1)
            nc.vector.tensor_copy(both[:, 0:CAP], lists[0:E, :]).then_inc(half_lists, 1)
            dve.wait_ge(half_lists, 1)
            dve.wait_ge(half_moved, 16)
            cur, nxt = both, both_b
            for r in range(ROUNDS):
                top = final[:, 8 * r:8 * r + 8]
                linked(nc.vector.max(top, cur))
                if r < ROUNDS - 1:
                    linked(nc.vector.match_replace(nxt, top, cur, 0.0))
                    cur, nxt = nxt, cur
            dve.sem_inc(final_ready, 1)
            dve.wait_ge(slots_full, 1)
            ts = nc.vector.tensor_scalar
            linked(nc.vector.tensor_copy(slot_key[:, :], psum[0][:, 0:32]))
            ts(slot_hi[:, :], slot_key[:, :], 3, None, ALU.arith_shift_right)
            linked(ts(slot_lo[:, :], slot_key[:, :], 7, None, ALU.bitwise_and))
            linked(ts(slot_key[:, :], slot_hi[:, :], -1.0, float(TOK), ALU.mult, ALU.add))
            ts(x_row[:, :], slot_key[:, :], float(TOK - 1), None, ALU.min)
            linked(ts(slot_key[:, :], slot_key[:, :], float(TOPK), None, ALU.mult))
            nc.vector.tensor_tensor(z_row[:, :], slot_key[:, :], slot_lo[:, :], ALU.add).then_inc(rows_ready, 1)

            with dve.Fori(0, E_ITERS) as it:
                for p in AB:
                    for q in range(NB // 2):
                        h = e_h[p][:, 256 * q:256 * q + 256]
                        n = it * 24 + (12 * p + 3 * q)
                        dve.wait_ge(e_exp[p], it * 4 + (q + 1))
                        ts(h, h, 1.0, None, ALU.add).then_inc(e_link, 1)
                        dve.wait_ge(e_link, n + 1)
                        nc.vector.reciprocal(h, h).then_inc(e_link, 1)
                        dve.wait_ge(e_link, n + 2)
                        nc.vector.tensor_tensor(h, h, psum[2 + q][0:FI, 0:256], ALU.mult).then_inc(e_link, 1)
                        dve.wait_ge(e_link, n + 3)
                        nc.vector.tensor_tensor(h, h, psum[2 + q][0:FI, 256:512], ALU.mult).then_inc(e_h_ready[p], 1)
                    dve.wait_ge(outputs_free[p], it + 1)
                    for n in range(NB):
                        if n % 4 == 0:
                            dve.wait_ge(e_y_full[p], it * 2 + (n // 4 + 1))
                        for u in range(2):
                            rows = slice(64 * u, 64 * u + 64)
                            column = it * (NB * XW + 4 * NB) + (n * XW + D + 2 * (NB * p + n) + u)
                            score = e_x[p][rows, :, :].rearrange("p n w -> p (n w)")[:, bass.ds(column, 1)]
                            last = nc.vector.tensor_tensor(e_y[rows, NB * p + n, :],
                                                           psum[6 + n // 4][rows, (n % 4) * 128:(n % 4) * 128 + 128],
                                                           score.to_broadcast([64, D]), ALU.mult)
                        if n % 4 == 3:
                            last.then_inc(e_y_ready[p], 1)

        def experts_pool(pool):
            pool.wait_ge(rows_ready, 1)
            pool.wait_ge(zeroed, 24 * 16)
            for q in AB:
                pool.wait_ge(p1.out_done[q], ITERS * 16 + 1)

            def gather(it, p):
                for n in range(NB * p, NB * p + NB):
                    j = it * 2 * NB + n
                    pool.indirect_dma_start(
                        out=e_x[p][:, it * NB + n - NB * p, :], out_offset=None, in_=xg[:, :],
                        in_offset=bass.IndirectOffsetOnAxis(ap=x_row[:, j:j + 1].bitcast(U32), axis=0),
                    ).then_inc(gathered[it][p], 16)

            def scatter(it, p):
                for n in range(NB * p, NB * p + NB):
                    j = it * 2 * NB + n
                    if n % 4 == 0:
                        pool.wait_ge(e_y_ready[p], it * 2 + ((n % NB) // 4 + 1))
                    pool.indirect_dma_start(
                        out=zd[:, :], out_offset=bass.IndirectOffsetOnAxis(ap=z_row[:, j:j + 1].bitcast(U32), axis=0),
                        in_=e_y[:, n, :], in_offset=None, bounds_check=TOK * TOPK - 1, oob_is_err=False,
                    ).then_inc(scattered[p], 16)

            for it in range(E_ITERS):
                for p in AB:
                    gather(it, p)
            for it in range(E_ITERS):
                for p in AB:
                    scatter(it, p)
                if it + 1 < E_ITERS:
                    for p in AB:
                        pool.wait_ge(scattered[p], (it + 1) * 16 * NB)
                        pool.sem_inc(outputs_free[p], 1)

        def experts_transfers(sp):
            w = lambda name, first: inp[name][:, bass.ds(first, 16), :]

            def load_w13(it, p):
                sp.dma_start(e_w1[p], w("w1T", it * 32 + 16 * p)).then_inc(w13_in[p], 16)
                sp.dma_start(e_w3[p], w("w3T", it * 32 + 16 * p)).then_inc(w13_in[p], 16)

            for q in AB:
                sp.wait_ge(p1.r_keyed[q], ITERS)
            for p in AB:
                load_w13(0, p)
            for p in AB:
                sp.dma_start(e_w2[p], w("w2T", 16 * p)).then_inc(w2_in[p], 16)
            for dst, name in late3:
                sp.dma_start(dst, dram(name)).then_inc(weights_in, 16)
            sp.wait_ge(half_lists, 1)
            sp.dma_start(both[:, CAP:2 * CAP], lists[E:128, :]).then_inc(half_moved, 16)
            for it in range(1, E_ITERS):
                for p in AB:
                    sp.wait_ge(e_h_full[p], it * 4)
                    load_w13(it, p)
                for p in AB:
                    sp.wait_ge(e_y_full[p], it * 2)
                    sp.dma_start(e_w2[p], w("w2T", it * 32 + 16 * p)).then_inc(w2_in[p], 16)

        loads1 = [(w0_qkv[:, :], "L0_Wqkv"), (b0_o[:, :], "L0_bout")]
        loads1 += [(w0_o[32 * j:32 * j + 8, :, :], ("L0_Wout", j)) for j in range(4)]
        loads1 += [(wx_q[:, :], "L0_Wq"), (wx_kv[:, 0:128], "L0_Wk"), (wx_kv[:, 128:256], "L0_Wv"),
                   (bx_o[:, :], "L0_bo"), (gate_w[:, :], "gate_w"), (gate_b[:, :], "gate_b"),
                   (token_key, "token_key")]
        loads1 += [(wx_o[32 * j:32 * j + 16, :, :], ("L0_Wo", j)) for j in range(4)]
        loads3 = [(ws13[:, :, :], "ws13"), (w1_qkv[:, :], "L1_Wqkv"), (b1_qk[:, :], "b1_qk"),
                  (b1_v[:, :], "b1_v"), (w1_o[:, :, :], "L1_Wout"), (b1_o[:, :], "L1_bout"), (w1x_q[:, :], "L1_Wq"),
                  (w1x_k[:, :], "L1_Wk"), (w1x_v[:, :], "L1_Wv"), (w1x_o[:, :, :], "L1_Wo"), (b1x_o[:, :], "L1_bo"),
                  (bf_cols[:, :], "bf_cols")]
        late3 = [(ws2, "ws2"), (wf_qkv[:, 0:128], "q_w"), (wf_qkv[:, 128:256], "k_w"),
                 (wf_qkv[:, 256:384], "v_w"), (bf_v[:, :], "v_b")]
        stage = prob[:, :, :].rearrange("p a (b c) -> p (a b) c", c=128)
        consts = [(ident[:, :], "ident"), (tri, "tri"), (head_mask[:, :], "head_mask"),
                  (ones_g[:, :, :, :], "ones_g"), (ones_u[:, :, :, :], "ones_u"), (pick_sum[:, :, :], "pick_sum"),
                  (stage[:, 0:4, :], "spread_s"), (stage[:, 4:12, :], "spread_b"), (part_cols[:, :], "part_cols"), (upper[:, :], "upper")]
        consts_in = sem("consts_in")
        weights1_in = sem("weights1_in")
        zero_filled = sem("zero_filled")
        cleared = sem("cleared")

        def dram(name):
            if isinstance(name, tuple):
                w, j = name
                d = 8 if w == "L0_Wout" else 16
                return inp[w].rearrange("(u j d) o -> j d u o", j=4, d=d)[j]
            if name in ("L1_Wout", "L1_Wo"):
                return inp[name].rearrange("(c p) o -> p c o", p=128)
            return inp[name]

        block = ctx.enter_context(nc.Block())

        @block.sync
        def _(sp):
            for s in AB:
                for sems in (p1.out_done, p1.key_moved, p3.out_done):
                    sp.sem_inc(sems[s], 1)
                sp.sem_inc(outputs_free[s], 1)

            def load1(seq, s):
                row = lambda name: inp[name][bass.ds(seq, 1), :, :]
                sp.dma_start(x_in[s], row("x").rearrange("o (t p) d -> p (o t) d", p=128)).then_inc(p1.x_in[s], 16)
                sp.dma_start(xt_in[s], row("xT").rearrange("o d t -> d (o t)")).then_inc(p1.x_in[s], 16)

            def load_context(y, seq, s):
                sp.dma_start(ctx_t[s][:, :, :], inp["ctxT2"][bass.ds(seq, 1), :, :].rearrange(
                    "o d (a k) -> d (o a) k", a=2)).then_inc(y.ctx_in[s], 16)

            def store1(v, s):
                seq = v.it * 2 + s
                sp.wait_ge(p1.r_masked[s], v.once())
                sp.dma_start(xg[bass.ds(seq * T, T), :].rearrange("(t p) w -> p t w", p=128), xs[s]).then_inc(
                    p1.out_done[s], 16)

            for dst, name in consts:
                sp.dma_start(dst, dram(name)).then_inc(consts_in, 16)
            for s in AB:
                load1(s, s)
                load_context(p1, s, s)
            sp.wait_ge(cleared, 1)
            for dst, name in loads1:
                sp.dma_start(dst, dram(name)).then_inc(weights1_in, 16)
            for dst, name in loads3:
                sp.dma_start(dst, dram(name)).then_inc(weights_in, 16)
            for e, m in NESTED:
                for h in range(max(1, m // 16)):
                    u, j = h // 4, h % 4
                    sp.dma_start(wf_o[32 * j:32 * j + 16, e + (e > 0) + u, 0:m], inp["o_w"][16 * h:16 * h + 16, 0:m]).then_inc(
                        weights_in, 16)
                p = 64 * (e % 2)
                sp.dma_start(bf_o[p:p + 64, e // 2, 0:m], inp["o_b"][p:p + 64, 0:m]).then_inc(weights_in, 16)
            sp.wait_ge(zero_filled, 1)
            zrows = zd.rearrange("(n p r) d -> n p (r d)", p=128, r=8)
            for n in range(24):
                sp.dma_start(zrows[n], zeros).then_inc(zeroed, 16)
            with sp.Fori(0, ITERS - 1) as it:
                v = View("p1", it)
                for s in AB:
                    sp.wait_ge(*v.drained(("V", L0, s, 0)))
                    sp.wait_ge(p1.res_ready[s], v.attn(L0))
                    load1(it * 2 + (2 + s), s)
                for s in AB:
                    sp.wait_ge(*v.drained(("V", L0X, s, 0)))
                    load_context(p1, it * 2 + (2 + s), s)
                for s in AB:
                    store1(v, s)
            for s in AB:
                store1(View("p1", ITERS - 1), s)

            experts_transfers(sp)
            def load3(seq, s):
                sp.dma_start(x3_in[s][:, :, :], xg[bass.ds(seq * T, T), 0:D].rearrange(
                    "(t p) w -> p t w", p=128)).then_inc(p3.x_in[s], 16)

            def load_routed(seq, s):
                sp.dma_start(routed[s].rearrange("p t k d -> p t (k d)"), zd[bass.ds(seq * T * TOPK, T * TOPK), :].rearrange(
                    "(t p k) d -> p t (k d)", p=128, k=TOPK)).then_inc(p3.routed_in[s], 16)

            def store3(v, s):
                sp.wait_ge(p3.x_ready[s], v.ln(L1F))
                sp.dma_start(out[bass.ds(v.it * 2 + s, 1), :, :].rearrange("o (t p) d -> p (o t) d", p=128),
                             x_out[s][:, :, :]).then_inc(p3.out_done[s], 16)

            for s in AB:
                load3(s, s)
                load_context(p3, s, s)
            for p in AB:
                sp.wait_ge(scattered[p], E_ITERS * 16 * NB)
            for s in AB:
                load_routed(s, s)
            with sp.Fori(0, ITERS - 1) as it:
                v = View("p3", it)
                for s in AB:
                    sp.wait_ge(p3.x_used[s], v.once())
                    load3(it * 2 + (2 + s), s)
                    load_routed(it * 2 + (2 + s), s)
                for s in AB:
                    sp.wait_ge(*v.drained(("V", L1X, s, 1)))
                    load_context(p3, it * 2 + (2 + s), s)
                for s in AB:
                    store3(v, s)
            for s in AB:
                store3(View("p3", ITERS - 1), s)
            for s in AB:
                sp.wait_ge(p3.out_done[s], ITERS * 16 + 1)

        N3 = len(loads3) + len(late3) + sum(max(1, m // 16) + 1 for _, m in NESTED)

        def run_phase(eng, tag, do_step):
            def body(it, aheads):
                for step, ahead in plan[tag]:
                    if ahead in aheads:
                        do_step(eng, View(tag, it, ahead), step)
                    elif do_step is tensor_step:
                        absent_step(eng, View(tag, it, ahead), step)

            body(-1, (1,))
            with eng.Fori(0, ITERS - 1) as it:
                body(it, (0, 1))
            body(ITERS - 1, (0,))

        @block.tensor
        def _(pe):
            pe.wait_ge(consts_ready, 1)
            pe.wait_ge(weights1_in, 16 * len(loads1))
            run_phase(pe, "p1", tensor_step)
            experts_tensor(pe)
            pe.wait_ge(p3_ready, 1)
            run_phase(pe, "p3", tensor_step)

        @block.scalar
        def _(act):
            act.wait_ge(consts_ready, 1)
            run_phase(act, "p1", scalar_step)
            experts_scalar(act)
            act.wait_ge(p3_ready, 1)
            run_phase(act, "p3", scalar_step)

        @block.vector
        def _(dve):
            for y in (p1, p3):
                for b in range(8):
                    dve.sem_inc(y.free[b], 1)
            dve.sem_inc(p1.sorted, 1)
            ms, cp, ts = nc.vector.memset, nc.vector.tensor_copy, nc.vector.tensor_scalar
            for t in (w0_o[:, :, :], wx_o[:, :, :], wf_o[:, :, :]):
                ms(t, 0.0)
            ms(sel_h[:, :, :], 0.0)
            for s in AB:
                ms(shift[s][:, :, :], 0.0)
                ms(rdiag[s][:, :, :], 0.0)
            ms(bf_o[:, :, :], 0.0).then_inc(cleared, 1)
            ms(zeros, 0.0).then_inc(zero_filled, 1)
            for s in AB:
                ms(va[s][:, :, :, :], 1.0)
                ms(r_sel[s][:, :, :], BIG)
                for u in range(2):
                    mine = va_x[s][64 * u:64 * u + 64, :, :].rearrange("p (c u) d -> p c u d", u=2)
                    ms(mine[:, :, 1 - u, :], 0.0)
                    ms(mine[:, :, u, :], 1.0)
            ms(mask_s[:, 128:256], -250.0)
            dve.wait_ge(consts_in, 16 * len(consts))
            ts(mask_s[:, 0:128], tri[:, 0:128], -250.0, None, ALU.mult)
            ts(mask_t[:, :], tri[:, 128:256], -250.0, None, ALU.mult)
            cp(ident_b[:, :], ident[:, :])
            cp(upper_b[:, :], upper[:, :])
            cp(spread_s[:, :, :], stage[:, 0:4, :])
            cp(spread_b[:, :, :], stage[:, 4:12, :])
            ts(neg_ident[:, :], ident[:, :], -1.0, None, ALU.mult)
            ts(ident_inf[:, :], ident[:, :], 1.0e28, None, ALU.mult)
            ts(ident_add[:, :], ident[:, :], 320.0, None, ALU.mult)
            dve.wait_ge(cleared, 1)
            ms(sel_h[32:33, :, :], 320.0)
            for s in AB:
                ms(shift[s][32:33, 1, 0:128], -250.0)
            cp(sel_h[0:16, :, :], ident[0:16, 0:16].unsqueeze(2).to_broadcast([16, 16, 128])).then_inc(consts_ready, 1)
            dve.wait_ge(weights1_in, 16 * len(loads1))
            run_phase(dve, "p1", vector_step)
            experts_vector(dve)
            for s in AB:
                dve.wait_ge(e_y_ready[s], 2 * E_ITERS)
                ms(kx[s][:, :, :], 0.0)
                ms(vx[s][:, :, :], 0.0)
            dve.wait_ge(weights_in, 16 * N3)
            ms(kb[:, :, :], 0.0).then_inc(p3_ready, 1)
            run_phase(dve, "p3", vector_step)

        @block.gpsimd
        def _(pool):
            nc.gpsimd.memset(powers[:, 0:2], EPS)
            nc.gpsimd.memset(powers[:, 2:4], -0.5)
            pool.wait_ge(weights1_in, 16 * len(loads1))
            run_phase(pool, "p1", pool_step)
            experts_pool(pool)
            pool.wait_ge(p3_ready, 1)
            run_phase(pool, "p3", pool_step)


def constants():
    c = {}
    p = np.arange(128)
    c["ident"] = np.eye(128, dtype=np.float32)
    tri = (p[None, :] > p[:, None]).astype(np.float32)
    c["tri"] = np.concatenate([tri, tri.T], 1)
    c["head_mask"] = np.concatenate([p[:, None] // 8 == np.arange(16)[None], p[:, None] // 16 == np.arange(8)[None]],
                                    1).astype(np.float32)
    r = np.arange(32)
    u = np.arange(2)
    g = r[None, None, :] % 8 == 2 * np.arange(4)[None, :, None] + u[:, None, None]
    c["ones_g"] = np.broadcast_to(g, (128, 2, 4, 32)).copy()
    c["ones_u"] = (p[:, None, None, None] // 64 == u[None, :, None, None]) * g[None]
    own = (r[None] // 4 % 2 == np.array([[0], [1], [2]])) | (np.arange(3)[:, None] == 2)
    c["pick_sum"] = (p[:, None, None] == 32 * (r % 4) + 31) & own[None]
    row, part = p[:, None, None] % 64, p[:, None, None] % 32 // 8
    n = np.arange(4)[None, :, None]
    c["spread_s"] = (row == 32 * (n // 2) + 4 * (n % 2) + p[None, None, :] // 32 + 8 * part) & (part < 3)
    n = np.arange(8)[None, :, None]
    c["spread_b"] = (row == 32 * (n % 2) + 2 * (n // 2) + p[None, None, :] // 64 + 8 * part) & (part < 3)
    c["part_cols"] = -1.0 * (p[:, None] % 32 // 8 >= np.array([[1, 2]]))
    e = np.arange(E)
    c["upper"] = (p[:, None] % E < e[None, :]).astype(np.float32)
    c["token_key"] = 8.0 * (TOK - np.arange(T)[None, :] - T * (p[:, None] // E))
    return {k: np.ascontiguousarray(a, dtype=np.float32) for k, a in c.items()}


def laid_out(i):
    rows = lambda a: np.broadcast_to(a, (128, a.shape[0]))
    ctx_t = i["ctx_768"].transpose(0, 2, 1)
    return {
        "x": i["x"], "xT": i["x"].transpose(0, 2, 1), "ctxT2": np.concatenate([ctx_t, ctx_t], 2),
        "L0_Wqkv": i["L0_attn_Wqkv"].T, "L0_Wout": i["L0_attn_Wout"].T, "L0_bout": rows(i["L0_attn_bout"]),
        "L0_Wq": i["L0_xattn_Wq"], "L0_Wk": i["L0_xattn_Wk"], "L0_Wv": i["L0_xattn_Wv"],
        "L0_Wo": i["L0_xattn_Wo"], "L0_bo": rows(i["L0_xattn_bo"]),
        "gate_w": i["L0_ffn_gate_w"].T, "gate_b": rows(i["L0_ffn_gate_b"]),
        "w1T": i["L0_ffn_w1"].transpose(2, 0, 1), "w3T": i["L0_ffn_w3"].transpose(2, 0, 1),
        "w2T": i["L0_ffn_w2"].transpose(2, 0, 1),
        "ws13": np.concatenate([i["L0_ffn_ws1"].T.reshape(D, 2, FI), i["L0_ffn_ws3"].T.reshape(D, 2, FI)], 1),
        "ws2": i["L0_ffn_ws2"].T.reshape(2, FI, D).transpose(1, 0, 2),
        "L1_Wqkv": i["L1_attn_W_qkv"], "b1_qk": i["L1_attn_b_qkv"][:2048].reshape(16, 128).T,
        "b1_v": rows(i["L1_attn_b_qkv"][2048:]), "L1_Wout": i["L1_attn_W_out"], "L1_bout": rows(i["L1_attn_b_out"]),
        "L1_Wq": i["L1_xattn_Wq"], "L1_Wk": i["L1_xattn_Wk"], "L1_Wv": i["L1_xattn_Wv"],
        "L1_Wo": i["L1_xattn_Wo"], "L1_bo": rows(i["L1_xattn_bo"]),
        "q_w": i["L1_ffn_q_w"].T, "k_w": i["L1_ffn_k_w"].T, "v_w": i["L1_ffn_v_w"].T,
        "bf_cols": np.stack([i["L1_ffn_norm_w"], i["L1_ffn_norm_b"], i["L1_ffn_q_b"], i["L1_ffn_k_b"]], 1),
        "v_b": rows(i["L1_ffn_v_b"]), "o_w": i["L1_ffn_o_w"].T, "o_b": rows(i["L1_ffn_o_b"]),
    }


def kernel(**inputs):
    import concourse.bacc as _bacc
    from concourse.bass_utils import run_bass_kernel_spmd as _run

    nc = _bacc.Bacc("TRN2", target_bir_lowering=False, num_devices=1)
    given = {k: np.asarray(a) for k, a in inputs.items()}
    arrays, args = {}, {}
    for name, a in {**laid_out(given), **constants()}.items():
        a = np.ascontiguousarray(a)
        arrays[f"in_{name}"] = a
        args[name] = nc.dram_tensor(f"in_{name}", a.shape, mybir.dt.from_np(a.dtype), kind="ExternalInput").ap()
    out = nc.dram_tensor("out", (SEQS, T, D), FP32, kind="ExternalOutput").ap()
    decoder_program(nc, args, out)
    r = _run(nc, [arrays], core_ids=[0])
    return r.results[0]["out"]
```
